# Optimizing a Trainium2 kernel written in Bass

```python
import numpy as np
import jax
import jax.numpy as jnp

def _softmax(x, axis=-1):
    return jax.nn.softmax(x, axis=axis)

def _gelu(x):
    return jax.nn.gelu(x, approximate=True)

def _silu(x):
    return jax.nn.silu(x)

def _sigmoid(x):
    return jax.nn.sigmoid(x)

def _layernorm(x, axis=-1, eps=1e-05):
    m = jnp.mean(x, axis=axis, keepdims=True)
    v = jnp.var(x, axis=axis, keepdims=True)
    return (x - m) / jnp.sqrt(v + eps)

def _scatter_add(tgt, idx, src, axis=0):
    return tgt.at[idx].add(src)

def _segment_sum(src, seg, n):
    return jax.ops.segment_sum(src, seg, n)
kernel_name = 'mk_macaron_d2_jaxref_r8_b773a1'

def setup_inputs(seed: int=0):
    np.random.seed(seed)
    _w = jnp.asarray

    def _L0_attn_setup():
        import jax, jax.numpy as jnp
        import numpy as np
        B, S, E, H = (4, 256, 256, 16)
        D = E // H
        ROPE_BASE = 10000.0

        def rope(x, base=ROPE_BASE, offset=0):
            d = x.shape[-1]
            s = x.shape[-2]
            inv_freq = base ** (-jnp.arange(0, d, 2, dtype=jnp.float32) / d)
            pos = jnp.arange(offset, s + offset, dtype=jnp.float32)
            ang = pos[:, None] * inv_freq
            sin, cos = (jnp.sin(ang), jnp.cos(ang))
            xe, xo = (x[..., 0::2], x[..., 1::2])
            re = xe * cos - xo * sin
            ro = xe * sin + xo * cos
            return jnp.stack([re, ro], axis=-1).reshape(x.shape)
        key = jax.random.key(seed)
        ks = jax.random.split(key, 9)
        w = lambda k, shp: jax.random.normal(k, shp, dtype=jnp.float32) * 0.02
        return {'x': jax.random.normal(ks[0], (B, S, E), dtype=jnp.float32), 'Wq': w(ks[1], (E, E)), 'bq': w(ks[2], (E,)), 'Wk': w(ks[3], (E, E)), 'bk': w(ks[4], (E,)), 'Wv': w(ks[5], (E, E)), 'bv': w(ks[6], (E,)), 'Wo': w(ks[7], (E, E)), 'bo': w(ks[8], (E,))}
    _L0_attn_in = _L0_attn_setup()

    def _L0_ffn_setup():
        import jax, jax.numpy as jnp
        import numpy as np
        TOP_K = 4

        def _silu_and_mul(gu):
            g, u = jnp.split(gu, 2, axis=-1)
            return jax.nn.silu(g) * u
        key = jax.random.key(seed)
        ks = jax.random.split(key, 7)
        H, E, I, Is = (256, 16, 176, 704)
        s = 0.02
        return {'hidden_states': jax.random.normal(ks[0], (4, 128, H), dtype=jnp.float32), 'gate_w': jax.random.normal(ks[1], (E, H), dtype=jnp.float32) * s, 'sgate_w': jax.random.normal(ks[2], (1, H), dtype=jnp.float32) * s, 'w13': jax.random.normal(ks[3], (E, 2 * I, H), dtype=jnp.float32) * s, 'w2': jax.random.normal(ks[4], (E, H, I), dtype=jnp.float32) * s, 'shared_gate_up_w': jax.random.normal(ks[5], (2 * Is, H), dtype=jnp.float32) * s, 'shared_down_w': jax.random.normal(ks[6], (H, Is), dtype=jnp.float32) * s}
    _L0_ffn_in = _L0_ffn_setup()

    def _L1_attn_setup():
        import jax, jax.numpy as jnp
        import numpy as np
        ROPE_DIM = 64
        GN_GROUPS = 32
        GN_CHANNELS = 256
        GN_EPS = 1e-05

        def rope_rotate(x):
            T = x.shape[-2]
            inv_freq = 1.0 / 10000.0 ** (jnp.arange(0, ROPE_DIM, 2, dtype=jnp.float32) / ROPE_DIM)
            freqs = jnp.arange(T, dtype=jnp.float32)[:, None] * inv_freq[None, :]
            freqs = jnp.repeat(freqs, 2, axis=-1)
            cos, sin = (jnp.cos(freqs), jnp.sin(freqs))
            xr = x[..., :ROPE_DIM]
            x1, x2 = (xr[..., 0::2], xr[..., 1::2])
            rot = jnp.stack((-x2, x1), axis=-1).reshape(xr.shape)
            xr = xr * cos + rot * sin
            return jnp.concatenate([xr, x[..., ROPE_DIM:]], axis=-1)

        def group_norm_rows(x2d, weight, bias):
            N, Cc = x2d.shape
            xg = x2d.reshape(N, GN_GROUPS, Cc // GN_GROUPS)
            mu = xg.mean(-1, keepdims=True)
            var = xg.var(-1, keepdims=True)
            xn = ((xg - mu) * jax.lax.rsqrt(var + GN_EPS)).reshape(N, Cc)
            return xn * weight + bias

        def _reference_tuple_inner(X, S_n, W_Q, hh_b, gn_weight, gn_bias):
            B, T, _ = X.shape
            Q = jax.nn.relu(rope_rotate(X @ W_Q))
            H = jnp.tanh(Q + hh_b)
            C = H.shape[-1]
            out = group_norm_rows(H.reshape(-1, C), gn_weight, gn_bias).reshape(B, T, C)
            out = jnp.swapaxes(out, -2, -1).reshape(B, T, C)
            return (out, S_n)
        key = jax.random.key(seed)
        ks = jax.random.split(key, 4)
        B, T, I, C = (2, 512, 256, 256)
        X = jax.random.normal(ks[0], (B, T, I), dtype=jnp.float32)
        S_n = jnp.zeros((B, C), dtype=jnp.float32)
        W_Q = jax.random.normal(ks[1], (I, C), dtype=jnp.float32) / I
        hh_b = jax.random.normal(ks[2], (C,), dtype=jnp.float32) * 0.02
        gn_weight = jnp.ones((C,), dtype=jnp.float32)
        gn_bias = jnp.zeros((C,), dtype=jnp.float32)
        return {'X': X, 'S_n': S_n, 'W_Q': W_Q, 'hh_b': hh_b, 'gn_weight': gn_weight, 'gn_bias': gn_bias}
    _L1_attn_in = _L1_attn_setup()

    def _L1_ffn_setup():
        import jax, jax.numpy as jnp
        import numpy as np
        K = 2
        SCALING = 16.0 / 16.0
        key = jax.random.key(seed)
        ks = jax.random.split(key, 7)
        B, T, D, O, E, R = (2, 512, 256, 256, 8, 16)
        return {'x': jax.random.normal(ks[0], (B, T, D), dtype=jnp.float32), 'W': jax.random.normal(ks[1], (O, D), dtype=jnp.float32) * (1.0 / np.sqrt(D)), 'b': jax.random.normal(ks[2], (O,), dtype=jnp.float32) * 0.02, 'lora_A': jax.random.normal(ks[3], (E, R, D), dtype=jnp.float32) * (1.0 / np.sqrt(D)), 'lora_B': jax.random.normal(ks[4], (E, O, R), dtype=jnp.float32) * 0.02, 'gate_w': jax.random.normal(ks[5], (E, D), dtype=jnp.float32) * 0.02, 'gate_b': jax.random.normal(ks[6], (E,), dtype=jnp.float32) * 0.02}
    _L1_ffn_in = _L1_ffn_setup()
    _d = {'L0_attn_x': _L0_attn_in['x'], 'L0_attn_Wq': _L0_attn_in['Wq'], 'L0_attn_bq': _L0_attn_in['bq'], 'L0_attn_Wk': _L0_attn_in['Wk'], 'L0_attn_bk': _L0_attn_in['bk'], 'L0_attn_Wv': _L0_attn_in['Wv'], 'L0_attn_bv': _L0_attn_in['bv'], 'L0_attn_Wo': _L0_attn_in['Wo'], 'L0_attn_bo': _L0_attn_in['bo'], 'L0_ffn_gate_w': _L0_ffn_in['gate_w'], 'L0_ffn_sgate_w': _L0_ffn_in['sgate_w'], 'L0_ffn_w13': _L0_ffn_in['w13'], 'L0_ffn_w2': _L0_ffn_in['w2'], 'L0_ffn_shared_gate_up_w': _L0_ffn_in['shared_gate_up_w'], 'L0_ffn_shared_down_w': _L0_ffn_in['shared_down_w'], 'L1_attn_S_n': _L1_attn_in['S_n'], 'L1_attn_W_Q': _L1_attn_in['W_Q'], 'L1_attn_hh_b': _L1_attn_in['hh_b'], 'L1_attn_gn_weight': _L1_attn_in['gn_weight'], 'L1_attn_gn_bias': _L1_attn_in['gn_bias'], 'L1_ffn_W': _L1_ffn_in['W'], 'L1_ffn_b': _L1_ffn_in['b'], 'L1_ffn_lora_A': _L1_ffn_in['lora_A'], 'L1_ffn_lora_B': _L1_ffn_in['lora_B'], 'L1_ffn_gate_w': _L1_ffn_in['gate_w'], 'L1_ffn_gate_b': _L1_ffn_in['gate_b']}
    _x0 = _d['L0_attn_x']
    _d['L0_attn_x'] = jax.random.normal(jax.random.fold_in(jax.random.key(seed), 1), (8, 512, 256), dtype=_x0.dtype)
    del _x0
    return _d

def reference(L0_attn_x, L0_attn_Wq, L0_attn_bq, L0_attn_Wk, L0_attn_bk, L0_attn_Wv, L0_attn_bv, L0_attn_Wo, L0_attn_bo, L0_ffn_gate_w, L0_ffn_sgate_w, L0_ffn_w13, L0_ffn_w2, L0_ffn_shared_gate_up_w, L0_ffn_shared_down_w, L1_attn_S_n, L1_attn_W_Q, L1_attn_hh_b, L1_attn_gn_weight, L1_attn_gn_bias, L1_ffn_W, L1_ffn_b, L1_ffn_lora_A, L1_ffn_lora_B, L1_ffn_gate_w, L1_ffn_gate_b):

    def _L0_attn_ref(x, Wq, bq, Wk, bk, Wv, bv, Wo, bo):
        import jax, jax.numpy as jnp
        import numpy as np
        B, S, E, H = (4, 256, 256, 16)
        D = E // H
        ROPE_BASE = 10000.0

        def rope(x, base=ROPE_BASE, offset=0):
            d = x.shape[-1]
            s = x.shape[-2]
            inv_freq = base ** (-jnp.arange(0, d, 2, dtype=jnp.float32) / d)
            pos = jnp.arange(offset, s + offset, dtype=jnp.float32)
            ang = pos[:, None] * inv_freq
            sin, cos = (jnp.sin(ang), jnp.cos(ang))
            xe, xo = (x[..., 0::2], x[..., 1::2])
            re = xe * cos - xo * sin
            ro = xe * sin + xo * cos
            return jnp.stack([re, ro], axis=-1).reshape(x.shape)
        b, s, _ = x.shape
        scale = D ** (-0.5)

        def proj(W, bias):
            y = jnp.einsum('bse,fe->bsf', x, W) + bias
            return y.reshape(b, s, H, D).transpose(0, 2, 1, 3)
        q = rope(proj(Wq, bq))
        k = rope(proj(Wk, bk))
        v = proj(Wv, bv)
        attn = jnp.einsum('bhqd,bhkd->bhqk', q, k) * scale
        causal = jnp.triu(jnp.ones((s, s), dtype=bool), k=1)
        attn = jnp.where(causal, -jnp.inf, attn)
        attn_weights = jax.nn.softmax(attn, axis=-1)
        out = jnp.einsum('bhqk,bhkd->bhqd', attn_weights, v)
        out = out.transpose(0, 2, 1, 3).reshape(b, s, E)
        return jnp.einsum('bse,fe->bsf', out, Wo) + bo

    def _L0_ffn_ref(hidden_states, gate_w, sgate_w, w13, w2, shared_gate_up_w, shared_down_w):
        import jax, jax.numpy as jnp
        import numpy as np
        TOP_K = 4

        def _silu_and_mul(gu):
            g, u = jnp.split(gu, 2, axis=-1)
            return jax.nn.silu(g) * u
        B, S, H = hidden_states.shape
        x = hidden_states.reshape(-1, H)
        E = gate_w.shape[0]
        shared = _silu_and_mul(x @ shared_gate_up_w.T) @ shared_down_w.T
        shared = shared * jax.nn.sigmoid(x @ sgate_w.T)
        router_logits = x @ gate_w.T
        routing_weights = jax.nn.softmax(router_logits.astype(jnp.float32), axis=-1)
        topk_w, topk_ids = jax.lax.top_k(routing_weights, TOP_K)

        def body(acc, ew):
            w13_e, w2_e, e = ew
            coef = jnp.sum(jnp.where(topk_ids == e, topk_w, 0.0), axis=-1)
            h = _silu_and_mul(x @ w13_e.T)
            acc = acc + (h @ w2_e.T).astype(jnp.float32) * coef[:, None]
            return (acc, None)
        init = jnp.zeros((x.shape[0], H), dtype=jnp.float32)
        sparse_out, _ = jax.lax.scan(body, init, (w13, w2, jnp.arange(E)))
        out = shared + sparse_out.astype(x.dtype)
        return out.reshape(B, S, H)

    def _L1_attn_ref(X, S_n, W_Q, hh_b, gn_weight, gn_bias):
        import jax, jax.numpy as jnp
        import numpy as np
        ROPE_DIM = 64
        GN_GROUPS = 32
        GN_CHANNELS = 256
        GN_EPS = 1e-05

        def rope_rotate(x):
            T = x.shape[-2]
            inv_freq = 1.0 / 10000.0 ** (jnp.arange(0, ROPE_DIM, 2, dtype=jnp.float32) / ROPE_DIM)
            freqs = jnp.arange(T, dtype=jnp.float32)[:, None] * inv_freq[None, :]
            freqs = jnp.repeat(freqs, 2, axis=-1)
            cos, sin = (jnp.cos(freqs), jnp.sin(freqs))
            xr = x[..., :ROPE_DIM]
            x1, x2 = (xr[..., 0::2], xr[..., 1::2])
            rot = jnp.stack((-x2, x1), axis=-1).reshape(xr.shape)
            xr = xr * cos + rot * sin
            return jnp.concatenate([xr, x[..., ROPE_DIM:]], axis=-1)

        def group_norm_rows(x2d, weight, bias):
            N, Cc = x2d.shape
            xg = x2d.reshape(N, GN_GROUPS, Cc // GN_GROUPS)
            mu = xg.mean(-1, keepdims=True)
            var = xg.var(-1, keepdims=True)
            xn = ((xg - mu) * jax.lax.rsqrt(var + GN_EPS)).reshape(N, Cc)
            return xn * weight + bias

        def _reference_tuple_inner(X, S_n, W_Q, hh_b, gn_weight, gn_bias):
            B, T, _ = X.shape
            Q = jax.nn.relu(rope_rotate(X @ W_Q))
            H = jnp.tanh(Q + hh_b)
            C = H.shape[-1]
            out = group_norm_rows(H.reshape(-1, C), gn_weight, gn_bias).reshape(B, T, C)
            out = jnp.swapaxes(out, -2, -1).reshape(B, T, C)
            return (out, S_n)
        return _reference_tuple_inner(X, S_n, W_Q, hh_b, gn_weight, gn_bias)[0]

    def _L1_ffn_ref(x, W, b, lora_A, lora_B, gate_w, gate_b):
        import jax, jax.numpy as jnp
        import numpy as np
        K = 2
        SCALING = 16.0 / 16.0
        orig_shape = x.shape
        D = orig_shape[-1]
        O = W.shape[0]
        x_flat = x.reshape(-1, D)
        base = x_flat @ W.T + b
        logits = x_flat @ gate_w.T + gate_b
        topk_logits, topk_idx = jax.lax.top_k(logits, K)
        gates = jax.nn.softmax(topk_logits, axis=-1)
        xA = jnp.einsum('nd,erd->ner', x_flat, lora_A)
        delta_all = jnp.einsum('ner,eor->neo', xA, lora_B)
        delta_topk = jnp.take_along_axis(delta_all, topk_idx[:, :, None], axis=1)
        lora_update = jnp.sum(delta_topk * gates[:, :, None], axis=1)
        out = base + SCALING * lora_update
        return out.reshape(*orig_shape[:-1], O)
    x = L0_attn_x
    x = x + 0.5 * _L0_ffn_ref(_layernorm(x, axis=-1), L0_ffn_gate_w, L0_ffn_sgate_w, L0_ffn_w13, L0_ffn_w2, L0_ffn_shared_gate_up_w, L0_ffn_shared_down_w)
    x = x + _L0_attn_ref(_layernorm(x, axis=-1), L0_attn_Wq, L0_attn_bq, L0_attn_Wk, L0_attn_bk, L0_attn_Wv, L0_attn_bv, L0_attn_Wo, L0_attn_bo)
    x = x + 0.5 * _L0_ffn_ref(_layernorm(x, axis=-1), L0_ffn_gate_w, L0_ffn_sgate_w, L0_ffn_w13, L0_ffn_w2, L0_ffn_shared_gate_up_w, L0_ffn_shared_down_w)
    x = x + 0.5 * _L1_ffn_ref(_layernorm(x, axis=-1), L1_ffn_W, L1_ffn_b, L1_ffn_lora_A, L1_ffn_lora_B, L1_ffn_gate_w, L1_ffn_gate_b)
    x = x + _L1_attn_ref(_layernorm(x, axis=-1), L1_attn_S_n, L1_attn_W_Q, L1_attn_hh_b, L1_attn_gn_weight, L1_attn_gn_bias)
    x = x + 0.5 * _L1_ffn_ref(_layernorm(x, axis=-1), L1_ffn_W, L1_ffn_b, L1_ffn_lora_A, L1_ffn_lora_B, L1_ffn_gate_w, L1_ffn_gate_b)
    return x

_drawn_inputs = setup_inputs


def setup_inputs(seed=0):
    import zlib

    import numpy as np

    out = dict(_drawn_inputs(seed))
    spreads = {'L1_attn_S_n': (0.0, 0.1),
     'L1_attn_gn_weight': (1.0, 0.2),
     'L1_attn_gn_bias': (0.0, 0.395)}
    factors = {'L0_attn_Wq': 8.0,
     'L0_attn_bq': 8.0,
     'L0_attn_Wk': 8.0,
     'L0_attn_bk': 8.0,
     'L0_attn_Wv': 4.438,
     'L0_attn_bv': 7.808,
     'L0_attn_Wo': 3.806,
     'L0_attn_bo': 2.9,
     'L0_ffn_gate_w': 8.0,
     'L0_ffn_sgate_w': 8.0,
     'L0_ffn_w13': 8.0,
     'L0_ffn_w2': 8.0,
     'L0_ffn_shared_gate_up_w': 3.641,
     'L0_ffn_shared_down_w': 3.643,
     'L1_ffn_b': 13.614,
     'L1_ffn_gate_b': 64.0,
     'L1_ffn_lora_A': 5.024,
     'L1_ffn_lora_B': 5.032,
     'L1_ffn_gate_w': 6.179}
    for name, (base, spread) in spreads.items():
        noise = np.random.default_rng([zlib.crc32(name.encode()), seed]).standard_normal(out[name].shape)
        drawn = base * np.exp(spread * noise) if base else spread * noise
        out[name] = jnp.asarray(drawn.astype(out[name].dtype))
    for name, factor in factors.items():
        out[name] = (out[name] * factor).astype(out[name].dtype)
    return out
```

```python
from contextlib import ExitStack

import concourse.bass as bass
import numpy as np
from concourse import mybir

F32 = mybir.dt.float32
BF16 = mybir.dt.bfloat16
U32 = mybir.dt.uint32
ALU = mybir.AluOpType
ACT = mybir.ActivationFunctionType
AX_X = mybir.AxisListType.X

P = 128
B, T, E = 8, 512, 256
TILES = T // P
KT = E // P
NE, TOPK = 16, 4
I = 176
SH = 704 // I
UNITS = NE + SH
HK = I // 2
H, D = 16, 16
STACK = 6 * D
ROWS = STACK + 3
LE, LK, R = 8, 2, 16
LR = LE * R
LCOLS = E + LR + LE
RD = 64
G, GC = 32, 8
EPS = 1e-5
NEG = -1e30
WORK = 10000


class Chain:

    def __init__(self, eng, sem, per, need):
        self.eng, self.sem, self.per, self.need = eng, sem, per, need

    def start(self, it):
        self.it, self.n = it, 0

    def step(self, ins, stand=None):
        self.n += 1
        ins.then_inc(self.sem, 1)
        (stand or self.need)(self.eng, self.sem, self.it * self.per + self.n)

    def end(self):
        assert self.n == self.per, self.n


def build(nc, d, out):
    with ExitStack() as ctx:
        def sb(name, shape, dt=F32):
            return ctx.enter_context(nc.sbuf_tensor(name, shape, dt))[(slice(None),) * len(shape)]

        def sem(name):
            return ctx.enter_context(nc.semaphore(name))

        X = sb("X", [P, B * TILES, E])
        w13 = sb("w13", [P, KT, UNITS * 2 * I])
        w2 = sb("w2", [P, 2, UNITS * E])
        gates_w = sb("gates_w", [P, KT, NE + 1])
        wqkv = sb("wqkv", [P, KT, 3 * E])
        wo = sb("wo", [P, KT, E])
        wl = sb("wl", [P, KT, LCOLS])
        wlb = sb("wlb", [LR, E])
        wmix = sb("wmix", [P, KT, E])
        bqkv = sb("bqkv", [P, 3 * E])
        bo = sb("bo", [P, E])
        bl = sb("bl", [P, E])
        blh = sb("blh", [P, E])
        bgate = sb("bgate", [P, LE])
        bmix = sb("bmix", [P, E])
        gnw = sb("gnw", [P, E])
        gnb = sb("gnb", [P, E])
        ident = sb("ident", [P, P])
        identb = sb("identb", [P, P], BF16)
        mask_qk = sb("mask_qk", [P, P], BF16)
        mask_kq = sb("mask_kq", [P, P], BF16)
        iota16 = sb("iota16", [P, NE])
        rope_a = sb("rope_a", [P, TILES, 2, D])
        rope_m = sb("rope_m", [P, TILES, 2, RD])
        epsc = sb("epsc", [P, G * TILES])
        mhalf = sb("mhalf", [P, G * TILES])
        stats = sb("stats", [P, TILES, 6])
        mv = sb("mv", [P, B * TILES, 2])
        mvb = sb("mvb", [P, TILES, 2])
        veps = sb("veps", [P, TILES])
        rstd = sb("rstd", [P, B * TILES])
        xn = sb("xn", [P, TILES, E])
        xnT = sb("xnT", [P, KT, T])
        ffn_coef = sb("ffn_coef", [P, B * TILES, UNITS])
        work = sb("work", [P, WORK])

        used = [0]

        def part(shape, dt=F32):
            n = int(np.prod(shape[1:]))
            words = n if dt in (F32, U32) else (n + 1) // 2
            ap = work[0:shape[0], used[0]:used[0] + words]
            used[0] += words
            assert used[0] <= WORK, used[0]
            if dt != F32:
                ap = ap.bitcast(dt)
            if len(shape) == 3:
                ap = ap.rearrange("p (a b) -> p a b", b=shape[2])
            if len(shape) == 4:
                ap = ap.rearrange("p (a b c) -> p a b c", b=shape[2], c=shape[3])
            return ap

        bank = [ctx.enter_context(nc.psum_tensor(f"bank{i}", [P, 512], F32))[:, :] for i in range(8)]

        s_w = {n: sem(f"s_{n}") for n in ("x", "const", "ffn")}
        s_init = sem("s_init")
        s_out = sem("s_out")
        s_pool = sem("s_pool")
        s_go = sem("s_go")
        s_stood = sem("s_stood")
        PHASES = ("f0", "at", "f1", "l0", "mx", "l1")
        done = {p: sem(f"done_{p}") for p in PHASES}

        counted = []

        def sems(ph, names):
            made = {n: sem(f"{ph}_{n}") for n in names.split()}
            counted.extend(made.values())
            return made

        PREP = "stats aggr mv veps rstd xn xt xnT prev"
        ro = {p: sems(p + "r", PREP + " logits lg chain ex") for p in ("f0", "f1")}
        un = {p: sems(p + "u", "xn xt xnT up act hid tr hT down acc") for p in ("f0", "f1")}
        at = sems("at", PREP + " qk v qkb vb rot_c chain split tr qkT s mx m3 m3T m3s maxrow st pexp pv osb on onT oT wo tmp x")
        lo = {p: sems(p, PREP + " up lg chain ex gated tr gT lora x") for p in ("l0", "l1")}
        mi = sems("mx", PREP + " up chain th ve rs tr x")

        block = ctx.enter_context(nc.Block())

        def need(eng, sem, n):
            eng.wait_ge(sem, n + 1)

        def stand(eng, sem, n):
            need(eng, sem, n)
            eng.sem_inc(s_stood, 1)

        def each_batch(eng):
            return eng.Fori(0, B)

        def ln_vector(v, s, b, with_stats=True):
            if with_stats:
                for j in range(TILES):
                    v.bn_stats(stats[:, j, :], X[:, b * TILES + j, :]).then_inc(s["stats"], 1)
                stand(v, s["stats"], (b + 1) * TILES)
                for j in range(TILES):
                    v.bn_aggr(mvb[:, j, :], stats[:, j, :]).then_inc(s["aggr"], 1)
                need(v, s["aggr"], (b + 1) * TILES)
                v.tensor_copy(mv[:, bass.ds(b * TILES, TILES), :], mvb[:, :, :]).then_inc(s["mv"], 1)
                need(v, s["rstd"], b + 1)
            need(v, s["xt"], b)
            for j in range(TILES):
                t = b * TILES + j
                v.tensor_scalar(xn[:, j, :], X[:, t, :], mv[:, t, 0:1], rstd[:, bass.ds(t, 1)],
                                ALU.subtract, ALU.mult).then_inc(s["xn"], 1)

        def ln_gpsimd(g, s, b):
            need(g, s["mv"], b + 1)
            g.tensor_tensor(veps[:, :], mv[:, bass.ds(b * TILES, TILES), 1], epsc[:, 0:TILES], ALU.add).then_inc(s["veps"], 1)
            need(g, s["veps"], b + 1)
            g.tensor_tensor(rstd[:, bass.ds(b * TILES, TILES)], veps[:, :], mhalf[:, 0:TILES], ALU.pow).then_inc(s["rstd"], 1)

        def ln_tensor(t, s, b):
            need(t, s["xn"], (b + 1) * TILES)
            need(t, s["xnT"], b * KT)
            for k in range(KT):
                for j in range(TILES):
                    m = t.transpose(bank[k][:, j * P:(j + 1) * P], xn[:, j, k * P:(k + 1) * P], ident[:, :])
            m.then_inc(s["xt"], 1)

        def ln_scalar(a, s, b, natural=False):
            need(a, s["xt"], b + 1)
            need(a, s["prev"], b)
            for k in range(KT):
                if natural:
                    dst = xnT[:, k, :].rearrange("p (h t o) -> p h o t", h=2, o=2)
                    src = bank[k][:, :].rearrange("p (h o t) -> p h o t", h=2, o=2)
                else:
                    dst, src = xnT[:, k, :], bank[k][:, :]
                a.activation(dst, src, ACT.Copy).then_inc(s["xnT"], 1)

        used[0] = 0
        lg = part([P, TILES, NE + 1])
        lgs = part([P, TILES, NE])
        top8 = part([P, TILES, 8])
        idx8 = part([P, TILES, 8], U32)
        idxf = part([P, TILES, 8])
        ex = part([P, TILES, NE + 1])
        den = part([P, TILES])
        rden = part([P, TILES])
        onehot = part([P, TILES, TOPK, NE])
        sg = part([P, 2, I])
        hid = part([P, 2, I])
        hT = part([HK, 2, 2 * P])
        psL = bank[2][:, 0:TILES * 32].rearrange("p (j c) -> p j c", c=32)[:, :, 0:NE + 1]

        def router_tensor(t, s):
            with each_batch(t) as b:
                ln_tensor(t, s, b)
                need(t, s["xnT"], (b + 1) * KT)
                need(t, s["lg"], b)
                for j in range(TILES):
                    for k in range(KT):
                        m = t.matmul(bank[2][:, j * 32:j * 32 + NE + 1], xnT[:, k, j * P:(j + 1) * P],
                                     gates_w[:, k, :], start=(k == 0), stop=(k == KT - 1))
                m.then_inc(s["prev"], 1)

        def router_scalar(a, s):
            with each_batch(a) as b:
                ln_scalar(a, s, b)
                need(a, s["logits"], b + 1)
                a.activation(ex[:, :, 0:NE], lgs[:, :, :], ACT.Exp).then_inc(s["ex"], 1)
                a.activation(ex[:, :, NE:NE + 1], lg[:, :, NE:NE + 1], ACT.Exp, scale=-1.0).then_inc(s["ex"], 1)

        def router_gpsimd(g, s):
            with each_batch(g) as b:
                ln_gpsimd(g, s, b)

        def router_vector(v, s):
            ch = Chain(v, s["chain"], 12, need)
            with each_batch(v) as b:
                ch.start(b)
                ln_vector(v, s, b)
                need(v, s["prev"], b + 1)
                v.tensor_copy(lg[:, :, :], psL).then_inc(s["lg"], 1)
                stand(v, s["lg"], b + 1)
                for j in range(TILES):
                    ins = v.max(top8[:, j, :], lg[:, j, 0:NE])
                ch.step(ins, stand)
                for j in range(TILES):
                    ins = v.max_index(idx8[:, j, :], top8[:, j, :], lg[:, j, 0:NE])
                ch.step(ins)
                ch.step(v.tensor_copy(idxf[:, :, :], idx8[:, :, :]))
                v.tensor_tensor(lgs[:, :, :], lg[:, :, 0:NE], top8[:, :, 0:1].to_broadcast([P, TILES, NE]),
                                ALU.subtract).then_inc(s["logits"], 1)
                ch.step(v.tensor_tensor(
                    onehot[:, :, :, :], idxf[:, :, 0:TOPK].unsqueeze(3).to_broadcast([P, TILES, TOPK, NE]),
                    iota16[:, :].unsqueeze(1).unsqueeze(1).to_broadcast([P, TILES, TOPK, NE]), ALU.is_equal))
                need(v, s["ex"], 2 * b + 2)
                ch.step(v.tensor_reduce(den[:, :], ex[:, :, 0:NE], AX_X, ALU.add))
                ch.step(v.reciprocal(rden[:, :], den[:, :]))
                ch.step(v.tensor_scalar(rden[:, :], rden[:, :], 0.5, None, ALU.mult))
                ch.step(v.tensor_tensor(lgs[:, :, :], ex[:, :, 0:NE],
                                        rden[:, :].unsqueeze(2).to_broadcast([P, TILES, NE]), ALU.mult))
                ch.step(v.tensor_tensor(onehot[:, :, :, :], onehot[:, :, :, :],
                                        lgs[:, :, :].unsqueeze(2).to_broadcast([P, TILES, TOPK, NE]), ALU.mult))
                v.tensor_reduce(ffn_coef[:, bass.ds(b * TILES, TILES), 0:NE],
                                onehot[:, :, :, :].rearrange("p j k e -> p j e k"), AX_X, ALU.add)
                ch.step(v.tensor_scalar(den[:, :], ex[:, :, NE], 2.0, 2.0, ALU.mult, ALU.add))
                ch.step(v.reciprocal(rden[:, :], den[:, :]))
                ch.step(v.tensor_copy(ffn_coef[:, bass.ds(b * TILES, TILES), NE:UNITS],
                                      rden[:, :].unsqueeze(2).to_broadcast([P, TILES, SH])))
                ch.end()

        AHEAD = 2

        def unit_up(t, s, u, j, e):
            need(t, s["hid"], u + 1)
            for k in range(KT):
                m = t.matmul(bank[2 + j % 2][:, 0:2 * I], xnT[:, k, j * P:(j + 1) * P],
                             w13[:, k, bass.ds(e * (2 * I), 2 * I)], start=(k == 0), stop=(k == KT - 1))
            m.then_inc(s["up"], 1)

        def unit_tr(t, s, u, j):
            need(t, s["hid"], u + 1 + AHEAD)
            need(t, s["hT"], u + 1)
            for c in range(2):
                m = t.transpose(bank[4 + j % 2][0:HK, c * P:(c + 1) * P], hid[:, j % 2, c * HK:(c + 1) * HK],
                                ident[:, :])
            m.then_inc(s["tr"], 1)

        def unit_down(t, s, u, j, e):
            need(t, s["hT"], u + 1 + AHEAD)
            need(t, s["acc"], u + 1)
            for c in range(2):
                m = t.matmul(bank[6 + j % 2][:, 0:E], hT[:, j % 2, c * P:(c + 1) * P],
                             w2[0:HK, c, bass.ds(e * E, E)], start=(c == 0), stop=(c == 1))
            m.then_inc(s["down"], 1)

        def units_tensor(t, s):
            with each_batch(t) as b:
                ln_tensor(t, s, b)
                stand(t, s["xnT"], (b + 1) * KT)
                with t.Fori(0, UNITS) as e:
                    u = (b * UNITS + e) * TILES
                    for j in range(TILES + 2):
                        if j < TILES:
                            unit_up(t, s, u + j, j, e)
                        if 1 <= j <= TILES:
                            unit_tr(t, s, u + j - 1, j - 1)
                        if j >= 2:
                            unit_down(t, s, u + j - 2, j - 2, e)

        def units_scalar(a, s):
            a.sem_inc(s["hT"], AHEAD)
            with each_batch(a) as b:
                need(a, s["xt"], b + 1)
                need(a, s["up"], b * UNITS * TILES)
                for k in range(KT):
                    a.activation(xnT[:, k, :], bank[k][:, :], ACT.Copy).then_inc(s["xnT"], 1)
                with a.Fori(0, UNITS) as e:
                    u = (b * UNITS + e) * TILES
                    for j in range(TILES + 1):
                        if j < TILES:
                            need(a, s["up"], u + j + 1)
                            need(a, s["hid"], u + j + 1)
                            a.activation(sg[:, j % 2, :], bank[2 + j % 2][:, 0:I], ACT.Silu).then_inc(s["act"], 1)
                        if j >= 1:
                            i = j - 1
                            need(a, s["tr"], u + i + 1 + AHEAD)
                            need(a, s["down"], u + i + 1)
                            a.activation(hT[:, i % 2, :], bank[4 + i % 2][0:HK, 0:2 * P], ACT.Copy).then_inc(s["hT"], 1)

        def units_vector(v, s):
            v.sem_inc(s["hid"], AHEAD)
            v.sem_inc(s["acc"], AHEAD)
            v.sem_inc(s["tr"], AHEAD)
            v.sem_inc(s["down"], AHEAD)
            with each_batch(v) as b:
                ln_vector(v, s, b, with_stats=False)
                with v.Fori(0, UNITS) as e:
                    u = (b * UNITS + e) * TILES
                    for j in range(TILES + 2):
                        if j < TILES:
                            need(v, s["act"], u + j + 1)
                            need(v, s["tr"], u + j + 1)
                            v.scalar_tensor_tensor(out=hid[:, j % 2, :], in0=sg[:, j % 2, :],
                                                   scalar=ffn_coef[:, b * TILES + j, bass.ds(e, 1)],
                                                   in1=bank[2 + j % 2][:, I:2 * I],
                                                   op0=ALU.mult, op1=ALU.mult).then_inc(s["hid"], 1)
                        if j >= 2:
                            i = j - 2
                            t = b * TILES + i
                            need(v, s["down"], u + i + 1 + AHEAD)
                            v.tensor_tensor(X[:, t, :], X[:, t, :], bank[6 + i % 2][:, 0:E], ALU.add).then_inc(s["acc"], 1)

        used[0] = 0
        QT, KTt = (w2[:, i, 0:H * T // 2].bitcast(BF16).rearrange("p (h t) -> p h t", t=T) for i in range(2))
        stk = part([P, 2 * H, STACK], BF16)
        qk = part([P, 2 * H, D])
        rc = part([P, 2 * H, D])
        rs = part([P, 2 * H, D])
        V = part([P, TILES, H, D + 1])
        nmx = part([P, TILES, H])
        m3 = part([P, TILES, 3, H], BF16)
        m3T = part([48, T], BF16)
        OFF = [0, 512, 896, 1152]
        PT = part([P, 2, 1280])
        osb = part([P, TILES, H, D + 1])
        ors = part([P, TILES * H])
        at_end = used[0]
        on, oT = xn, xnT
        HG = 4

        def psT(i):
            return bank[i][:, :].bitcast(BF16)

        def attn_tensor(t):
            s = at
            t.wait_ge(s_init, INIT + 1)
            with each_batch(t) as b:
                ln_tensor(t, s, b)
                need(t, s["xnT"], (b + 1) * KT)
                for n in range(TILES):
                    i = b * TILES + n
                    if n >= 2:
                        need(t, s["qkb"], i - 1)
                    for k in range(KT):
                        m = t.matmul(bank[2 + n % 2][:, :], xnT[:, k, n * P:(n + 1) * P], wqkv[:, k, 0:2 * E],
                                     start=(k == 0), stop=(k == KT - 1))
                    m.then_inc(s["qk"], 1)
                    if n >= 2:
                        need(t, s["vb"], i - 1)
                    for k in range(KT):
                        m = t.matmul(bank[4 + n % 2][:, 0:E], xnT[:, k, n * P:(n + 1) * P], wqkv[:, k, 2 * E:3 * E],
                                     start=(k == 0), stop=(k == KT - 1))
                    m.then_inc(s["v"], 1)
                for n in range(TILES):
                    need(t, s["split"], b * TILES + n + 1)
                    for g in range(4):
                        r = n * 4 + g
                        need(t, s["qkT"], b * 16 + r - 1) if r >= 2 else need(t, s["xnT"], (b + 1) * KT)
                        for h in range(8):
                            m = t.transpose(psT(g % 2)[0:STACK, h * P:(h + 1) * P], stk[:, g * 8 + h, :], identb[:, :])
                        m.then_inc(s["tr"], 1)
                need(t, s["qkT"], (b + 1) * 16)
                need(t, s["vb"], (b + 1) * TILES)
                for i, (n, hs) in enumerate(MAX_STEPS):
                    w = (n + 1) * P
                    if i >= 2:
                        need(t, s["mx"], b * len(MAX_STEPS) + i - 1)
                    for c, h in enumerate(hs):
                        o = c * w
                        t.matmul(bank[2 + i % 2][:, o:o + w], QT[0:STACK, h, n * P:(n + 1) * P], KTt[0:STACK, h, 0:w],
                                 start=(c == 0), stop=False, skip_group_check=True)
                        m = t.matmul(bank[2 + i % 2][:, o + n * P:o + w], identb[:, :], mask_qk[:, :],
                                     start=False, stop=True, skip_group_check=True)
                    m.then_inc(s["s"], 1)
                stand(t, s["m3"], b + 1)
                for n in range(TILES):
                    m = t.transpose(psT(0)[0:48, n * P:(n + 1) * P], m3[:, n, :, :].rearrange("p c h -> p (c h)"), identb[:, :])
                m.then_inc(s["m3T"], 1)
                need(t, s["maxrow"], (b + 1) * 48)
                for h in range(H + 1):
                    if h < H:
                        for n in range(TILES):
                            i = h * TILES + n
                            w = T - n * P
                            if i >= 2:
                                need(t, s["pexp"], b * H * TILES + i - 1)
                            t.matmul(bank[4 + i % 2][:, 0:w], KTt[0:ROWS, h, n * P:(n + 1) * P], QT[0:ROWS, h, n * P:T],
                                     start=True, stop=False, skip_group_check=True)
                            m = t.matmul(bank[4 + i % 2][:, 0:P], identb[:, :], mask_kq[:, :],
                                         start=False, stop=True, skip_group_check=True)
                            m.then_inc(s["st"], 1)
                    if h >= 1:
                        g = h - 1
                        need(t, s["pexp"], (b * H + g + 1) * TILES)
                        if g % HG == 0 and g // HG >= 2:
                            need(t, s["osb"], b * (H // HG) + g // HG - 1)
                        ps = bank[6 + g // HG % 2]
                        for n in range(TILES):
                            o = ((g % HG) * TILES + n) * (D + 1)
                            for k in range(n + 1):
                                m = t.matmul(ps[:, o:o + D + 1], PT[:, g % 2, OFF[k] + (n - k) * P:OFF[k] + (n - k + 1) * P],
                                             V[:, k, g, :], start=(k == 0), stop=(k == n))
                        m.then_inc(s["pv"], 1)
                need(t, s["on"], b + 1)
                for c in range(KT):
                    for n in range(TILES):
                        m = t.transpose(bank[c][:, n * P:(n + 1) * P], on[:, n, c * P:(c + 1) * P], ident[:, :])
                m.then_inc(s["onT"], 1)
                need(t, s["oT"], (b + 1) * KT)
                for j in range(TILES):
                    if j >= 2:
                        need(t, s["tmp"], b * TILES + j - 1)
                    for c in range(KT):
                        cols = oT[:, c, :].rearrange("p (h t o) -> p h o t", h=2, o=2)[:, j // 2, j % 2, :]
                        m = t.matmul(bank[6 + j % 2][:, 0:E], cols, wo[:, c, :], start=(c == 0), stop=(c == KT - 1))
                    m.then_inc(s["wo"], 1)
                need(t, s["x"], (b + 1) * TILES)

        MAX_STEPS = [(0, list(range(4 * i, 4 * i + 4))) for i in range(4)]
        MAX_STEPS += [(1, [2 * i, 2 * i + 1]) for i in range(8)]
        MAX_STEPS += [(2, [i]) for i in range(16)] + [(3, [i]) for i in range(16)]

        def attn_scalar(a):
            s = at
            with each_batch(a) as b:
                need(a, s["xt"], b + 1)
                need(a, s["x"], b * TILES)
                for k in range(KT):
                    dst = xnT[:, k, :].rearrange("p (h t o) -> p h o t", h=2, o=2)
                    src = bank[k][:, :].rearrange("p (h o t) -> p h o t", h=2, o=2)
                    for hf in range(2):
                        ins = a.activation(dst[:, hf], src[:, hf], ACT.Copy)
                    ins.then_inc(s["xnT"], 1)
                for n in range(TILES):
                    for g in range(4):
                        r = n * 4 + g
                        need(a, s["tr"], b * 16 + r + 1)
                        dst = QT if g < 2 else KTt
                        a.activation(dst[0:STACK, (g % 2) * 8:(g % 2) * 8 + 8, n * P:(n + 1) * P],
                                     psT(g % 2)[0:STACK, :].rearrange("p (h t) -> p h t", h=8), ACT.Copy).then_inc(s["qkT"], 1)
                need(a, s["m3T"], b + 1)
                a.activation(m3T[:, :], psT(0)[0:48, 0:T], ACT.Copy).then_inc(s["m3s"], 1)
                need(a, s["st"], b * H * TILES + 1)
                for h in range(H):
                    for n in range(TILES):
                        i = h * TILES + n
                        need(a, s["st"], b * H * TILES + i + 1)
                        if n == 0 and h >= 2:
                            need(a, s["pv"], b * H + h - 1)
                        w = T - n * P
                        a.activation(PT[:, h % 2, OFF[n]:OFF[n] + w], bank[4 + i % 2][:, 0:w], ACT.Exp,
                                     scale=float(D) ** -0.5).then_inc(s["pexp"], 1)
                need(a, s["onT"], b + 1)
                for c in range(KT):
                    a.activation(oT[:, c, :], bank[c][:, :], ACT.Copy).then_inc(s["oT"], 1)

        def attn_vector(v):
            s = at
            v.memset(V[:, :, :, D:D + 1], 1.0)
            v.memset(KTt[96:96 + 3, :, :], 1.0).then_inc(s_init, 1)
            v.wait_ge(s_init, INIT + 1)
            ch = Chain(v, s["chain"], 5 * TILES + 4, need)
            with each_batch(v) as b:
                ch.start(b)
                ln_vector(v, s, b)
                for n in range(TILES):
                    i = b * TILES + n
                    need(v, s["qk"], i + 1)
                    need(v, s["rot_c"], i)
                    v.tensor_tensor(qk[:, :, :].rearrange("p h d -> p (h d)"), bank[2 + n % 2][:, :], bqkv[:, 0:2 * E],
                                    ALU.add).then_inc(s["qkb"], 1)
                    need(v, s["v"], i + 1)
                    v.tensor_tensor(V[:, n, :, 0:D], bank[4 + n % 2][:, 0:E].rearrange("p (h d) -> p h d", d=D),
                                    bqkv[:, 2 * E:3 * E].rearrange("p (h d) -> p h d", d=D), ALU.add).then_inc(s["vb"], 1)
                    need(v, s["qkb"], i + 1)
                    pairs = qk[:, :, :].rearrange("p h (i o) -> p h i o", o=2)
                    turned = rs[:, :, :].rearrange("p h (i o) -> p h i o", o=2)
                    sine = rope_a[:, n, 1, :].rearrange("p (i o) -> p i o", o=2)
                    for o in range(2):
                        ins = v.tensor_tensor(turned[:, :, :, o], pairs[:, :, :, 1 - o],
                                              sine[:, :, o].unsqueeze(1).to_broadcast([P, 2 * H, D // 2]), ALU.mult)
                    ch.step(ins)
                    need(v, s["rot_c"], i + 1)
                    ch.step(v.tensor_tensor(rc[:, :, :], rc[:, :, :], rs[:, :, :], ALU.add))
                    need(v, s["tr"], b * 16 + 4 * n)
                    q_a, k_a = (0, 1, 2), (0, 3, 5)
                    for side, blocks in ((0, q_a), (1, k_a)):
                        for c in blocks:
                            ins = v.tensor_copy(stk[:, side * H:side * H + H, c * D:(c + 1) * D], rc[:, side * H:side * H + H, :])
                    ch.step(ins)
                    ch.step(v.tensor_tensor(rs[:, :, :], rc[:, :, :], stk[:, :, 0:D], ALU.subtract))
                    for side, blocks in ((0, (3, 4)), (1, (1, 4))):
                        for c in blocks:
                            ins = v.tensor_copy(stk[:, side * H:side * H + H, c * D:(c + 1) * D], rs[:, side * H:side * H + H, :])
                    ch.step(ins)
                    v.tensor_tensor(stk[:, 0:H, 5 * D:6 * D], rs[:, 0:H, :], stk[:, 0:H, 4 * D:5 * D], ALU.subtract)
                    v.tensor_tensor(stk[:, H:2 * H, 2 * D:3 * D], rs[:, H:2 * H, :], stk[:, H:2 * H, 4 * D:5 * D],
                                    ALU.subtract).then_inc(s["split"], 1)
                for i, (n, hs) in enumerate(MAX_STEPS):
                    need(v, s["s"], b * len(MAX_STEPS) + i + 1)
                    w = (n + 1) * P
                    v.tensor_reduce(nmx[:, n, hs[0]:hs[0] + len(hs)],
                                    bank[2 + i % 2][:, 0:len(hs) * w].rearrange("p (h k) -> p h k", k=w),
                                    AX_X, ALU.max, negate=True).then_inc(s["mx"], 1)
                need(v, s["mx"], (b + 1) * len(MAX_STEPS))
                flat = rc[:, :, :].rearrange("p h d -> p (h d)")[:, 0:TILES * H].rearrange("p (n h) -> p n h", h=H)
                ch.step(v.tensor_copy(m3[:, :, 0, :], nmx[:, :, :]))
                ch.step(v.tensor_tensor(flat, nmx[:, :, :], m3[:, :, 0, :], ALU.subtract))
                ch.step(v.tensor_copy(m3[:, :, 1, :], flat))
                v.tensor_tensor(m3[:, :, 2, :], flat, m3[:, :, 1, :], ALU.subtract).then_inc(s["m3"], 1)
                for g in range(H // HG):
                    need(v, s["pv"], b * H + (g + 1) * HG)
                    v.tensor_copy(osb[:, :, g * HG:(g + 1) * HG, :],
                                  bank[6 + g % 2][:, 0:HG * TILES * (D + 1)].rearrange("p (h n d) -> p n h d", n=TILES, d=D + 1)
                                  ).then_inc(s["osb"], 1)
                need(v, s["osb"], (b + 1) * (H // HG))
                o3 = osb[:, :, :, :].rearrange("p n h d -> p (n h) d")
                ch.step(v.reciprocal(ors[:, :], o3[:, :, D]))
                v.tensor_tensor(on[:, :, :].rearrange("p n (h d) -> p (n h) d", d=D), o3[:, :, 0:D],
                                ors[:, :].unsqueeze(2).to_broadcast([P, TILES * H, D]), ALU.mult).then_inc(s["on"], 1)
                for j in range(TILES):
                    t = b * TILES + j
                    need(v, s["wo"], t + 1)
                    tmp = osb[:, :, :, :].rearrange("p n h d -> p (n h d)")[:, j * E:(j + 1) * E]
                    v.tensor_tensor(tmp, bank[6 + j % 2][:, 0:E], bo[:, :], ALU.add).then_inc(s["tmp"], 1)
                    need(v, s["tmp"], t + 1)
                    v.tensor_tensor(X[:, t, :], X[:, t, :], tmp, ALU.add).then_inc(s["x"], 1)
                need(v, s["x"], (b + 1) * TILES)
                ch.end()

        def attn_gpsimd(g):
            s = at
            with each_batch(g) as b:
                ln_gpsimd(g, s, b)
                for n in range(TILES):
                    i = b * TILES + n
                    need(g, s["qkb"], i + 1)
                    need(g, s["split"], i)
                    g.tensor_tensor(rc[:, :, :], qk[:, :, :],
                                    rope_a[:, n, 0, :].unsqueeze(1).to_broadcast([P, 2 * H, D]), ALU.mult).then_inc(s["rot_c"], 1)

        def attn_sync(sp):
            s = at
            with each_batch(sp) as b:
                need(sp, s["m3s"], b + 1)
                for c in range(3):
                    sp.dma_start(QT[STACK + c:STACK + c + 1, :, :], m3T[c * H:(c + 1) * H, :]).then_inc(s["maxrow"], 16)

        used[0] = 0
        llg = part([P, TILES, LE])
        ltop = part([P, TILES, 8])
        lidx = part([P, TILES, 8], U32)
        lidxf = part([P, TILES, 8])
        ldiff = part([P, TILES, 1])
        lex = part([P, TILES, 1])
        lgw = part([P, TILES, LK])
        loh = part([P, TILES, LK, LE])
        lgm = part([P, TILES, LE])
        gxa = part([P, TILES, LR])
        gT = part([LR, T])

        def lora_tensor(t, s):
            with each_batch(t) as b:
                ln_tensor(t, s, b)
                need(t, s["xnT"], (b + 1) * KT)
                need(t, s["x"], b * TILES)
                for j in range(TILES):
                    for k in range(KT):
                        m = t.matmul(bank[2 + j][:, 0:LCOLS], xnT[:, k, j * P:(j + 1) * P], wl[:, k, :],
                                     start=(k == 0), stop=(k == KT - 1))
                    m.then_inc(s["up"], 1)
                need(t, s["gated"], b + 1)
                for j in range(TILES):
                    m = t.transpose(bank[6][:, j * P:(j + 1) * P], gxa[:, j, :], ident[:, :])
                m.then_inc(s["tr"], 1)
                need(t, s["gT"], b + 1)
                for j in range(TILES):
                    m = t.matmul(bank[2 + j][:, 0:E], gT[:, j * P:(j + 1) * P], wlb[:, :], start=False, stop=True,
                                 skip_group_check=True)
                    m.then_inc(s["lora"], 1)

        def lora_scalar(a, s):
            with each_batch(a) as b:
                need(a, s["xt"], b + 1)
                need(a, s["up"], b * TILES)
                for k in range(KT):
                    a.activation(xnT[:, k, :], bank[k][:, :], ACT.Copy).then_inc(s["xnT"], 1)
                need(a, s["lg"], b + 1)
                a.activation(lex[:, :, :], ldiff[:, :, :], ACT.Exp).then_inc(s["ex"], 1)
                need(a, s["tr"], b + 1)
                a.activation(gT[:, :], bank[6][:, :], ACT.Copy).then_inc(s["gT"], 1)

        def lora_gpsimd(g, s):
            with each_batch(g) as b:
                ln_gpsimd(g, s, b)

        def lora_vector(v, s):
            ch = Chain(v, s["chain"], 11, need)
            with each_batch(v) as b:
                ch.start(b)
                ln_vector(v, s, b)
                need(v, s["up"], (b + 1) * TILES)
                for j in range(TILES):
                    ins = v.tensor_tensor(llg[:, j, :], bank[2 + j][:, E + LR:LCOLS], bgate[:, :], ALU.add)
                ch.step(ins, stand)
                for j in range(TILES):
                    ins = v.max(ltop[:, j, :], llg[:, j, :])
                ch.step(ins)
                v.tensor_tensor(ldiff[:, :, :], ltop[:, :, 1:2], ltop[:, :, 0:1], ALU.subtract).then_inc(s["lg"], 1)
                for j in range(TILES):
                    ins = v.max_index(lidx[:, j, :], ltop[:, j, :], llg[:, j, :])
                ch.step(ins)
                ch.step(v.tensor_copy(lidxf[:, :, :], lidx[:, :, :]))
                ch.step(v.tensor_tensor(
                    loh[:, :, :, :], lidxf[:, :, 0:LK].unsqueeze(3).to_broadcast([P, TILES, LK, LE]),
                    iota16[:, 0:LE].unsqueeze(1).unsqueeze(1).to_broadcast([P, TILES, LK, LE]), ALU.is_equal))
                need(v, s["ex"], b + 1)
                ch.step(v.tensor_scalar(ldiff[:, :, :], lex[:, :, :], 1.0, None, ALU.add))
                ch.step(v.reciprocal(lgw[:, :, 0:1], ldiff[:, :, :]))
                ch.step(v.tensor_tensor(lgw[:, :, 1:2], lex[:, :, :], lgw[:, :, 0:1], ALU.mult))
                ch.step(v.tensor_tensor(loh[:, :, :, :], loh[:, :, :, :],
                                        lgw[:, :, :].unsqueeze(3).to_broadcast([P, TILES, LK, LE]), ALU.mult))
                ch.step(v.tensor_reduce(lgm[:, :, :], loh[:, :, :, :].rearrange("p j k e -> p j e k"), AX_X, ALU.add))
                for j in range(TILES):
                    ins = v.tensor_tensor(gxa[:, j, :].rearrange("p (e r) -> p e r", r=R),
                                          bank[2 + j][:, E:E + LR].rearrange("p (e r) -> p e r", r=R),
                                          lgm[:, j, :].unsqueeze(2).to_broadcast([P, LE, R]), ALU.mult)
                ins.then_inc(s["gated"], 1)
                for j in range(TILES):
                    ins = v.tensor_tensor(X[:, b * TILES + j, :], X[:, b * TILES + j, :], blh[:, :], ALU.add)
                ch.step(ins)
                for j in range(TILES):
                    t = b * TILES + j
                    need(v, s["lora"], t + 1)
                    v.scalar_tensor_tensor(out=X[:, t, :], in0=bank[2 + j][:, 0:E], scalar=0.5, in1=X[:, t, :],
                                           op0=ALU.mult, op1=ALU.add).then_inc(s["x"], 1)
                ch.end()

        used[0] = 0
        mr = part([P, TILES, RD])
        ms = part([P, TILES, RD])
        pre = part([P, TILES, E])
        hh = part([P, TILES, E])
        sq = part([P, TILES, E])
        mu = part([P, TILES * G])
        var = part([P, TILES * G])

        def mix_tensor(t):
            s = mi
            with each_batch(t) as b:
                ln_tensor(t, s, b)
                need(t, s["xnT"], (b + 1) * KT)
                need(t, s["x"], b * KT)
                for j in range(TILES):
                    for k in range(KT):
                        m = t.matmul(bank[2 + j][:, 0:E], xnT[:, k, j * P:(j + 1) * P], wmix[:, k, :],
                                     start=(k == 0), stop=(k == KT - 1))
                    m.then_inc(s["up"], 1)
                need(t, s["chain"], b * 14 + 14)
                for c in range(KT):
                    for j in range(TILES):
                        m = t.transpose(bank[6 + c][:, j * P:(j + 1) * P], hh[:, j, c * P:(c + 1) * P], ident[:, :])
                m.then_inc(s["tr"], 1)

        def mix_scalar(a):
            s = mi
            with each_batch(a) as b:
                need(a, s["xt"], b + 1)
                need(a, s["up"], b * TILES)
                for k in range(KT):
                    a.activation(xnT[:, k, :], bank[k][:, :], ACT.Copy).then_inc(s["xnT"], 1)
                need(a, s["chain"], b * 14 + 5)
                a.activation(hh[:, :, :], pre[:, :, :], ACT.Tanh).then_inc(s["th"], 1)

        def mix_gpsimd(g):
            s = mi
            with each_batch(g) as b:
                ln_gpsimd(g, s, b)
                need(g, s["chain"], b * 14 + 11)
                g.tensor_tensor(mu[:, :], var[:, :], mhalf[:, :], ALU.pow).then_inc(s["rs"], 1)

        def mix_vector(v):
            s = mi
            ch = Chain(v, s["chain"], 14, need)
            with each_batch(v) as b:
                ch.start(b)
                ln_vector(v, s, b)
                need(v, s["up"], (b + 1) * TILES)
                for j in range(TILES):
                    ps = bank[2 + j][:, 0:RD]
                    v.tensor_tensor(mr[:, j, :], ps, rope_m[:, j, 0, :], ALU.mult)
                    for o in range(2):
                        ins = v.tensor_tensor(ms[:, j, :].rearrange("p (i o) -> p i o", o=2)[:, :, o],
                                              ps.rearrange("p (i o) -> p i o", o=2)[:, :, 1 - o],
                                              rope_m[:, j, 1, :].rearrange("p (i o) -> p i o", o=2)[:, :, o], ALU.mult)
                ch.step(ins)
                ch.step(v.tensor_tensor(mr[:, :, :], mr[:, :, :], ms[:, :, :], ALU.add))
                for j in range(TILES):
                    ins = v.scalar_tensor_tensor(out=pre[:, j, RD:E], in0=bank[2 + j][:, RD:E], scalar=0.0,
                                                 in1=bmix[:, RD:E], op0=ALU.max, op1=ALU.add)
                ch.step(ins)
                ch.step(v.tensor_scalar(mr[:, :, :], mr[:, :, :], 0.0, None, ALU.max))
                ch.step(v.tensor_tensor(pre[:, :, 0:RD], mr[:, :, :], bmix[:, 0:RD].unsqueeze(1).to_broadcast([P, TILES, RD]),
                                        ALU.add))
                need(v, s["th"], b + 1)
                groups = hh[:, :, :].rearrange("p j (g c) -> p (j g) c", c=GC)
                squares = sq[:, :, :].rearrange("p j (g c) -> p (j g) c", c=GC)
                wide = [P, TILES * G, GC]
                ch.step(v.tensor_reduce(mu[:, :], groups, AX_X, ALU.add))
                ch.step(v.tensor_scalar(mu[:, :], mu[:, :], 1.0 / GC, None, ALU.mult))
                ch.step(v.tensor_tensor(groups, groups, mu[:, :].unsqueeze(2).to_broadcast(wide), ALU.subtract))
                ch.step(v.tensor_tensor(squares, groups, groups, ALU.mult))
                ch.step(v.tensor_reduce(var[:, :], squares, AX_X, ALU.add))
                ch.step(v.tensor_scalar(var[:, :], var[:, :], 1.0 / GC, EPS, ALU.mult, ALU.add))
                need(v, s["rs"], b + 1)
                ch.step(v.tensor_tensor(groups, groups, mu[:, :].unsqueeze(2).to_broadcast(wide), ALU.mult))
                ch.step(v.tensor_tensor(hh[:, :, :], hh[:, :, :], gnw[:, :].unsqueeze(1).to_broadcast([P, TILES, E]), ALU.mult))
                ch.step(v.tensor_tensor(hh[:, :, :], hh[:, :, :], gnb[:, :].unsqueeze(1).to_broadcast([P, TILES, E]), ALU.add))
                need(v, s["tr"], b + 1)
                for c in range(KT):
                    for hf in range(2):
                        x = X[:, b * TILES + 2 * c + hf, :]
                        src = bank[6 + c][:, hf * E:(hf + 1) * E].rearrange("p (o t) -> p t o", o=2)
                        ins = v.tensor_tensor(x.rearrange("p (t o) -> p t o", o=2), x.rearrange("p (t o) -> p t o", o=2), src,
                                              ALU.add)
                    ins.then_inc(s["x"], 1)
                need(v, s["x"], (b + 1) * KT)
                ch.end()

        INIT = 2
        mask_f = (hh[:, 0, 0:P], hh[:, 1, 0:P])
        BIASES = ((bqkv[:, :], "bqkv"), (bo[:, :], "bo"), (bl[:, :], "bl"), (bgate[:, :], "bgate"), (bmix[:, :], "bmix"),
                  (gnw[:, :], "gnw"), (gnb[:, :], "gnb"), (iota16[:, :], "iota16"))
        WEIGHTS = ((wqkv, "wqkv"), (wo, "wo"), (wl, "wl"), (wmix, "wmix"))
        CONSTS = 16 * (3 + 2 + len(BIASES) + len(WEIGHTS) + 1)

        @block.sync
        def _(sp):
            x = d["L0_attn_x"].rearrange("b (h p o) e -> b p h (o e)", h=2, o=2)
            for b in range(B):
                sp.dma_start(X[:, bass.ds(b * TILES, TILES), :].rearrange("p (h o) e -> p h (o e)", o=2), x[b]).then_inc(s_w["x"], 16)
            for c in counted:
                sp.sem_inc(c, 1)
            sp.sem_inc(s_go, 1)
            for dst, name in ((gates_w, "gates_w"), (w13, "w13")):
                sp.dma_start(dst[:, :, :], d[name].rearrange("(k p) n -> p k n", p=P)).then_inc(s_w["ffn"], 16)
            sp.dma_start(w2[0:HK, :, :], d["w2"].rearrange("(k p) n -> p k n", p=HK)).then_inc(s_w["ffn"], 16)
            sp.wait_ge(done["f0"], 1)
            attn_sync(sp)
            sp.wait_ge(done["at"], 1)
            sp.dma_start(w2[0:HK, :, :], d["w2"].rearrange("(k p) n -> p k n", p=HK)).then_inc(s_w["ffn"], 16)
            sp.wait_ge(done["l1"], 1)
            o = out.rearrange("b (h p o) e -> b p h (o e)", h=2, o=2)
            for b in range(B):
                sp.dma_start(o[b], X[:, bass.ds(b * TILES, TILES), :].rearrange("p (h o) e -> p h (o e)", o=2)).then_inc(s_out, 16)
            sp.wait_ge(s_out, 16 * B)

        @block.gpsimd
        def _(g):
            g.memset(epsc[:, :], EPS).then_inc(s_pool, 1)
            g.memset(mhalf[:, :], -0.5).then_inc(s_pool, 1)
            for dst, name in ((ident, "ident"), (mask_f[0], "mask_qk"), (mask_f[1], "mask_kq")):
                g.dma_start(dst, d[name]).then_inc(s_w["const"], 16)
            g.dma_start(rope_a[:, :, :, :], d["rope_a"].rearrange("p (n s c) -> p n s c", n=TILES, s=2)).then_inc(s_w["const"], 16)
            g.dma_start(rope_m[:, :, :, :], d["rope_m"].rearrange("p (n s c) -> p n s c", n=TILES, s=2)).then_inc(s_w["const"], 16)
            for dst, name in BIASES:
                n = d[name].shape[0]
                g.dma_start(dst, d[name].rearrange("(a n) -> a n", a=1).to_broadcast([P, n])).then_inc(s_w["const"], 16)
            for dst, name in WEIGHTS:
                g.dma_start(dst[:, :, :], d[name].rearrange("(k p) n -> p k n", p=P)).then_inc(s_w["const"], 16)
            g.dma_start(wlb[:, :], d["wlb"]).then_inc(s_w["const"], 16)
            g.wait_ge(s_pool, 2)
            g.wait_ge(s_go, 1)
            router_gpsimd(g, ro["f0"])
            g.wait_ge(done["f0"], 1)
            attn_gpsimd(g)
            g.wait_ge(done["at"], 1)
            router_gpsimd(g, ro["f1"])
            g.wait_ge(done["f1"], 1)
            lora_gpsimd(g, lo["l0"])
            g.wait_ge(done["l0"], 1)
            mix_gpsimd(g)
            g.wait_ge(done["mx"], 1)
            lora_gpsimd(g, lo["l1"])

        @block.scalar
        def _(a):
            a.wait_ge(s_go, 1)
            router_scalar(a, ro["f0"])
            units_scalar(a, un["f0"])
            a.wait_ge(done["f0"], 1)
            attn_scalar(a)
            a.wait_ge(done["at"], 1)
            router_scalar(a, ro["f1"])
            units_scalar(a, un["f1"])
            a.wait_ge(done["f1"], 1)
            lora_scalar(a, lo["l0"])
            a.wait_ge(done["l0"], 1)
            mix_scalar(a)
            a.wait_ge(done["mx"], 1)
            lora_scalar(a, lo["l1"])

        @block.tensor
        def _(t):
            t.wait_ge(s_w["const"], CONSTS)
            t.wait_ge(s_w["ffn"], 48)
            t.wait_ge(s_init, INIT)
            t.wait_ge(s_go, 1)
            router_tensor(t, ro["f0"])
            need(t, ro["f0"]["lg"], B)
            units_tensor(t, un["f0"])
            t.wait_ge(done["f0"], 1)
            attn_tensor(t)
            t.wait_ge(done["at"], 1)
            router_tensor(t, ro["f1"])
            need(t, ro["f1"]["lg"], B)
            t.wait_ge(s_w["ffn"], 64)
            units_tensor(t, un["f1"])
            t.wait_ge(done["f1"], 1)
            lora_tensor(t, lo["l0"])
            t.wait_ge(done["l0"], 1)
            mix_tensor(t)
            t.wait_ge(done["mx"], 1)
            lora_tensor(t, lo["l1"])

        @block.vector
        def _(v):
            v.wait_ge(s_w["const"], CONSTS)
            v.wait_ge(s_go, 1)
            v.tensor_copy(identb[:, :], ident[:, :])
            v.tensor_copy(mask_qk[:, :], mask_f[0])
            v.tensor_copy(mask_kq[:, :], mask_f[1]).then_inc(s_init, 1)
            v.tensor_scalar(blh[:, :], bl[:, :], 0.5, None, ALU.mult).then_inc(s_init, 1)
            v.wait_ge(s_init, INIT)
            v.wait_ge(s_w["x"], 16 * B)

            def close(ph, sem_x, n):
                need(v, sem_x, n)
                v.tensor_copy(stats[:, 0, 0:1], mv[:, 0, 0:1]).then_inc(done[ph], 1)
                v.wait_ge(done[ph], 1)

            for ph in ("f0", "at", "f1", "l0", "mx", "l1"):
                if ph in ("f0", "f1"):
                    router_vector(v, ro[ph])
                    units_vector(v, un[ph])
                    close(ph, un[ph]["acc"], B * UNITS * TILES + AHEAD)
                elif ph == "at":
                    attn_vector(v)
                    close(ph, at["x"], B * TILES)
                elif ph == "mx":
                    mix_vector(v)
                    close(ph, mi["x"], B * KT)
                else:
                    lora_vector(v, lo[ph])
                    close(ph, lo[ph]["x"], B * TILES)


def tables():
    c = {}
    c["ident"] = np.eye(P, dtype=np.float32)
    q, k = np.arange(P)[:, None], np.arange(P)[None, :]
    c["mask_qk"] = np.where(k > q, np.float32(NEG), np.float32(0))
    c["mask_kq"] = np.ascontiguousarray(c["mask_qk"].T)
    c["iota16"] = np.arange(NE, dtype=np.float32)

    def rope(pos, dim):
        inv = (np.float32(1) / np.power(np.float32(10000.0), np.arange(0, dim, 2, dtype=np.float32) / np.float32(dim))).astype(np.float32)
        ang = pos.astype(np.float32)[..., None] * inv
        cos = np.repeat(np.cos(ang), 2, -1)
        sin = np.stack([-np.sin(ang), np.sin(ang)], -1).reshape(cos.shape)
        return np.stack([cos, sin], -2).astype(np.float32)

    p, n = np.arange(P)[:, None], np.arange(TILES)[None, :]
    c["rope_a"] = rope(n * P + p, D).reshape(P, -1)
    c["rope_m"] = rope((n // 2) * 256 + 2 * p + n % 2, RD).reshape(P, -1)
    return c


def kernel(**inputs):
    import numpy as _np
    import concourse.bacc as _bacc
    from concourse import mybir as _mybir
    from concourse.bass_utils import run_bass_kernel_spmd as _run

    a = {n: _np.asarray(v) for n, v in inputs.items()}
    su = a["L0_ffn_shared_gate_up_w"].reshape(2, SH, I, E)
    host = {
        "L0_attn_x": a["L0_attn_x"],
        "gates_w": _np.concatenate([a["L0_ffn_gate_w"], a["L0_ffn_sgate_w"]], 0).T,
        "w13": _np.concatenate([a["L0_ffn_w13"].reshape(NE * 2 * I, E), su.transpose(1, 0, 2, 3).reshape(SH * 2 * I, E)], 0).T,
        "w2": _np.concatenate([a["L0_ffn_w2"].transpose(2, 0, 1),
                               a["L0_ffn_shared_down_w"].reshape(E, SH, I).transpose(2, 1, 0)], 1).reshape(I, UNITS * E),
        "wqkv": _np.concatenate([a["L0_attn_Wq"], a["L0_attn_Wk"], a["L0_attn_Wv"]], 0).T,
        "wo": a["L0_attn_Wo"].T,
        "wl": _np.concatenate([a["L1_ffn_W"], a["L1_ffn_lora_A"].reshape(LR, E), a["L1_ffn_gate_w"]], 0).T,
        "wlb": a["L1_ffn_lora_B"].transpose(0, 2, 1).reshape(LR, E),
        "wmix": a["L1_attn_W_Q"],
        "bqkv": _np.concatenate([a["L0_attn_bq"], a["L0_attn_bk"], a["L0_attn_bv"]]),
        "bo": a["L0_attn_bo"], "bl": a["L1_ffn_b"], "bgate": a["L1_ffn_gate_b"], "bmix": a["L1_attn_hh_b"],
        "gnw": a["L1_attn_gn_weight"], "gnb": a["L1_attn_gn_bias"],
    }
    host.update(tables())
    nc = _bacc.Bacc("TRN2", target_bir_lowering=False, num_devices=1)
    arrays, d = {}, {}
    for name, v in host.items():
        arrays[f"in_{name}"] = _np.ascontiguousarray(v)
        d[name] = nc.dram_tensor(f"in_{name}", v.shape, _mybir.dt.from_np(v.dtype), kind="ExternalInput").ap()
    out = nc.dram_tensor("out_x", (B, T, E), F32, kind="ExternalOutput").ap()
    build(nc, d, out)
    r = _run(nc, [arrays], core_ids=[0])
    return r.results[0]["out_x"]
```

```python
from contextlib import ExitStack

import concourse.bass as bass
import numpy as np
from concourse import mybir

F32 = mybir.dt.float32
BF16 = mybir.dt.bfloat16
U32 = mybir.dt.uint32
I32 = mybir.dt.int32
ALU = mybir.AluOpType
ACT = mybir.ActivationFunctionType
AX_X = mybir.AxisListType.X

P = 128
B, T, E = 8, 512, 256
TILES = T // P
KT = E // P
NE, TOPK = 16, 4
I = 176
SH = 704 // I
UNITS = NE + SH
SLOT_TILES = B * T * TOPK // P + NE
HK = I // 2
H, D = 16, 16
STACK = 6 * D
ROWS = STACK + 3
LE, LK, R = 8, 2, 16
LR = LE * R
LCOLS = E + LR + LE
RD = 64
G, GC = 32, 8
EPS = 1e-5
NEG = -1e30
WORK = 10000


class Chain:

    def __init__(self, eng, sem, per, need):
        self.eng, self.sem, self.per, self.need = eng, sem, per, need

    def start(self, it):
        self.it, self.n = it, 0

    def step(self, ins, stand=None):
        self.n += 1
        ins.then_inc(self.sem, 1)
        (stand or self.need)(self.eng, self.sem, self.it * self.per + self.n)

    def end(self):
        assert self.n == self.per, self.n


def build(nc, d, XS, YS, out):
    with ExitStack() as ctx:
        def sb(name, shape, dt=F32):
            return ctx.enter_context(nc.sbuf_tensor(name, shape, dt))[(slice(None),) * len(shape)]

        def sem(name):
            return ctx.enter_context(nc.semaphore(name))

        X = sb("X", [P, B * TILES, E])
        w13 = sb("w13", [P, KT, UNITS * 2 * I])
        w2 = sb("w2", [P, 2, UNITS * E])
        gates_w = sb("gates_w", [P, KT, NE + 1])
        wqkv = sb("wqkv", [P, KT, 3 * E])
        wo = sb("wo", [P, KT, E])
        wl = sb("wl", [P, KT, LCOLS])
        wlb = sb("wlb", [LR, E])
        wmix = sb("wmix", [P, KT, E])
        bqkv = sb("bqkv", [P, 3 * E])
        bo = sb("bo", [P, E])
        bl = sb("bl", [P, E])
        blh = sb("blh", [P, E])
        bgate = sb("bgate", [P, LE])
        bmix = sb("bmix", [P, E])
        gnw = sb("gnw", [P, KT])
        gnb = sb("gnb", [P, KT])
        ident = sb("ident", [P, P])
        identb = sb("identb", [P, P], BF16)
        mask_qk = sb("mask_qk", [P, P], BF16)
        mask_kq = sb("mask_kq", [P, P], BF16)
        iota = sb("iota", [P, SLOT_TILES])
        tri = sb("tri", [P, P], BF16)
        ones = sb("ones", [P, P], BF16)
        zeros = sb("zeros", [P, E])
        rope_a = sb("rope_a", [P, TILES, 2, D])
        rope_m = sb("rope_m", [P, TILES, 2, RD])
        epsc = sb("epsc", [P, TILES])
        mhalf = sb("mhalf", [P, TILES])
        stats = sb("stats", [P, TILES, 6])
        mv = sb("mv", [P, B * TILES, 2])
        mvb = sb("mvb", [P, TILES, 2])
        veps = sb("veps", [P, TILES])
        rstd = sb("rstd", [P, B * TILES])
        xn = sb("xn", [P, TILES, E])
        xnT = sb("xnT", [P, KT, T])
        work = sb("work", [P, WORK])

        used = [0]

        def part(shape, dt=F32):
            n = int(np.prod(shape[1:]))
            words = n if dt in (F32, U32, I32) else (n + 1) // 2
            ap = work[0:shape[0], used[0]:used[0] + words]
            used[0] += words
            assert used[0] <= WORK, used[0]
            if dt != F32:
                ap = ap.bitcast(dt)
            if len(shape) == 3:
                ap = ap.rearrange("p (a b) -> p a b", b=shape[2])
            if len(shape) == 4:
                ap = ap.rearrange("p (a b c) -> p a b c", b=shape[2], c=shape[3])
            return ap

        bank = [ctx.enter_context(nc.psum_tensor(f"bank{i}", [P, 512], F32))[:, :] for i in range(8)]

        s_w = {n: sem(f"s_{n}") for n in ("x", "const", "late", "ffn", "slots")}
        s_init = sem("s_init")
        s_out = sem("s_out")
        s_pool = sem("s_pool")
        s_go = sem("s_go")
        s_zero = sem("s_zero")
        s_again = sem("s_again")
        s_stood = sem("s_stood")
        PHASES = ("f0", "at", "f1", "l0", "mx", "l1")
        done = {p: sem(f"done_{p}") for p in PHASES}

        counted = []

        def sems(ph, names):
            made = {n: sem(f"{ph}_{n}") for n in names.split()}
            counted.extend(made.values())
            return made

        PREP = "stats aggr mv veps rstd xn xt xnT prev"
        mo = sems("mo", PREP + " logits lg chain ex member count ichain ready sxn sfree gidx comb cchain "
                  "u_xn u_xt u_xnT u_up u_act u_hid u_tr u_hT u_down u_acc "
                  "ld0 ld1 ld2 ld3 r_tx r_xT r_up r_act r_hid r_tr r_hT r_down r_ys st0 st1 st2 st3")
        dmas = [{n: sem(f"f{layer}_{n}") for n in ("scat", "gat0", "gat1")} for layer in range(2)]
        at = sems("at", PREP + " qk v qkb vb rot_c tile split tr qkT s mx rest m3 m3T m3s maxrow st pexp pv ot bt recip norm onT oT wo xbo x")
        lo = sems("lo", PREP + " biased read up lg chain ex gated tr gT lora")
        mi = sems("mx", PREP + " biased pre chain th ve sd gn tr x")

        block = ctx.enter_context(nc.Block())

        def need(eng, sem, n):
            if not isinstance(n, int) or n > 0:
                eng.wait_ge(sem, n + 1)

        def stand(eng, sem, n):
            need(eng, sem, n)
            eng.sem_inc(s_stood, 1)

        def each_batch(eng):
            return eng.Fori(0, B)

        def each_batch_ahead(eng, first, step):
            first()
            with eng.Fori(0, B - 1) as b:
                step(b, True)
            step(B - 1, False)

        def ln_stats(v, s, b):
            for j in range(TILES):
                v.bn_stats(stats[:, j, :], X[:, b * TILES + j, :]).then_inc(s["stats"], 1)
            stand(v, s["stats"], (b + 1) * TILES)
            for j in range(TILES):
                v.bn_aggr(mvb[:, j, :], stats[:, j, :]).then_inc(s["aggr"], 1)
            need(v, s["aggr"], (b + 1) * TILES)
            v.tensor_copy(mv[:, bass.ds(b * TILES, TILES), :], mvb[:, :, :]).then_inc(s["mv"], 1)

        def ln_normal(v, s, b):
            need(v, s["rstd"], b + 1)
            need(v, s["xt"], b)
            for j in range(TILES):
                t = b * TILES + j
                v.tensor_scalar(xn[:, j, :], X[:, t, :], mv[:, t, 0:1], rstd[:, bass.ds(t, 1)],
                                ALU.subtract, ALU.mult).then_inc(s["xn"], 1)

        def ln_vector(v, s, b):
            ln_stats(v, s, b)
            ln_normal(v, s, b)

        def ln_gpsimd(g, s, b):
            need(g, s["mv"], b + 1)
            g.tensor_tensor(veps[:, :], mv[:, bass.ds(b * TILES, TILES), 1], epsc[:, 0:TILES], ALU.add).then_inc(s["veps"], 1)
            need(g, s["veps"], b + 1)
            g.tensor_tensor(rstd[:, bass.ds(b * TILES, TILES)], veps[:, :], mhalf[:, 0:TILES], ALU.pow).then_inc(s["rstd"], 1)

        def ln_tensor(t, s, b):
            need(t, s["xn"], (b + 1) * TILES)
            need(t, s["xnT"], b * KT)
            for k in range(KT):
                for j in range(TILES):
                    m = t.transpose(bank[k][:, j * P:(j + 1) * P], xn[:, j, k * P:(k + 1) * P], ident[:, :])
            m.then_inc(s["xt"], 1)

        def ln_scalar(a, s, b, natural=False):
            need(a, s["xt"], b + 1)
            need(a, s["prev"], b)
            for k in range(KT):
                if natural:
                    dst = xnT[:, k, :].rearrange("p (h t o) -> p h o t", h=2, o=2)
                    src = bank[k][:, :].rearrange("p (h o t) -> p h o t", h=2, o=2)
                else:
                    dst, src = xnT[:, k, :], bank[k][:, :]
                a.activation(dst, src, ACT.Copy).then_inc(s["xnT"], 1)

        used[0] = 0
        lg = part([P, TILES, NE + 1])
        lgs = part([P, TILES, NE])
        top8 = part([P, TILES, 8])
        idx8 = part([P, TILES, 8], U32)
        idxf = part([P, TILES, 8])
        ex = part([P, TILES, NE + 1])
        exk = part([P, TILES, TOPK])
        den = part([P, TILES])
        rden = part([P, TILES])
        onehot = part([P, TILES, TOPK, NE])
        chosen = part([P, B * TILES * TOPK, NE], BF16)
        chosen4 = chosen.rearrange("p (t k) e -> p t k e", k=TOPK)
        member = part([P, B * TILES, NE], BF16)
        wk = part([P, B * TILES, TOPK])
        wsh = part([P, B * TILES])
        slot = part([P, B * TILES * TOPK], U32)
        slots16 = part([P, 2, TILES * TOPK], U32)
        tile_e = part([P, SLOT_TILES], I32)
        ntile = part([P, 2, NE])
        ntile_i = part([P, NE], I32)
        sg = part([P, 2, I])
        hid = part([P, 2, I])
        hT = part([HK, 2, 2 * P])
        xT = part([P, 2, 2 * P])
        region_a = used[0]
        big = part([P, SLOT_TILES * NE])
        region_a_end = used[0]
        used[0] = region_a
        xs = part([P, 4, E])
        ys = part([P, 4, E])
        used[0] = region_a_end
        region_b = used[0]
        tot = part([P, 2, B * TILES, NE])
        pos = part([P, B * TILES, NE])
        used[0] = region_b
        xsc = part([P, 2, TILES, E])
        used[0] = region_b
        got = part([P, 2, TOPK, E])
        psL = bank[2][:, 0:TILES * 32].rearrange("p (j c) -> p j c", c=32)[:, :, 0:NE + 1]

        def router_tensor(t, s):
            def step(b, ahead):
                need(t, s["xnT"], (b + 1) * KT)
                need(t, s["lg"], b)
                for j in range(TILES):
                    for k in range(KT):
                        m = t.matmul(bank[2][:, j * 32:j * 32 + NE + 1], xnT[:, k, j * P:(j + 1) * P],
                                     gates_w[:, k, :], start=(k == 0), stop=(k == KT - 1))
                m.then_inc(s["prev"], 1)
                if ahead:
                    ln_tensor(t, s, b + 1)

            each_batch_ahead(t, lambda: ln_tensor(t, s, 0), step)
            need(t, s["member"], 1)
            members = member.rearrange("p t e -> p (t e)")
            t.matmul(bank[3][:, :], tri[:, :], members, start=True, stop=True)
            t.matmul(bank[4][:, :], ones[:, :], members, start=True, stop=True).then_inc(s["count"], 1)

        def router_scalar(a, s):
            def step(b, ahead):
                if ahead:
                    ln_scalar(a, s, b + 1)
                need(a, s["logits"], b + 1)
                a.activation(ex[:, :, 0:NE], lgs[:, :, :], ACT.Exp)
                a.activation(exk[:, :, :], idxf[:, :, 0:TOPK], ACT.Exp)
                a.activation(ex[:, :, NE:NE + 1], lg[:, :, NE:NE + 1], ACT.Exp, scale=-1.0).then_inc(s["ex"], 1)

            each_batch_ahead(a, lambda: ln_scalar(a, s, 0), step)

        def router_gpsimd(g, s):
            with each_batch(g) as b:
                ln_gpsimd(g, s, b)

        def router_vector(v, s):
            ch = Chain(v, s["chain"], 10, need)
            def step(b, ahead):
                ch.start(b)
                if ahead:
                    ln_stats(v, s, b + 1)
                need(v, s["prev"], b + 1)
                v.tensor_copy(lg[:, :, :], psL).then_inc(s["lg"], 1)
                if ahead:
                    ln_normal(v, s, b + 1)
                stand(v, s["lg"], b + 1)
                for j in range(TILES):
                    ins = v.max(top8[:, j, :], lg[:, j, 0:NE])
                ch.step(ins, stand)
                for j in range(TILES):
                    ins = v.max_index(idx8[:, j, :], top8[:, j, :], lg[:, j, 0:NE])
                ch.step(ins)
                ch.step(v.tensor_copy(idxf[:, :, :], idx8[:, :, :]))
                ch.step(v.tensor_tensor(
                    chosen4[:, bass.ds(b * TILES, TILES), :, :],
                    idxf[:, :, 0:TOPK].unsqueeze(3).to_broadcast([P, TILES, TOPK, NE]),
                    iota[:, 0:NE].unsqueeze(1).unsqueeze(1).to_broadcast([P, TILES, TOPK, NE]), ALU.is_equal))
                v.tensor_reduce(member[:, bass.ds(b * TILES, TILES), :],
                                chosen4[:, bass.ds(b * TILES, TILES), :, :].rearrange("p j k e -> p j e k"), AX_X, ALU.max)
                v.tensor_tensor(lgs[:, :, :], lg[:, :, 0:NE], top8[:, :, 0:1].to_broadcast([P, TILES, NE]),
                                ALU.subtract)
                v.tensor_tensor(idxf[:, :, 0:TOPK], top8[:, :, 0:TOPK], top8[:, :, 0:1].to_broadcast([P, TILES, TOPK]),
                                ALU.subtract).then_inc(s["logits"], 1)
                need(v, s["ex"], b + 1)
                ch.step(v.tensor_reduce(den[:, :], ex[:, :, 0:NE], AX_X, ALU.add))
                ch.step(v.reciprocal(rden[:, :], den[:, :]))
                ch.step(v.tensor_scalar(rden[:, :], rden[:, :], 0.5, None, ALU.mult))
                v.tensor_tensor(wk[:, bass.ds(b * TILES, TILES), :], exk[:, :, :],
                                rden[:, :].unsqueeze(2).to_broadcast([P, TILES, TOPK]), ALU.mult)
                ch.step(v.tensor_scalar(den[:, :], ex[:, :, NE], 2.0, 2.0, ALU.mult, ALU.add))
                ch.step(v.reciprocal(rden[:, :], den[:, :]))
                ch.step(v.tensor_copy(wsh[:, bass.ds(b * TILES, TILES)], rden[:, :]))
                ch.end()

            each_batch_ahead(v, lambda: ln_vector(v, s, 0), step)
            v.tensor_copy(den[:, :], rden[:, :]).then_inc(s["member"], 1)
            c = Chain(v, s["ichain"], 24, need)
            c.start(0)
            need(v, s["count"], 1)
            c.step(v.tensor_copy(tot[:, 0].rearrange("p t e -> p (t e)"), bank[4][:, :]))
            src, n = 0, 1
            while n < B * TILES:
                v.tensor_copy(tot[:, 1 - src, 0:n, :], tot[:, src, 0:n, :])
                c.step(v.tensor_tensor(tot[:, 1 - src, n:, :], tot[:, src, n:, :], tot[:, src, 0:B * TILES - n, :], ALU.add))
                src, n = 1 - src, 2 * n
            flat = tot[:, 1 - src].rearrange("p t e -> p (t e)")
            c.step(v.tensor_tensor(flat, tot[:, src].rearrange("p t e -> p (t e)"), bank[4][:, :], ALU.subtract))
            c.step(v.tensor_tensor(pos.rearrange("p t e -> p (t e)"), flat, bank[3][:, :], ALU.add))
            c.step(v.tensor_scalar(ntile_i[:, :], tot[:, src, B * TILES - 1, :], 1.0 / P,
                                   (P - 1.0) / P - 0.5 + 0.5 / P, ALU.mult, ALU.add))
            c.step(v.tensor_copy(ntile[:, 0, :], ntile_i[:, :]))
            e_src, n = 0, 1
            while n < NE:
                v.tensor_copy(ntile[:, 1 - e_src, 0:n], ntile[:, e_src, 0:n])
                c.step(v.tensor_tensor(ntile[:, 1 - e_src, n:], ntile[:, e_src, n:], ntile[:, e_src, 0:NE - n], ALU.add))
                e_src, n = 1 - e_src, 2 * n
            ends = ntile[:, e_src, :]
            starts = ntile[:, 1 - e_src, :]
            c.step(v.tensor_copy(starts, ntile_i[:, :]))
            c.step(v.tensor_tensor(starts, ends, starts, ALU.subtract))
            c.step(v.tensor_scalar(starts, starts, float(P), None, ALU.mult))
            c.step(v.tensor_tensor(pos[:, :, :], pos[:, :, :], starts.unsqueeze(1).to_broadcast([P, B * TILES, NE]), ALU.add))
            picked = big[:, 0:B * TILES * TOPK * NE].rearrange("p (t k e) -> p t k e", k=TOPK, e=NE)
            c.step(v.tensor_tensor(picked, chosen4[:, :, :, :], pos[:, :, :].unsqueeze(2).to_broadcast([P, B * TILES, TOPK, NE]),
                                   ALU.mult))
            slotf = tot[:, 0].rearrange("p t e -> p (t e)")[:, 0:B * TILES * TOPK]
            c.step(v.tensor_reduce(slotf, big[:, 0:B * TILES * TOPK * NE].rearrange("p (a e) -> p a e", e=NE), AX_X, ALU.add))
            c.step(v.tensor_copy(slot[:, :], slotf))
            table = big[0:1, :].rearrange("p (i e) -> p i e", e=NE)
            wide = [1, SLOT_TILES, NE]
            c.step(v.tensor_tensor(table, iota[0:1, :].unsqueeze(2).to_broadcast(wide), ends[0:1].unsqueeze(1).to_broadcast(wide),
                                   ALU.is_ge))
            tef = pos.rearrange("p t e -> p (t e)")[0:1, 0:SLOT_TILES]
            c.step(v.tensor_reduce(tef, table, AX_X, ALU.add))
            c.step(v.tensor_scalar(tile_e[0:1, :], tef, float(NE - 1), None, ALU.min))
            c.end()
            v.tensor_copy(den[:, :], rden[:, :]).then_inc(s["ready"], 1)

        AHEAD = 2
        NU = SH * TILES
        HALF = B // 2

        def shared_tensor(t, s, b):
            need(t, s["u_xn"], (b + 1) * TILES)
            need(t, s["u_xnT"], b * KT)
            for k in range(KT):
                for j in range(TILES):
                    m = t.transpose(bank[k][:, j * P:(j + 1) * P], xn[:, j, k * P:(k + 1) * P], ident[:, :])
            m.then_inc(s["u_xt"], 1)
            need(t, s["u_xnT"], (b + 1) * KT)
            for q in range(NU + 2):
                if q < NU:
                    e, j = NE + q // TILES, q % TILES
                    need(t, s["u_hid"], b * NU + q + 1)
                    for k in range(KT):
                        m = t.matmul(bank[2 + q % 2][:, 0:2 * I], xnT[:, k, j * P:(j + 1) * P],
                                     w13[:, k, e * 2 * I:(e + 1) * 2 * I], start=(k == 0), stop=(k == KT - 1))
                    m.then_inc(s["u_up"], 1)
                if 1 <= q <= NU:
                    i = q - 1
                    need(t, s["u_hid"], b * NU + i + 1 + AHEAD)
                    need(t, s["u_hT"], b * NU + i + 1)
                    for c in range(2):
                        m = t.transpose(bank[4 + i % 2][0:HK, c * P:(c + 1) * P], hid[:, i % 2, c * HK:(c + 1) * HK], ident[:, :])
                    m.then_inc(s["u_tr"], 1)
                if q >= 2:
                    i = q - 2
                    e = NE + i // TILES
                    need(t, s["u_hT"], b * NU + i + 1 + AHEAD)
                    need(t, s["u_acc"], b * NU + i + 1)
                    for c in range(2):
                        m = t.matmul(bank[6 + i % 2][:, 0:E], hT[:, i % 2, c * P:(c + 1) * P], w2[0:HK, c, e * E:(e + 1) * E],
                                     start=(c == 0), stop=(c == 1))
                    m.then_inc(s["u_down"], 1)

        def shared_scalar(a, s, b):
            need(a, s["u_xt"], b + 1)
            need(a, s["u_up"], b * NU)
            for k in range(KT):
                a.activation(xnT[:, k, :], bank[k][:, :], ACT.Copy).then_inc(s["u_xnT"], 1)
            for q in range(NU + 1):
                if q < NU:
                    need(a, s["u_up"], b * NU + q + 1)
                    need(a, s["u_hid"], b * NU + q + 1)
                    a.activation(sg[:, q % 2, :], bank[2 + q % 2][:, 0:I], ACT.Silu).then_inc(s["u_act"], 1)
                if q >= 1:
                    i = q - 1
                    need(a, s["u_tr"], b * NU + i + 1 + AHEAD)
                    need(a, s["u_down"], b * NU + i + 1)
                    a.activation(hT[:, i % 2, :], bank[4 + i % 2][0:HK, 0:2 * P], ACT.Copy).then_inc(s["u_hT"], 1)

        def shared_vector(v, s, b, between):
            need(v, s["u_xt"], b)
            for j in range(TILES):
                t = b * TILES + j
                v.tensor_scalar(xn[:, j, :], X[:, t, :], mv[:, t, 0:1], rstd[:, bass.ds(t, 1)],
                                ALU.subtract, ALU.mult).then_inc(s["u_xn"], 1)
            for q in range(NU + 2):
                if q < NU:
                    need(v, s["u_act"], b * NU + q + 1)
                    need(v, s["u_tr"], b * NU + q + 1)
                    v.scalar_tensor_tensor(out=hid[:, q % 2, :], in0=sg[:, q % 2, :], scalar=wsh[:, bass.ds(b * TILES + q % TILES, 1)],
                                           in1=bank[2 + q % 2][:, I:2 * I], op0=ALU.mult, op1=ALU.mult).then_inc(s["u_hid"], 1)
                if q >= 2:
                    i = q - 2
                    t = b * TILES + i % TILES
                    need(v, s["u_down"], b * NU + i + 1 + AHEAD)
                    v.tensor_tensor(X[:, t, :], X[:, t, :], bank[6 + i % 2][:, 0:E], ALU.add).then_inc(s["u_acc"], 1)
                    between(i)

        def scatter_vector(v, s, b, h):
            need(v, s["sfree"], b + 1)
            v.tensor_copy(slots16[:, h, :], slot[:, bass.ds(b * TILES * TOPK, TILES * TOPK)])
            for j in range(TILES):
                t = b * TILES + j
                ins = v.tensor_scalar(xsc[:, h, j, :], X[:, t, :], mv[:, t, 0:1], rstd[:, bass.ds(t, 1)], ALU.subtract, ALU.mult)
            ins.then_inc(s["sxn"], 1)

        def scatter_gpsimd(g, s, dma, b, h):
            need(g, s["sxn"], b + 1)
            g.sem_inc(s_stood, 1)
            for j in range(TILES):
                for k in range(TOPK):
                    c = j * TOPK + k
                    g.indirect_dma_start(XS[:, :], bass.IndirectOffsetOnAxis(slots16[:, h, c:c + 1], 0),
                                         xsc[:, h, j, :], None).then_inc(dma["scat"], 16)
            g.wait_ge(dma["scat"], (b + 1) * TILES * TOPK * 16)
            g.sem_inc(s["sfree"], 1)

        def gather_gpsimd(g, s, dma, tile, q):
            need(g, s["comb"], tile + 1)
            g.sem_inc(s_stood, 1)
            for k in range(TOPK):
                c = (q % (2 * TILES)) * TOPK + k
                idx = slots16.rearrange("p a c -> p (a c)")[:, c:c + 1]
                g.indirect_dma_start(got[:, q % 2, k, :], None, YS[:, :], bass.IndirectOffsetOnAxis(idx, 0)).then_inc(dma[f"gat{q % 2}"], 16)

        def combine_vector(v, s, dma, ch, i, q):
            tile = i * 2 * TILES + q
            need(v, s["u_acc"], (i + HALF) * NU + 2 * q + 2 + AHEAD)
            v.wait_ge(dma[f"gat{q % 2}"], (i * TILES + q // 2 + 1) * TOPK * 16)
            for k in range(TOPK):
                ins = v.scalar_tensor_tensor(out=X[:, tile, :], in0=got[:, q % 2, k, :], scalar=wk[:, tile, k:k + 1],
                                             in1=X[:, tile, :], op0=ALU.mult, op1=ALU.add)
                if k < TOPK - 1:
                    ch.step(ins)
            ins.then_inc(s["comb"], 1)
            need(v, s["comb"], tile + 1 + AHEAD)

        UNROLL = 8
        RING = 4

        def routed(eng, step):
            for r in range(UNROLL):
                step(0, r, lambda lag, r=r: 0 <= r - lag)
            with eng.Fori(1, SLOT_TILES // UNROLL - 1) as n:
                for r in range(UNROLL):
                    step(n, r, lambda lag: True)
            for r in range(UNROLL + 2):
                n = SLOT_TILES // UNROLL - 1
                step(n, r, lambda lag, r=r: r - lag < UNROLL)

        def expert_of(t, i):
            return t.value_load(tile_e[0:1, bass.ds(i, 1)], min_val=0, max_val=NE - 1)

        def routed_tensor(t, s):
            def turn(n, r):
                i = n * UNROLL + r
                need(t, s[f"ld{r % RING}"], 16 * (n * (UNROLL // RING) + r // RING + 1))
                need(t, s["r_xT"], i + 1)
                for k in range(KT):
                    m = t.transpose(bank[r % 2][:, k * P:(k + 1) * P], xs[:, r % RING, k * P:(k + 1) * P], ident[:, :])
                m.then_inc(s["r_tx"], 1)

            expert = {}

            def step(n, r, has):
                i = n * UNROLL + r
                if r == 0:
                    for l in (-2, -1, 0):
                        if has(-l):
                            expert[l] = expert_of(t, i + l)
                if has(-1):
                    turn(n, r + 1)
                if has(0):
                    need(t, s["r_xT"], i + 1 + AHEAD)
                    need(t, s["r_hid"], i + 1)
                    for k in range(KT):
                        m = t.matmul(bank[2 + r % 2][:, 0:2 * I], xT[:, r % 2, k * P:(k + 1) * P],
                                     w13[:, k, bass.ds(expert[r] * (2 * I), 2 * I)], start=(k == 0), stop=(k == KT - 1))
                    m.then_inc(s["r_up"], 1)
                    if r + 1 < UNROLL:
                        expert[r + 1] = expert_of(t, i + 1)
                if has(1):
                    h = (r - 1) % 2
                    need(t, s["r_hid"], i + AHEAD)
                    need(t, s["r_hT"], i)
                    for c in range(2):
                        m = t.transpose(bank[4 + h][0:HK, c * P:(c + 1) * P], hid[:, h, c * HK:(c + 1) * HK], ident[:, :])
                    m.then_inc(s["r_tr"], 1)
                if has(2):
                    h = r % 2
                    need(t, s["r_hT"], i - 1 + AHEAD)
                    need(t, s["r_ys"], i - 1)
                    for c in range(2):
                        m = t.matmul(bank[6 + h][:, 0:E], hT[:, h, c * P:(c + 1) * P],
                                     w2[0:HK, c, bass.ds(expert[r - 2] * E, E)], start=(c == 0), stop=(c == 1))
                    m.then_inc(s["r_down"], 1)

            need(t, s["u_acc"], HALF * NU + AHEAD)
            turn(0, 0)
            routed(t, step)

        def routed_scalar(a, s):
            def copy_x(n, r):
                i = n * UNROLL + r
                need(a, s["r_tx"], i + 1 + RING)
                need(a, s["r_up"], i + 1)
                a.activation(xT[:, r % 2, :], bank[r % 2][:, 0:2 * P], ACT.Copy).then_inc(s["r_xT"], 1)

            def step(n, r, has):
                i = n * UNROLL + r
                if has(-1):
                    copy_x(n, r + 1)
                if has(0):
                    need(a, s["r_up"], i + 1 + AHEAD)
                    need(a, s["r_hid"], i + 1)
                    a.activation(sg[:, r % 2, :], bank[2 + r % 2][:, 0:I], ACT.Silu).then_inc(s["r_act"], 1)
                if has(1):
                    h = (r - 1) % 2
                    need(a, s["r_tr"], i + AHEAD)
                    need(a, s["r_down"], i)
                    a.activation(hT[:, h, :], bank[4 + h][0:HK, 0:2 * P], ACT.Copy).then_inc(s["r_hT"], 1)

            copy_x(0, 0)
            routed(a, step)

        def routed_vector(v, s):
            def step(n, r, has):
                i = n * UNROLL + r
                if has(0):
                    need(v, s["r_act"], i + 1)
                    need(v, s["r_tr"], i + 1)
                    v.tensor_tensor(hid[:, r % 2, :], sg[:, r % 2, :], bank[2 + r % 2][:, I:2 * I], ALU.mult).then_inc(s["r_hid"], 1)
                if has(2):
                    need(v, s["r_down"], i - 1 + AHEAD)
                    need(v, s[f"st{(r - 2) % RING}"], 16 * (n * (UNROLL // RING) + (r - 2) // RING))
                    v.tensor_copy(ys[:, (r - 2) % RING, :], bank[6 + r % 2][:, 0:E]).then_inc(s["r_ys"], 1)

            routed(v, step)

        def routed_sync(sp, s, dma):
            def load(n, r):
                i = n * UNROLL + r
                need(sp, s["r_tx"], i + 1)
                sp.dma_start(xs[:, r % RING, :], XS[bass.ds(i * P, P), :]).then_inc(s[f"ld{r % RING}"], 16)

            def step(n, r, has):
                i = n * UNROLL + r
                if has(-3):
                    load(n, r + 3)
                if has(2):
                    need(sp, s["r_ys"], i - 1 + AHEAD)
                    sp.dma_start(YS[bass.ds((i - 2) * P, P), :], ys[:, (r - 2) % RING, :]).then_inc(s[f"st{(r - 2) % RING}"], 16)

            sp.wait_ge(dma["scat"], 16 * B * TILES * TOPK)
            load(0, 0)
            load(0, 1)
            load(0, 2)
            routed(sp, step)

        def moe_tensor(t, s, loaded):
            router_tensor(t, s)
            t.wait_ge(s_w["ffn"], loaded)
            need(t, s["ready"], 1)
            with t.Fori(0, HALF) as i:
                shared_tensor(t, s, i)
            routed_tensor(t, s)
            need(t, s["r_ys"], SLOT_TILES + AHEAD)
            with t.Fori(0, HALF) as i:
                shared_tensor(t, s, i + HALF)

        def moe_scalar(a, s):
            router_scalar(a, s)
            with a.Fori(0, HALF) as i:
                shared_scalar(a, s, i)
            routed_scalar(a, s)
            with a.Fori(0, HALF) as i:
                shared_scalar(a, s, i + HALF)

        def moe_vector(v, s, dma):
            for n in ("u_hid", "u_acc", "u_tr", "u_down", "u_hT", "r_hid", "r_ys", "r_tr", "r_down", "r_hT", "r_xT", "r_up",
                      "comb", "sfree"):
                v.sem_inc(s[n], AHEAD)
            v.sem_inc(s["r_tx"], RING)
            router_vector(v, s)
            with v.Fori(0, HALF) as i:
                scatter_vector(v, s, 2 * i, 0)
                shared_vector(v, s, i, lambda q: scatter_vector(v, s, 2 * i + 1, 1) if q == NU // 2 else None)
            routed_vector(v, s)
            ch = Chain(v, s["cchain"], 2 * TILES * (TOPK - 1), need)
            with v.Fori(0, HALF) as i:
                ch.start(i)
                v.tensor_copy(slots16.rearrange("p a c -> p (a c)"),
                              slot[:, bass.ds(i * 2 * TILES * TOPK, 2 * TILES * TOPK)]).then_inc(s["gidx"], 1)
                shared_vector(v, s, i + HALF,
                              lambda q: combine_vector(v, s, dma, ch, i, q // 2) if q % 2 else None)
                ch.end()

        def moe_gpsimd(g, s, dma):
            router_gpsimd(g, s)
            g.wait_ge(s_w["slots"], 16)
            with g.Fori(0, HALF) as i:
                for h in range(2):
                    scatter_gpsimd(g, s, dma, 2 * i + h, h)
            for r in range(RING):
                need(g, s[f"st{r}"], 16 * SLOT_TILES // RING)
            with g.Fori(0, HALF) as i:
                need(g, s["gidx"], i + 1)
                for q in range(2 * TILES):
                    gather_gpsimd(g, s, dma, i * 2 * TILES + q, q)

        used[0] = 0
        SL = 4
        SH4 = H // SL
        NST = SH4 * TILES
        VW = 32
        OFF = [0, 512, 896, 1152]
        QT, KTt = ([w[:, i, 0:H * T // 2].bitcast(BF16).rearrange("p (h t) -> p h t", t=T) for w in (w2, w13)] for i in range(2))
        VV = [w13[:, i, H * T // 2:H * T // 2 + TILES * H * VW].rearrange("p (n h d) -> p n h d", h=H, d=VW) for i in range(2)]
        on = w2[:, 0, H * T // 2:H * T // 2 + TILES * E].rearrange("p (n e) -> p n e", e=E)
        oT = w2[:, 1, H * T // 2:H * T // 2 + KT * T].rearrange("p (k t) -> p k t", t=T)
        stk = part([P, 2 * H, STACK], BF16)
        qk = part([P, 2 * H, D])
        rc = part([P, 2 * H, D])
        rs = part([P, 2 * H, D])
        nmx = part([P, TILES, SH4])
        nmx_rest = part([P, TILES, SH4])
        m3 = part([P, TILES, 3, SH4], BF16)
        m3T = part([3 * SH4, T], BF16)
        PT = part([P, SH4, 1280])
        OT = part([P, T])
        ors = part([P, TILES, SH4])

        def psT(i):
            return bank[i][:, :].bitcast(BF16)

        MAX_STEPS = [(0, [0, 1, 2, 3]), (1, [0, 1]), (1, [2, 3])] + [(n, [h]) for n in (2, 3) for h in range(SH4)]
        NMAX = len(MAX_STEPS)
        MAX_AT = {0: (0, 1), 1: (2,), 2: (3, 4), 3: (5,), 4: (6, 7), 5: (8,), 6: (9,), 7: (10,)}
        MAX_AT_LAST = {7: (0, 1), 8: (2, 3), 9: (4, 5), 10: (6, 7), 11: (8, 9), 12: (10,)}

        def each_slot_batch(eng, batch):
            batch(0, 0, lambda i: i >= 0)
            with eng.Fori(0, 2) as i:
                batch(2 * i + 1, 1, lambda i: True)
                batch(2 * i + 2, 0, lambda i: True)
            for b in range(5, B):
                batch(b, b % 2, lambda i, b=b: b + i < B)

        def attn_tensor(t):
            s = at

            def normal(b):
                need(t, s["xn"], (b + 1) * TILES)
                need(t, s["qkT"], b * 16)
                need(t, s["vb"], b * TILES)
                for k in range(KT):
                    for j in range(TILES):
                        m = t.transpose(bank[k][:, j * P:(j + 1) * P], xn[:, j, k * P:(k + 1) * P], ident[:, :])
                m.then_inc(s["xt"], 1)

            def project_qk(b, n):
                if n == 0:
                    need(t, s["xnT"], (b + 1) * KT)
                else:
                    need(t, s["qkT"], b * 16 + 4 * n - 1)
                for k in range(KT):
                    m = t.matmul(bank[0][:, :], xnT[:, k, n * P:(n + 1) * P], wqkv[:, k, 0:2 * E],
                                 start=(k == 0), stop=(k == KT - 1))
                m.then_inc(s["qk"], 1)

            def stacks(b, n, g):
                if g < 2:
                    need(t, s["split"], b * TILES + n + 1)
                    if g == 1:
                        need(t, s["vb"], b * TILES + n)
                else:
                    need(t, s["qkT"], b * 16 + 4 * n + g - 1)
                for h in range(8):
                    m = t.transpose(psT(g % 2)[0:STACK, h * P:(h + 1) * P], stk[:, g * 8 + h, :], identb[:, :])
                m.then_inc(s["tr"], 1)

            def project_v(b, n):
                need(t, s["qkT"], b * 16 + 4 * n + 4)
                for k in range(KT):
                    m = t.matmul(bank[1][:, 0:E], xnT[:, k, n * P:(n + 1) * P], wqkv[:, k, 2 * E:3 * E],
                                 start=(k == 0), stop=(k == KT - 1))
                m.then_inc(s["v"], 1)

            def score(b, g, buf, r):
                n, hs = MAX_STEPS[r]
                w = (n + 1) * P
                c = b * SL + g
                if r == 1:
                    need(t, s["m3s"], c)
                else:
                    need(t, s["mx"], c * NMAX + max(r - 1, 0))
                for c, h in enumerate(hs):
                    h += g * SH4
                    o = c * w
                    t.matmul(bank[2 + r % 2][:, o:o + w], QT[buf][0:STACK, h, n * P:(n + 1) * P], KTt[buf][0:STACK, h, 0:w],
                             start=(c == 0), stop=False, skip_group_check=True)
                    m = t.matmul(bank[2 + r % 2][:, o + n * P:o + w], identb[:, :], mask_qk[:, :],
                                 start=False, stop=True, skip_group_check=True)
                m.then_inc(s["s"], 1)

            def turn_maxima(b, g):
                stand(t, s["m3"], b * SL + g + 1)
                for n in range(TILES):
                    m = t.transpose(psT(3)[0:3 * SH4, n * P:(n + 1) * P], m3[:, n, :, :].rearrange("p c h -> p (c h)"), identb[:, :])
                m.then_inc(s["m3T"], 1)

            def score_t(b, g, buf, i):
                h, n = g * SH4 + i // TILES, i % TILES
                w = T - n * P
                need(t, s["pexp"], (b * SL + g) * NST + i - 1)
                t.matmul(bank[4 + i % 2][:, 0:w], KTt[buf][0:ROWS, h, n * P:(n + 1) * P], QT[buf][0:ROWS, h, n * P:T],
                         start=True, stop=False, skip_group_check=True)
                m = t.matmul(bank[4 + i % 2][:, 0:P], identb[:, :], mask_kq[:, :],
                             start=False, stop=True, skip_group_check=True)
                m.then_inc(s["st"], 1)

            def values(c, g, buf, p, k):
                if k == 0:
                    need(t, s["pexp"], c * NST + (p + 1) * NST // 2)
                    need(t, s["ot"], c)
                for h in (2 * p, 2 * p + 1):
                    m = t.matmul(bank[6][VW * h:VW * (h + 1), k * P:T], VV[buf][:, k, g * SH4 + h, :],
                                 PT[:, h, OFF[k]:OFF[k] + T - k * P], start=(k == 0), stop=(k == TILES - 1),
                                 skip_group_check=True)
                if k == TILES - 1:
                    m.then_inc(s["pv"], 1)

            def turn_back(c, b):
                need(t, s["ot"], c + 1)
                need(t, s["norm"], c)
                if b is not None:
                    need(t, s["x"], b * 2 + 2)
                for n in range(TILES):
                    m = t.transpose(bank[7][:, n * P:(n + 1) * P], OT[:, n * P:(n + 1) * P], ident[:, :])
                m.then_inc(s["bt"], 1)

            def turn_out(b, c):
                need(t, s["norm"], (b + 1) * SL)
                need(t, s["oT"], b * KT + c)
                for n in range(TILES):
                    m = t.transpose(bank[7][:, n * P:(n + 1) * P], on[:, n, c * P:(c + 1) * P], ident[:, :])
                m.then_inc(s["onT"], 1)

            def project_out(b, w):
                need(t, s["oT"], (b + 1) * KT)
                need(t, s["x"], b * 2 + w)
                for o in range(2):
                    for c in range(KT):
                        cols = oT[:, c, :].rearrange("p (h t o) -> p h o t", h=2, o=2)[:, w, o, :]
                        m = t.matmul(bank[7][:, o * E:(o + 1) * E], cols, wo[:, c, :], start=(c == 0), stop=(c == KT - 1),
                                     skip_group_check=True)
                m.then_inc(s["wo"], 1)

            def batch(b, buf, has):
                for g in range(SL):
                    c = b * SL + g
                    nb, ng, nbuf = (b, g + 1, buf) if g < 3 else (b + 1, 0, 1 - buf)
                    prev = g > 0 or has(-1)
                    need(t, s["maxrow"], (c + 1) * 48)
                    for i in range(NST):
                        score_t(b, g, buf, i)
                        if g < 3 or has(1):
                            for r in (MAX_AT if g < 3 else MAX_AT_LAST).get(i, ()):
                                if r == 0 and g == 3:
                                    need(t, s["qkT"], (b + 2) * 16)
                                score(nb, ng, nbuf, r)
                            if i == (9 if g < 3 else 14):
                                turn_maxima(nb, ng)
                        if 1 <= i < 5 and prev:
                            values(c - 1, (g - 1) % SL, buf if g else 1 - buf, 1, i - 1)
                        if 2 <= i < 6 and has(1):
                            stacks(b + 1, g, i - 2)
                        if i == 6 and prev:
                            turn_back(c - 1, b - 1 if g == 1 and has(-1) else None)
                        if i == 8 and g < 3 and has(1):
                            project_qk(b + 1, g + 1)
                        if i == (9 if g < 3 else 7) and has(1):
                            project_v(b + 1, g)
                        if i == 8 and g == 3 and has(2):
                            normal(b + 2)
                        if i == 13 and g == 3 and has(2):
                            project_qk(b + 2, 0)
                        if 9 <= i < 13:
                            values(c, g, buf, 0, i - 9)
                        if g == 0 and has(-1):
                            if i in (9, 11):
                                turn_out(b - 1, (i - 9) // 2)
                            if i in (13, 15):
                                project_out(b - 1, (i - 13) // 2)

            t.wait_ge(s_init, INIT + 1)
            normal(0)
            for n in range(TILES):
                project_qk(0, n)
                for g in range(4):
                    stacks(0, n, g)
                project_v(0, n)
            normal(1)
            project_qk(1, 0)
            for r in range(NMAX):
                score(0, 0, 0, r)
            turn_maxima(0, 0)
            each_slot_batch(t, batch)
            c = B * SL
            for k in range(TILES):
                values(c - 1, SL - 1, 1, 1, k)
            turn_back(c - 1, None)
            for k in range(KT):
                turn_out(B - 1, k)
            for w in range(2):
                project_out(B - 1, w)

        def attn_scalar(a):
            s = at

            def normal(b):
                need(a, s["xt"], b + 1)
                need(a, s["v"], b * TILES)
                for k in range(KT):
                    dst = xnT[:, k, :].rearrange("p (h t o) -> p h o t", h=2, o=2)
                    src = bank[k][:, :].rearrange("p (h o t) -> p h o t", h=2, o=2)
                    for hf in range(2):
                        ins = a.activation(dst[:, hf], src[:, hf], ACT.Copy)
                    ins.then_inc(s["xnT"], 1)

            def stacks(b, n, g, buf):
                need(a, s["tr"], b * 16 + 4 * n + g + 1)
                dst = QT[buf] if g < 2 else KTt[buf]
                a.activation(dst[0:STACK, (g % 2) * 8:(g % 2) * 8 + 8, n * P:(n + 1) * P],
                             psT(g % 2)[0:STACK, :].rearrange("p (h t) -> p h t", h=8), ACT.Copy).then_inc(s["qkT"], 1)

            def maxima(c):
                need(a, s["m3T"], c + 1)
                need(a, s["maxrow"], c * 48)
                a.activation(m3T[:, :], psT(3)[0:3 * SH4, 0:T], ACT.Copy).then_inc(s["m3s"], 1)

            def outputs(c):
                need(a, s["pv"], 2 * c + 2)
                need(a, s["bt"], c)
                a.activation(OT[:, :], bank[6][:, :], ACT.Copy).then_inc(s["ot"], 1)

            def turned(b, c):
                need(a, s["onT"], b * KT + c + 1)
                need(a, s["wo"], b * 2)
                a.activation(oT[:, c, :], bank[7][:, :], ACT.Copy).then_inc(s["oT"], 1)

            def batch(b, buf, has):
                for g in range(SL):
                    c = b * SL + g
                    for i in range(NST):
                        need(a, s["st"], c * NST + i + 1)
                        if i % (NST // 2) == 0:
                            need(a, s["pv"], 2 * (c - 1) + i // (NST // 2) + 1)
                        n = i % TILES
                        w = T - n * P
                        a.activation(PT[:, i // TILES, OFF[n]:OFF[n] + w], bank[4 + i % 2][:, 0:w], ACT.Exp,
                                     scale=float(D) ** -0.5).then_inc(s["pexp"], 1)
                        if i == 5 and (g > 0 or has(-1)):
                            outputs(c - 1)
                        if 3 <= i < 7 and has(1):
                            stacks(b + 1, g, i - 3, 1 - buf)
                        if g == 0 and has(-1) and i in (10, 12):
                            turned(b - 1, (i - 10) // 2)
                        if i == 9 and g == 3 and has(2):
                            normal(b + 2)
                        if i == (10 if g < 3 else 15) and (g < 3 or has(1)):
                            maxima(c + 1)

            normal(0)
            for n in range(TILES):
                for g in range(4):
                    stacks(0, n, g, 0)
            normal(1)
            maxima(0)
            each_slot_batch(a, batch)
            outputs(B * SL - 1)
            for k in range(KT):
                turned(B - 1, k)

        def attn_vector(v):
            s = at
            for i in range(2):
                v.memset(VV[i][:, :, :, D:VW], 1.0)
                v.memset(KTt[i][96:96 + 3, :, :], 1.0)
            v.memset(ors[:, :, :], 1.0).then_inc(s_init, 1)
            v.wait_ge(s_init, INIT + 1)

            def project_qk(b, n):
                i = b * TILES + n
                need(v, s["qk"], i + 1)
                need(v, s["rot_c"], i)
                v.tensor_tensor(qk[:, :, :].rearrange("p h d -> p (h d)"), bank[0][:, :], bqkv[:, 0:2 * E],
                                ALU.add).then_inc(s["qkb"], 1)

            def chained(ins, n):
                ins.then_inc(s["tile"], 1)
                need(v, s["tile"], n)

            def split(b, n):
                i = b * TILES + n
                need(v, s["qkb"], i + 1)
                pairs = qk[:, :, :].rearrange("p h (i o) -> p h i o", o=2)
                turned = rs[:, :, :].rearrange("p h (i o) -> p h i o", o=2)
                sine = rope_a[:, n, 1, :].rearrange("p (i o) -> p i o", o=2)
                for o in range(2):
                    ins = v.tensor_tensor(turned[:, :, :, o], pairs[:, :, :, 1 - o],
                                          sine[:, :, o].unsqueeze(1).to_broadcast([P, 2 * H, D // 2]), ALU.mult)
                chained(ins, i * 5 + 1)
                need(v, s["rot_c"], i + 1)
                chained(v.tensor_tensor(rc[:, :, :], rc[:, :, :], rs[:, :, :], ALU.add), i * 5 + 2)
                need(v, s["tr"], i * 4)
                q, k = slice(0, H), slice(H, 2 * H)

                def blocks(side, first, count, step=1):
                    return stk[:, side, :].rearrange("p h (c d) -> p h c d", d=D)[:, :, first:first + (count - 1) * step + 1:step, :]

                def wide(src, side, count):
                    return src[:, side, :].unsqueeze(2).to_broadcast([P, H, count, D])

                v.tensor_copy(blocks(q, 0, 3), wide(rc, q, 3))
                chained(v.tensor_copy(blocks(k, 2, 3), wide(rc, k, 3)), i * 5 + 3)
                v.tensor_tensor(rs[:, q, :], rc[:, q, :], stk[:, q, 0:D], ALU.subtract)
                chained(v.tensor_tensor(rs[:, k, :], rc[:, k, :], stk[:, k, 2 * D:3 * D], ALU.subtract), i * 5 + 4)
                v.tensor_copy(blocks(q, 4, 2), wide(rs, q, 2))
                chained(v.tensor_copy(blocks(k, 1, 2, 4), wide(rs, k, 2)), i * 5 + 5)
                v.tensor_tensor(stk[:, q, 3 * D:4 * D], rs[:, q, :], stk[:, q, 4 * D:5 * D], ALU.subtract)
                v.tensor_tensor(stk[:, k, 0:D], rs[:, k, :], stk[:, k, D:2 * D], ALU.subtract).then_inc(s["split"], 1)

            def project_v(b, n, buf):
                need(v, s["v"], b * TILES + n + 1)
                v.tensor_tensor(VV[buf][:, n, :, 0:D], bank[1][:, 0:E].rearrange("p (h d) -> p h d", d=D),
                                bqkv[:, 2 * E:3 * E].rearrange("p (h d) -> p h d", d=D), ALU.add).then_inc(s["vb"], 1)

            def maximum(c, r):
                n, hs = MAX_STEPS[r]
                w = (n + 1) * P
                need(v, s["s"], c * NMAX + r + 1)
                v.tensor_reduce(nmx[:, n, hs[0]:hs[0] + len(hs)],
                                bank[2 + r % 2][:, 0:len(hs) * w].rearrange("p (h k) -> p h k", k=w),
                                AX_X, ALU.max, negate=True).then_inc(s["mx"], 1)

            def split_maxima(c):
                need(v, s["mx"], (c + 1) * NMAX)
                need(v, s["m3T"], c)
                v.tensor_copy(m3[:, :, 0, :], nmx[:, :, :]).then_inc(s["rest"], 1)
                need(v, s["rest"], 3 * c + 1)
                v.tensor_tensor(nmx_rest[:, :, :], nmx[:, :, :], m3[:, :, 0, :], ALU.subtract).then_inc(s["rest"], 1)
                need(v, s["rest"], 3 * c + 2)
                v.tensor_copy(m3[:, :, 1, :], nmx_rest[:, :, :]).then_inc(s["rest"], 1)
                need(v, s["rest"], 3 * c + 3)
                v.tensor_tensor(m3[:, :, 2, :], nmx_rest[:, :, :], m3[:, :, 1, :], ALU.subtract).then_inc(s["m3"], 1)

            def norm(c, b, g):
                need(v, s["bt"], c + 1)
                if g == 0:
                    need(v, s["onT"], b * KT)
                ps = bank[7][:, :].rearrange("p (n h d) -> p n h d", h=SH4, d=VW)
                v.reciprocal(ors[:, :, :], ps[:, :, :, D]).then_inc(s["recip"], 1)
                need(v, s["recip"], c + 1)
                v.tensor_tensor(on[:, :, g * SH4 * D:(g + 1) * SH4 * D].rearrange("p n (h d) -> p n h d", d=D), ps[:, :, :, 0:D],
                                ors[:, :, :].unsqueeze(3).to_broadcast([P, TILES, SH4, D]), ALU.mult).then_inc(s["norm"], 1)

            def add(b, w):
                need(v, s["wo"], b * 2 + w + 1)
                need(v, s["xbo"], b + 1)
                x = X[:, bass.ds(b * TILES + 2 * w, 2), :]
                v.tensor_tensor(x, x, bank[7][:, :].rearrange("p (o e) -> p o e", e=E), ALU.add).then_inc(s["x"], 1)

            def batch(b, buf, has):
                for g in range(SL):
                    c = b * SL + g
                    prev = g > 0 or has(-1)
                    if g == 3:
                        if has(2):
                            ln_stats(v, s, b + 2)
                        norm(c - 1, b, g - 1)
                        if has(2):
                            ln_normal(v, s, b + 2)
                    if g < 3 or has(1):
                        for r in range(NMAX):
                            maximum(c + 1, r)
                            if r == 1 and g == 3:
                                project_v(b + 1, g, 1 - buf)
                        split_maxima(c + 1)
                    if g < 3 and prev:
                        norm(c - 1, b - (g == 0), (g - 1) % SL)
                    if has(1 if g < 3 else 2):
                        project_qk(b + (1 if g < 3 else 2), (g + 1) % TILES)
                    if g < 3 and has(1):
                        project_v(b + 1, g, 1 - buf)
                    if has(1 if g < 3 else 2):
                        split(b + (1 if g < 3 else 2), (g + 1) % TILES)
                    if g == 0 and has(-1):
                        add(b - 1, 0)
                        add(b - 1, 1)

            ln_vector(v, s, 0)
            for n in range(TILES):
                project_qk(0, n)
                split(0, n)
                project_v(0, n, 0)
            ln_vector(v, s, 1)
            project_qk(1, 0)
            split(1, 0)
            for r in range(NMAX):
                maximum(0, r)
            split_maxima(0)
            each_slot_batch(v, batch)
            norm(B * SL - 1, B - 1, SL - 1)
            for w in range(2):
                add(B - 1, w)

        def attn_gpsimd(g):
            s = at
            with each_batch(g) as b:
                ln_gpsimd(g, s, b)
                need(g, s["xn"], (b + 1) * TILES)
                x = X[:, bass.ds(b * TILES, TILES), :]
                g.tensor_tensor(x, x, bo[:, :].unsqueeze(1).to_broadcast([P, TILES, E]), ALU.add).then_inc(s["xbo"], 1)
                for n in range(TILES):
                    i = b * TILES + n
                    need(g, s["qkb"], i + 1)
                    need(g, s["split"], i)
                    g.tensor_tensor(rc[:, :, :], qk[:, :, :],
                                    rope_a[:, n, 0, :].unsqueeze(1).to_broadcast([P, 2 * H, D]), ALU.mult).then_inc(s["rot_c"], 1)

        def attn_sync(sp):
            s = at
            with sp.Fori(0, B // 2) as i:
                for buf in range(2):
                    for g in range(SL):
                        need(sp, s["m3s"], (2 * i + buf) * SL + g + 1)
                        for c in range(3):
                            sp.dma_start(QT[buf][STACK + c:STACK + c + 1, g * SH4:(g + 1) * SH4, :],
                                         m3T[c * SH4:(c + 1) * SH4, :]).then_inc(s["maxrow"], 16)

        used[0] = 0
        HT = TILES // 2
        llg = part([P, HT, LE])
        ltop = part([P, HT, 8])
        lidx = part([P, HT, 8], U32)
        lidxf = part([P, HT, 8])
        ldiff = part([P, HT, 1])
        lex = part([P, HT, 1])
        lgw = part([P, HT, LK])
        loh = part([P, HT, LK, LE])
        lgm = part([P, HT, LE])
        gxa = part([P, TILES, LR])
        gT = part([LR, 2, HT * P])

        def each_batch_lagging(eng, first, step):
            first()
            step(0, lambda i: i >= 0)
            with eng.Fori(1, B - 1) as b:
                step(b, lambda i: True)
            step(B - 1, lambda i: i <= 0)

        def lora_tensor(t, s):
            def project(b, h):
                if h == 0:
                    need(t, s["xnT"], (b + 1) * KT)
                for j in range(h * HT, h * HT + HT):
                    need(t, s["read"], b * TILES + j + 1)
                    for k in range(KT):
                        m = t.matmul(bank[2 + j][:, 0:LCOLS], xnT[:, k, j * P:(j + 1) * P], wl[:, k, :],
                                     start=(k == 0), stop=(k == KT - 1))
                    m.then_inc(s["up"], 1)

            def finish(b, h):
                need(t, s["gated"], 2 * b + h + 1)
                need(t, s["gT"], 2 * b + h)
                for j in range(HT):
                    m = t.transpose(bank[6][:, j * P:(j + 1) * P], gxa[:, h * HT + j, :], ident[:, :])
                m.then_inc(s["tr"], 1)
                need(t, s["gT"], 2 * b + h + 1)
                for j in range(HT):
                    m = t.matmul(bank[2 + h * HT + j][:, 0:E], gT[:, h, j * P:(j + 1) * P], wlb[:, :], start=False, stop=True,
                                 skip_group_check=True)
                    m.then_inc(s["lora"], 1)

            def step(b, has):
                project(b, 0)
                if has(-1):
                    finish(b - 1, 1)
                project(b, 1)
                if has(1):
                    ln_tensor(t, s, b + 1)
                finish(b, 0)

            each_batch_lagging(t, lambda: ln_tensor(t, s, 0), step)
            finish(B - 1, 1)

        def lora_scalar(a, s):
            def normal(b):
                need(a, s["xt"], b + 1)
                need(a, s["up"], b * TILES)
                for k in range(KT):
                    a.activation(xnT[:, k, :], bank[k][:, :], ACT.Copy).then_inc(s["xnT"], 1)

            def gates(b, h):
                need(a, s["lg"], 2 * b + h + 1)
                a.activation(lex[:, :, :], ldiff[:, :, :], ACT.Exp).then_inc(s["ex"], 1)

            def turned(b, h):
                need(a, s["tr"], 2 * b + h + 1)
                need(a, s["lora"], (b - 1) * TILES + (h + 1) * HT)
                a.activation(gT[:, h, :], bank[6][:, 0:HT * P], ACT.Copy).then_inc(s["gT"], 1)

            def step(b, has):
                if has(-1):
                    turned(b - 1, 1)
                gates(b, 0)
                gates(b, 1)
                if has(1):
                    normal(b + 1)
                turned(b, 0)

            each_batch_lagging(a, lambda: normal(0), step)
            turned(B - 1, 1)

        def lora_gpsimd(g, s):
            with each_batch(g) as b:
                ln_gpsimd(g, s, b)
                need(g, s["xn"], (b + 1) * TILES)
                x = X[:, bass.ds(b * TILES, TILES), :]
                g.tensor_tensor(x, x, blh[:, :].unsqueeze(1).to_broadcast([P, TILES, E]), ALU.add).then_inc(s["biased"], 1)

        def lora_vector(v, s):
            v.sem_inc(s["read"], TILES)
            ch = Chain(v, s["chain"], 10, need)

            def gates(b, h):
                u = 2 * b + h
                ch.start(u)
                need(v, s["up"], b * TILES + (h + 1) * HT)
                for j in range(HT):
                    ins = v.tensor_tensor(llg[:, j, :], bank[2 + h * HT + j][:, E + LR:LCOLS], bgate[:, :], ALU.add)
                ch.step(ins, stand)
                for j in range(HT):
                    ins = v.max(ltop[:, j, :], llg[:, j, :])
                ch.step(ins)
                v.tensor_tensor(ldiff[:, :, :], ltop[:, :, 1:2], ltop[:, :, 0:1], ALU.subtract).then_inc(s["lg"], 1)
                for j in range(HT):
                    ins = v.max_index(lidx[:, j, :], ltop[:, j, :], llg[:, j, :])
                ch.step(ins)
                ch.step(v.tensor_copy(lidxf[:, :, :], lidx[:, :, :]))
                ch.step(v.tensor_tensor(
                    loh[:, :, :, :], lidxf[:, :, 0:LK].unsqueeze(3).to_broadcast([P, HT, LK, LE]),
                    iota[:, 0:LE].unsqueeze(1).unsqueeze(1).to_broadcast([P, HT, LK, LE]), ALU.is_equal))
                need(v, s["ex"], u + 1)
                ch.step(v.tensor_scalar(ldiff[:, :, :], lex[:, :, :], 1.0, None, ALU.add))
                ch.step(v.reciprocal(lgw[:, :, 0:1], ldiff[:, :, :]))
                ch.step(v.tensor_tensor(lgw[:, :, 1:2], lex[:, :, :], lgw[:, :, 0:1], ALU.mult))
                ch.step(v.tensor_tensor(loh[:, :, :, :], loh[:, :, :, :],
                                        lgw[:, :, :].unsqueeze(3).to_broadcast([P, HT, LK, LE]), ALU.mult))
                ch.step(v.tensor_reduce(lgm[:, :, :], loh[:, :, :, :].rearrange("p j k e -> p j e k"), AX_X, ALU.add))
                ch.end()
                for j in range(HT):
                    ins = v.tensor_tensor(gxa[:, h * HT + j, :].rearrange("p (e r) -> p e r", r=R),
                                          bank[2 + h * HT + j][:, E:E + LR].rearrange("p (e r) -> p e r", r=R),
                                          lgm[:, j, :].unsqueeze(2).to_broadcast([P, LE, R]), ALU.mult)
                ins.then_inc(s["gated"], 1)

            def add(b, h):
                need(v, s["biased"], b + 1)
                for j in range(h * HT, h * HT + HT):
                    t = b * TILES + j
                    need(v, s["lora"], t + 1)
                    v.scalar_tensor_tensor(out=X[:, t, :], in0=bank[2 + j][:, 0:E], scalar=0.5, in1=X[:, t, :],
                                           op0=ALU.mult, op1=ALU.add).then_inc(s["read"], 1)

            def step(b, has):
                if has(1):
                    ln_stats(v, s, b + 1)
                gates(b, 0)
                if has(-1):
                    add(b - 1, 1)
                if has(1):
                    ln_normal(v, s, b + 1)
                gates(b, 1)
                add(b, 0)

            each_batch_lagging(v, lambda: ln_vector(v, s, 0), step)
            add(B - 1, 1)

        used[0] = 0
        mr = part([P, TILES, RD])
        ms = part([P, TILES, RD])
        pre = part([P, TILES, E])
        hh = part([P, TILES, E])
        sq = part([P, TILES, E])
        mu = part([P, TILES * G])
        var = part([P, TILES * G])
        sd = part([P, TILES * G])

        def mix_tensor(t):
            s = mi

            def project(b):
                ln_tensor(t, s, b)
                need(t, s["xnT"], (b + 1) * KT)
                need(t, s["pre"], b)
                for j in range(TILES):
                    for k in range(KT):
                        m = t.matmul(bank[2 + j][:, 0:E], xnT[:, k, j * P:(j + 1) * P], wmix[:, k, :],
                                     start=(k == 0), stop=(k == KT - 1))
                m.then_inc(s["prev"], 1)

            def step(b, ahead):
                if ahead:
                    project(b + 1)
                need(t, s["gn"], b + 1)
                need(t, s["x"], b)
                for c in range(KT):
                    for j in range(TILES):
                        m = t.transpose(bank[6 + c][:, j * P:(j + 1) * P], hh[:, j, c * P:(c + 1) * P], ident[:, :])
                m.then_inc(s["tr"], 1)

            each_batch_ahead(t, lambda: project(0), step)

        def mix_scalar(a):
            s = mi

            def step(b, ahead):
                need(a, s["pre"], b + 1)
                need(a, s["tr"], b)
                a.activation(hh[:, :, :], pre[:, :, :], ACT.Tanh).then_inc(s["th"], 1)
                if ahead:
                    ln_scalar(a, s, b + 1)
                need(a, s["ve"], b + 1)
                a.activation(sd[:, :], var[:, :], ACT.Sqrt).then_inc(s["sd"], 1)

            each_batch_ahead(a, lambda: ln_scalar(a, s, 0), step)

        def mix_gpsimd(g):
            s = mi
            with each_batch(g) as b:
                ln_gpsimd(g, s, b)
                need(g, s["xn"], (b + 1) * TILES)
                x = X[:, bass.ds(b * TILES, TILES), :].rearrange("p (c h) e -> p c (h e)", c=KT)
                g.tensor_tensor(x, x, gnb[:, :].unsqueeze(2).to_broadcast([P, KT, 2 * E]), ALU.add).then_inc(s["biased"], 1)

        def mix_vector(v):
            s = mi
            ch = Chain(v, s["chain"], 12, need)

            def add(b):
                need(v, s["tr"], b + 1)
                need(v, s["biased"], b + 1)
                for c in range(KT):
                    for hf in range(2):
                        x = X[:, b * TILES + 2 * c + hf, :]
                        src = bank[6 + c][:, hf * E:(hf + 1) * E].rearrange("p (o t) -> p t o", o=2)
                        ins = v.scalar_tensor_tensor(out=x.rearrange("p (t o) -> p t o", o=2), in0=src, scalar=gnw[:, c:c + 1],
                                                     in1=x.rearrange("p (t o) -> p t o", o=2), op0=ALU.mult, op1=ALU.add)
                ins.then_inc(s["x"], 1)

            def step(b, ahead):
                ch.start(b)
                if ahead:
                    ln_stats(v, s, b + 1)
                need(v, s["prev"], b + 1)
                for j in range(TILES):
                    ps = bank[2 + j][:, 0:RD]
                    v.tensor_tensor(mr[:, j, :], ps, rope_m[:, j, 0, :], ALU.mult)
                    for o in range(2):
                        ins = v.tensor_tensor(ms[:, j, :].rearrange("p (i o) -> p i o", o=2)[:, :, o],
                                              ps.rearrange("p (i o) -> p i o", o=2)[:, :, 1 - o],
                                              rope_m[:, j, 1, :].rearrange("p (i o) -> p i o", o=2)[:, :, o], ALU.mult)
                ch.step(ins)
                ins = v.tensor_tensor(mr[:, :, :], mr[:, :, :], ms[:, :, :], ALU.add)
                for j in range(TILES):
                    v.scalar_tensor_tensor(out=pre[:, j, RD:E], in0=bank[2 + j][:, RD:E], scalar=0.0,
                                           in1=bmix[:, RD:E], op0=ALU.max, op1=ALU.add)
                ch.step(ins)
                v.scalar_tensor_tensor(out=pre[:, :, 0:RD], in0=mr[:, :, :], scalar=0.0,
                                       in1=bmix[:, 0:RD].unsqueeze(1).to_broadcast([P, TILES, RD]),
                                       op0=ALU.max, op1=ALU.add).then_inc(s["pre"], 1)
                if ahead:
                    ln_normal(v, s, b + 1)
                need(v, s["th"], b + 1)
                groups = hh[:, :, :].rearrange("p j (g c) -> p (j g) c", c=GC)
                squares = sq[:, :, :].rearrange("p j (g c) -> p (j g) c", c=GC)
                wide = [P, TILES * G, GC]
                ch.step(v.tensor_reduce(mu[:, :], groups, AX_X, ALU.add))
                ch.step(v.tensor_scalar(mu[:, :], mu[:, :], 1.0 / GC, None, ALU.mult))
                ch.step(v.tensor_tensor(groups, groups, mu[:, :].unsqueeze(2).to_broadcast(wide), ALU.subtract))
                ch.step(v.tensor_tensor(squares, groups, groups, ALU.mult))
                ch.step(v.tensor_reduce(var[:, :], squares, AX_X, ALU.add))
                v.tensor_scalar(var[:, :], var[:, :], 1.0 / GC, EPS, ALU.mult, ALU.add).then_inc(s["ve"], 1)
                need(v, s["sd"], b + 1)
                ch.step(v.reciprocal(mu[:, :], sd[:, :]))
                ch.step(v.tensor_tensor(sq[:, 0, 0:TILES * G], mu[:, :], mu[:, :], ALU.mult))
                ch.step(v.tensor_tensor(sq[:, 0, 0:TILES * G], sq[:, 0, 0:TILES * G], var[:, :], ALU.mult))
                ch.step(v.tensor_scalar(sq[:, 0, 0:TILES * G], sq[:, 0, 0:TILES * G], -0.5, 1.5, ALU.mult, ALU.add))
                ch.step(v.tensor_tensor(mu[:, :], mu[:, :], sq[:, 0, 0:TILES * G], ALU.mult))
                v.tensor_tensor(groups, groups, mu[:, :].unsqueeze(2).to_broadcast(wide), ALU.mult).then_inc(s["gn"], 1)
                ch.end()
                add(b)

            each_batch_ahead(v, lambda: ln_vector(v, s, 0), step)

        INIT = 1
        mask_f = (hh[:, 0, 0:P], hh[:, 1, 0:P])
        BIASES = ((bqkv[:, :], "bqkv"), (bo[:, :], "bo"), (bl[:, :], "bl"), (bgate[:, :], "bgate"), (bmix[:, :], "bmix"))
        WEIGHTS = ((wqkv, "wqkv"), (wo, "wo"), (wl, "wl"), (wmix, "wmix"))
        CONSTS = 16 * 5
        LATE = 16 * (2 + len(BIASES) + len(WEIGHTS) + 3)

        def restart(sp, s):
            for c in s.values():
                sp.sem_clear(c)
                sp.sem_inc(c, 1)
            sp.sem_inc(s_again, 1)

        @block.sync
        def _(sp):
            x = d["L0_attn_x"].rearrange("b (h p o) e -> b p h (o e)", h=2, o=2)
            for b in range(B):
                sp.dma_start(X[:, bass.ds(b * TILES, TILES), :].rearrange("p (h o) e -> p h (o e)", o=2), x[b]).then_inc(s_w["x"], 16)
            for c in counted:
                sp.sem_inc(c, 1)
            sp.sem_inc(s_go, 1)
            sp.wait_ge(s_zero, 1)
            sp.dma_start(XS.rearrange("(i p) e -> p i e", p=P), zeros[:, :].unsqueeze(1).to_broadcast([P, SLOT_TILES, E]))\
              .then_inc(s_w["slots"], 16)
            sp.dma_start(w13[:, :, :], d["w13"].rearrange("(k p) n -> p k n", p=P)).then_inc(s_w["ffn"], 16)
            sp.dma_start(w2[0:HK, :, :], d["w2"].rearrange("(k p) n -> p k n", p=HK)).then_inc(s_w["ffn"], 16)
            routed_sync(sp, mo, dmas[0])
            sp.wait_ge(done["f0"], 1)
            restart(sp, mo)
            attn_sync(sp)
            sp.wait_ge(done["at"], 1)
            sp.dma_start(w13[:, :, :], d["w13"].rearrange("(k p) n -> p k n", p=P)).then_inc(s_w["ffn"], 16)
            sp.dma_start(w2[0:HK, :, :], d["w2"].rearrange("(k p) n -> p k n", p=HK)).then_inc(s_w["ffn"], 16)
            routed_sync(sp, mo, dmas[1])
            sp.wait_ge(done["l0"], 1)
            restart(sp, lo)
            sp.wait_ge(done["l1"], 1)
            o = out.rearrange("b (h p o) e -> b p h (o e)", h=2, o=2)
            for b in range(B):
                sp.dma_start(o[b], X[:, bass.ds(b * TILES, TILES), :].rearrange("p (h o) e -> p h (o e)", o=2)).then_inc(s_out, 16)
            sp.wait_ge(s_out, 16 * B)

        @block.gpsimd
        def _(g):
            g.memset(zeros[:, :], 0.0).then_inc(s_zero, 1)
            g.memset(epsc[:, :], EPS).then_inc(s_pool, 1)
            g.memset(mhalf[:, :], -0.5).then_inc(s_pool, 1)
            for dst, name in ((ident, "ident"), (mask_f[0], "mask_qk"), (mask_f[1], "mask_kq")):
                g.dma_start(dst, d[name]).then_inc(s_w["const"], 16)
            g.dma_start(iota[:, :], d["iota"].rearrange("(a n) -> a n", a=1).to_broadcast([P, SLOT_TILES])).then_inc(s_w["const"], 16)
            g.dma_start(gates_w[:, :, :], d["gates_w"].rearrange("(k p) n -> p k n", p=P)).then_inc(s_w["const"], 16)
            g.dma_start(rope_a[:, :, :, :], d["rope_a"].rearrange("p (n s c) -> p n s c", n=TILES, s=2)).then_inc(s_w["late"], 16)
            g.dma_start(rope_m[:, :, :, :], d["rope_m"].rearrange("p (n s c) -> p n s c", n=TILES, s=2)).then_inc(s_w["late"], 16)
            for dst, name in BIASES:
                n = d[name].shape[0]
                g.dma_start(dst, d[name].rearrange("(a n) -> a n", a=1).to_broadcast([P, n])).then_inc(s_w["late"], 16)
            for dst, name in WEIGHTS:
                g.dma_start(dst[:, :, :], d[name].rearrange("(k p) n -> p k n", p=P)).then_inc(s_w["late"], 16)
            g.dma_start(wlb[:, :], d["wlb"]).then_inc(s_w["late"], 16)
            for dst, name in ((gnw, "gnw"), (gnb, "gnb")):
                g.dma_start(dst[:, :], d[name]).then_inc(s_w["late"], 16)
            g.wait_ge(s_pool, 2)
            g.wait_ge(s_go, 1)
            moe_gpsimd(g, mo, dmas[0])
            g.wait_ge(done["f0"], 1)
            g.wait_ge(s_w["late"], LATE)
            attn_gpsimd(g)
            g.wait_ge(done["at"], 1)
            g.wait_ge(s_again, 1)
            g.sem_inc(s_stood, 1)
            moe_gpsimd(g, mo, dmas[1])
            g.wait_ge(done["f1"], 1)
            lora_gpsimd(g, lo)
            g.wait_ge(done["l0"], 1)
            mix_gpsimd(g)
            g.wait_ge(done["mx"], 1)
            g.wait_ge(s_again, 2)
            g.sem_inc(s_stood, 1)
            lora_gpsimd(g, lo)

        @block.scalar
        def _(a):
            a.wait_ge(s_go, 1)
            moe_scalar(a, mo)
            a.wait_ge(done["f0"], 1)
            attn_scalar(a)
            a.wait_ge(done["at"], 1)
            a.wait_ge(s_again, 1)
            a.sem_inc(s_stood, 1)
            moe_scalar(a, mo)
            a.wait_ge(done["f1"], 1)
            lora_scalar(a, lo)
            a.wait_ge(done["l0"], 1)
            mix_scalar(a)
            a.wait_ge(done["mx"], 1)
            a.wait_ge(s_again, 2)
            a.sem_inc(s_stood, 1)
            lora_scalar(a, lo)

        @block.tensor
        def _(t):
            t.wait_ge(s_w["const"], CONSTS)
            t.wait_ge(s_init, INIT)
            t.wait_ge(s_go, 1)
            moe_tensor(t, mo, 32)
            t.wait_ge(done["f0"], 1)
            t.wait_ge(s_w["late"], LATE)
            attn_tensor(t)
            t.wait_ge(done["at"], 1)
            t.wait_ge(s_again, 1)
            t.sem_inc(s_stood, 1)
            moe_tensor(t, mo, 64)
            t.wait_ge(done["f1"], 1)
            lora_tensor(t, lo)
            t.wait_ge(done["l0"], 1)
            mix_tensor(t)
            t.wait_ge(done["mx"], 1)
            t.wait_ge(s_again, 2)
            t.sem_inc(s_stood, 1)
            lora_tensor(t, lo)

        @block.vector
        def _(v):
            v.wait_ge(s_w["const"], CONSTS)
            v.wait_ge(s_go, 1)
            v.tensor_copy(identb[:, :], ident[:, :])
            v.tensor_copy(mask_qk[:, :], mask_f[0])
            v.memset(ones[:, :], 1.0)
            v.tensor_scalar(tri[:, :], mask_f[0], 0.0, None, ALU.is_lt)
            v.tensor_copy(mask_kq[:, :], mask_f[1]).then_inc(s_init, 1)
            v.wait_ge(s_init, INIT)
            v.wait_ge(s_w["x"], 16 * B)

            def close(ph, sem_x, n):
                need(v, sem_x, n)
                v.tensor_copy(stats[:, 0, 0:1], mv[:, 0, 0:1]).then_inc(done[ph], 1)
                v.wait_ge(done[ph], 1)

            for ph in ("f0", "at", "f1", "l0", "mx", "l1"):
                if ph in ("f1", "l1"):
                    v.wait_ge(s_again, 1 if ph == "f1" else 2)
                    v.sem_inc(s_stood, 1)
                if ph in ("f0", "f1"):
                    moe_vector(v, mo, dmas[0 if ph == "f0" else 1])
                    need(v, mo["comb"], B * TILES + AHEAD)
                    close(ph, mo["u_acc"], B * NU + AHEAD)
                elif ph == "at":
                    v.wait_ge(s_w["late"], LATE)
                    v.tensor_scalar(blh[:, :], bl[:, :], 0.5, None, ALU.mult)
                    attn_vector(v)
                    close(ph, at["x"], B * 2)
                elif ph == "mx":
                    mix_vector(v)
                    close(ph, mi["x"], B)
                else:
                    lora_vector(v, lo)
                    close(ph, lo["read"], (B + 1) * TILES)


def tables():
    c = {}
    c["ident"] = np.eye(P, dtype=np.float32)
    q, k = np.arange(P)[:, None], np.arange(P)[None, :]
    c["mask_qk"] = np.where(k > q, np.float32(NEG), np.float32(0))
    c["mask_kq"] = np.ascontiguousarray(c["mask_qk"].T)
    c["iota"] = np.arange(SLOT_TILES, dtype=np.float32)

    def rope(pos, dim):
        inv = (np.float32(1) / np.power(np.float32(10000.0), np.arange(0, dim, 2, dtype=np.float32) / np.float32(dim))).astype(np.float32)
        ang = pos.astype(np.float32)[..., None] * inv
        cos = np.repeat(np.cos(ang), 2, -1)
        sin = np.stack([-np.sin(ang), np.sin(ang)], -1).reshape(cos.shape)
        return np.stack([cos, sin], -2).astype(np.float32)

    p, n = np.arange(P)[:, None], np.arange(TILES)[None, :]
    c["rope_a"] = rope(n * P + p, D).reshape(P, -1)
    c["rope_m"] = rope((n // 2) * 256 + 2 * p + n % 2, RD).reshape(P, -1)
    return c


def kernel(**inputs):
    import numpy as _np
    import concourse.bacc as _bacc
    from concourse import mybir as _mybir
    from concourse.bass_utils import run_bass_kernel_spmd as _run

    a = {n: _np.asarray(v) for n, v in inputs.items()}
    su = a["L0_ffn_shared_gate_up_w"].reshape(2, SH, I, E)
    host = {
        "L0_attn_x": a["L0_attn_x"],
        "gates_w": _np.concatenate([a["L0_ffn_gate_w"], a["L0_ffn_sgate_w"]], 0).T,
        "w13": _np.concatenate([a["L0_ffn_w13"].reshape(NE * 2 * I, E), su.transpose(1, 0, 2, 3).reshape(SH * 2 * I, E)], 0).T,
        "w2": _np.concatenate([a["L0_ffn_w2"].transpose(2, 0, 1),
                               a["L0_ffn_shared_down_w"].reshape(E, SH, I).transpose(2, 1, 0)], 1).reshape(I, UNITS * E),
        "wqkv": _np.concatenate([a["L0_attn_Wq"], a["L0_attn_Wk"], a["L0_attn_Wv"]], 0).T,
        "wo": a["L0_attn_Wo"].T,
        "wl": _np.concatenate([a["L1_ffn_W"], a["L1_ffn_lora_A"].reshape(LR, E), a["L1_ffn_gate_w"]], 0).T,
        "wlb": a["L1_ffn_lora_B"].transpose(0, 2, 1).reshape(LR, E),
        "wmix": a["L1_attn_W_Q"],
        "bqkv": _np.concatenate([a["L0_attn_bq"], a["L0_attn_bk"], a["L0_attn_bv"]]),
        "bo": a["L0_attn_bo"], "bl": a["L1_ffn_b"], "bgate": a["L1_ffn_gate_b"], "bmix": a["L1_attn_hh_b"],
        "gnw": a["L1_attn_gn_weight"].reshape(KT, P).T, "gnb": a["L1_attn_gn_bias"].reshape(KT, P).T,
    }
    host.update(tables())
    nc = _bacc.Bacc("TRN2", target_bir_lowering=False, num_devices=1)
    arrays, d = {}, {}
    for name, v in host.items():
        arrays[f"in_{name}"] = _np.ascontiguousarray(v)
        d[name] = nc.dram_tensor(f"in_{name}", v.shape, _mybir.dt.from_np(v.dtype), kind="ExternalInput").ap()
    out = nc.dram_tensor("out_x", (B, T, E), F32, kind="ExternalOutput").ap()
    XS, YS = (nc.dram_tensor(n, (SLOT_TILES * P, E), F32, kind="Internal").ap() for n in ("slots_in", "slots_out"))
    build(nc, d, XS, YS, out)
    r = _run(nc, [arrays], core_ids=[0])
    return r.results[0]["out_x"]
```

```python
from contextlib import ExitStack

import concourse.bass as bass
import numpy as np
from concourse import mybir

F32 = mybir.dt.float32
BF16 = mybir.dt.bfloat16
U32 = mybir.dt.uint32
I32 = mybir.dt.int32
ALU = mybir.AluOpType
ACT = mybir.ActivationFunctionType
AX_X = mybir.AxisListType.X

P = 128
B, T, E = 8, 512, 256
TILES = T // P
KT = E // P
NE, TOPK = 16, 4
I = 176
SI = 704
CHUNKS = [min(P, SI - c) for c in range(0, SI, P)]
NC = len(CHUNKS)
SLOT_TILES = B * T * TOPK // P + NE
HK = I // 2
H, D = 16, 16
STACK = 6 * D
ROWS = STACK + 3
LE, LK, R = 8, 2, 16
LR = LE * R
LCOLS = E + LR + LE
RD = 64
G, GC = 32, 8
EPS = 1e-5
NEG = -1e30
WORK = 10400


class Chain:

    def __init__(self, eng, sem, per, need):
        self.eng, self.sem, self.per, self.need = eng, sem, per, need

    def start(self, it):
        self.it, self.n = it, 0

    def step(self, ins, stand=None):
        self.n += 1
        ins.then_inc(self.sem, 1)
        (stand or self.need)(self.eng, self.sem, self.it * self.per + self.n)

    def end(self):
        assert self.n == self.per, self.n


def build(nc, d, XS, YS, out):
    with ExitStack() as ctx:
        def sb(name, shape, dt=F32):
            return ctx.enter_context(nc.sbuf_tensor(name, shape, dt))[(slice(None),) * len(shape)]

        def sem(name):
            return ctx.enter_context(nc.semaphore(name))

        X = sb("X", [P, B * TILES, E])
        w13 = sb("w13", [P, KT, NE * 2 * I + 2 * SI])
        w2 = sb("w2", [P, 2, NE * E])
        ws2 = sb("ws2", [P, NC, E])
        gates_w = sb("gates_w", [P, KT, NE + 1])
        wqkv = sb("wqkv", [P, KT, 3 * E])
        wo = sb("wo", [P, KT, E])
        wl = sb("wl", [P, KT, LCOLS])
        wlb = sb("wlb", [LR, E])
        wmix = sb("wmix", [P, KT, E])
        bqkv = sb("bqkv", [P, 3 * E])
        bo = sb("bo", [P, E])
        bl = sb("bl", [P, E])
        blh = sb("blh", [P, E])
        bgate = sb("bgate", [P, LE])
        bmix = sb("bmix", [P, E])
        gnw = sb("gnw", [P, KT])
        gnb = sb("gnb", [P, KT])
        ident = sb("ident", [P, P])
        identb = sb("identb", [P, P], BF16)
        mask_qk = sb("mask_qk", [P, P], BF16)
        mask_kq = sb("mask_kq", [P, P], BF16)
        iota = sb("iota", [P, SLOT_TILES])
        tri = sb("tri", [P, P], BF16)
        ones = sb("ones", [P, P], BF16)
        zeros = sb("zeros", [P, E])
        rope_a = sb("rope_a", [P, TILES, 2, D])
        rope_m = sb("rope_m", [P, TILES, 2, RD])
        epsc = sb("epsc", [P, TILES])
        mhalf = sb("mhalf", [P, TILES])
        stats = sb("stats", [P, TILES, 6])
        mv = sb("mv", [P, B * TILES, 2])
        mvb = sb("mvb", [P, TILES, 2])
        veps = sb("veps", [P, TILES])
        rstd = sb("rstd", [P, B * TILES])
        xn = sb("xn", [P, TILES, E])
        xnT = sb("xnT", [P, KT, T])
        work = sb("work", [P, WORK])

        used = [0]

        def part(shape, dt=F32):
            n = int(np.prod(shape[1:]))
            words = n if dt in (F32, U32, I32) else (n + 1) // 2
            ap = work[0:shape[0], used[0]:used[0] + words]
            used[0] += words
            assert used[0] <= WORK, used[0]
            if dt != F32:
                ap = ap.bitcast(dt)
            if len(shape) == 3:
                ap = ap.rearrange("p (a b) -> p a b", b=shape[2])
            if len(shape) == 4:
                ap = ap.rearrange("p (a b c) -> p a b c", b=shape[2], c=shape[3])
            return ap

        bank = [ctx.enter_context(nc.psum_tensor(f"bank{i}", [P, 512], F32))[:, :] for i in range(8)]

        s_w = {n: sem(f"s_{n}") for n in ("x", "const", "late", "ffn", "slots")}
        s_init = sem("s_init")
        s_out = sem("s_out")
        s_pool = sem("s_pool")
        s_go = sem("s_go")
        s_zero = sem("s_zero")
        s_again = sem("s_again")
        s_stood = sem("s_stood")
        PHASES = ("f0", "at", "f1", "l0", "mx", "l1")
        done = {p: sem(f"done_{p}") for p in PHASES}

        counted = []

        def sems(ph, names):
            made = {n: sem(f"{ph}_{n}") for n in names.split()}
            counted.extend(made.values())
            return made

        PREP = "stats aggr mv veps rstd xn xt xnT prev"
        mo = sems("mo", PREP + " logits lg chain ex member count ichain tchain ready sxn sfree gidx comb cchain "
                  "u_xn u_xt u_xnT u_up u_act u_hid u_down u_acc "
                  "ld0 ld1 ld2 ld3 r_tx r_xT r_up r_act r_hid r_tr r_hT r_down r_ys st0 st1 st2 st3")
        dmas = [{n: sem(f"f{layer}_{n}") for n in ("scat", "gat0", "gat1")} for layer in range(2)]
        at = sems("at", PREP + " qk v qkb vb rot_c tile split tr qkT s mx rest m3 m3T m3s maxrow st pexp pv ot bt recip norm onT oT wo xbo x")
        lo = sems("lo", PREP + " biased read up lg chain ex gated tr gT lora")
        mi = sems("mx", PREP + " biased pre chain th ve sd rs8 gn tr x")

        block = ctx.enter_context(nc.Block())

        def need(eng, sem, n):
            if not isinstance(n, int) or n > 0:
                eng.wait_ge(sem, n + 1)

        def stand(eng, sem, n):
            need(eng, sem, n)
            eng.sem_inc(s_stood, 1)

        def each_batch(eng):
            return eng.Fori(0, B)

        def each_batch_ahead(eng, first, step):
            first()
            with eng.Fori(0, B - 1) as b:
                step(b, True)
            step(B - 1, False)

        def ln_stats(v, s, b):
            for j in range(TILES):
                v.bn_stats(stats[:, j, :], X[:, b * TILES + j, :]).then_inc(s["stats"], 1)
            stand(v, s["stats"], (b + 1) * TILES)
            for j in range(TILES):
                v.bn_aggr(mvb[:, j, :], stats[:, j, :]).then_inc(s["aggr"], 1)
            need(v, s["aggr"], (b + 1) * TILES)
            v.tensor_copy(mv[:, bass.ds(b * TILES, TILES), :], mvb[:, :, :]).then_inc(s["mv"], 1)

        def ln_normal(v, s, b):
            need(v, s["rstd"], b + 1)
            need(v, s["xt"], b)
            for j in range(TILES):
                t = b * TILES + j
                v.tensor_scalar(xn[:, j, :], X[:, t, :], mv[:, t, 0:1], rstd[:, bass.ds(t, 1)],
                                ALU.subtract, ALU.mult).then_inc(s["xn"], 1)

        def ln_vector(v, s, b):
            ln_stats(v, s, b)
            ln_normal(v, s, b)

        def ln_gpsimd(g, s, b):
            need(g, s["rstd"], b)
            need(g, s["mv"], b + 1)
            g.tensor_tensor(veps[:, :], mv[:, bass.ds(b * TILES, TILES), 1], epsc[:, 0:TILES], ALU.add).then_inc(s["veps"], 1)
            need(g, s["veps"], b + 1)
            g.tensor_tensor(rstd[:, bass.ds(b * TILES, TILES)], veps[:, :], mhalf[:, 0:TILES], ALU.pow).then_inc(s["rstd"], 1)

        def ln_tensor(t, s, b):
            need(t, s["xn"], (b + 1) * TILES)
            need(t, s["xnT"], b * KT)
            for k in range(KT):
                for j in range(TILES):
                    m = t.transpose(bank[k][:, j * P:(j + 1) * P], xn[:, j, k * P:(k + 1) * P], ident[:, :])
            m.then_inc(s["xt"], 1)

        def ln_scalar(a, s, b, natural=False):
            need(a, s["xt"], b + 1)
            need(a, s["prev"], b)
            for k in range(KT):
                if natural:
                    dst = xnT[:, k, :].rearrange("p (h t o) -> p h o t", h=2, o=2)
                    src = bank[k][:, :].rearrange("p (h o t) -> p h o t", h=2, o=2)
                else:
                    dst, src = xnT[:, k, :], bank[k][:, :]
                a.activation(dst, src, ACT.Copy).then_inc(s["xnT"], 1)

        used[0] = 0
        lg = part([P, TILES, NE + 1])
        lgs = part([P, TILES, NE])
        top8 = part([P, TILES, 8])
        idx8 = part([P, TILES, 8], U32)
        idxf = part([P, TILES, 8])
        ex = part([P, TILES, NE + 1])
        exk = part([P, TILES, TOPK])
        den = part([P, TILES])
        rden = part([P, TILES])
        once = used[0]
        chosen = part([P, B * TILES * TOPK, NE], BF16)
        chosen4 = chosen.rearrange("p (t k) e -> p t k e", k=TOPK)
        member = part([P, B * TILES, NE], BF16)
        once_end = used[0]
        used[0] = once
        big_t = part([1, SLOT_TILES * NE], BF16)
        assert used[0] <= once_end
        used[0] = once_end
        wk = part([P, B * TILES, TOPK])
        wsh = part([P, B * TILES])
        slot = part([P, B * TILES * TOPK], U32)
        slots16 = part([P, 2, TILES * TOPK], U32)
        tile_e = part([P, SLOT_TILES], I32)
        ntile = part([P, 2, NE])
        ntile_i = part([P, NE], I32)
        tilef = part([1, SLOT_TILES])
        one_tile = used[0]
        sg = part([P, 2, I])
        hid = part([P, 2, I])
        hT = part([HK, 2, 2 * P])
        xT = part([P, 2, 2 * P])
        region_a = used[0]
        used[0] = one_tile
        ssg = part([P, 2, T])
        assert used[0] <= region_a
        used[0] = region_a
        big = part([P, SLOT_TILES * NE])
        region_a_end = used[0]
        used[0] = region_a
        xs = part([P, 4, E])
        ys = part([P, 4, E])
        used[0] = region_a
        shid = part([P, NC, T])
        used[0] = max(region_a_end, used[0])
        region_b = used[0]
        tot = part([P, 2, B * TILES, NE])
        pos = part([P, B * TILES, NE])
        used[0] = region_b
        xsc = part([P, 2, TILES, E])
        used[0] = region_b
        got = part([P, 2, TOPK, E])
        psL = bank[2][:, 0:TILES * 32].rearrange("p (j c) -> p j c", c=32)[:, :, 0:NE + 1]

        def router_tensor(t, s):
            def step(b, ahead):
                need(t, s["xnT"], (b + 1) * KT)
                need(t, s["lg"], b)
                for j in range(TILES):
                    for k in range(KT):
                        m = t.matmul(bank[2][:, j * 32:j * 32 + NE + 1], xnT[:, k, j * P:(j + 1) * P],
                                     gates_w[:, k, :], start=(k == 0), stop=(k == KT - 1))
                m.then_inc(s["prev"], 1)
                if ahead:
                    ln_tensor(t, s, b + 1)

            each_batch_ahead(t, lambda: ln_tensor(t, s, 0), step)
            need(t, s["member"], 1)
            members = member.rearrange("p t e -> p (t e)")
            t.matmul(bank[6][:, :], tri[:, :], members, start=True, stop=True)
            t.matmul(bank[7][:, :], ones[:, :], members, start=True, stop=True).then_inc(s["count"], 1)

        def router_scalar(a, s):
            def step(b, ahead):
                if ahead:
                    ln_scalar(a, s, b + 1)
                need(a, s["logits"], b + 1)
                a.activation(ex[:, :, 0:NE], lgs[:, :, :], ACT.Exp)
                a.activation(exk[:, :, :], idxf[:, :, 0:TOPK], ACT.Exp)
                a.activation(ex[:, :, NE:NE + 1], lg[:, :, NE:NE + 1], ACT.Exp, scale=-1.0).then_inc(s["ex"], 1)

            each_batch_ahead(a, lambda: ln_scalar(a, s, 0), step)

        def router_gpsimd(g, s):
            with each_batch(g) as b:
                ln_gpsimd(g, s, b)

        def router_vector(v, s):
            ch = Chain(v, s["chain"], 10, need)
            def step(b, has):
                ch.start(b)
                need(v, s["prev"], b + 1)
                v.tensor_copy(lg[:, :, :], psL).then_inc(s["lg"], 1)
                if has(1):
                    ln_normal(v, s, b + 1)
                stand(v, s["lg"], b + 1)
                for j in range(TILES):
                    ins = v.max(top8[:, j, :], lg[:, j, 0:NE])
                ch.step(ins, stand)
                for j in range(TILES):
                    ins = v.max_index(idx8[:, j, :], top8[:, j, :], lg[:, j, 0:NE])
                ch.step(ins)
                ch.step(v.tensor_copy(idxf[:, :, :], idx8[:, :, :]))
                ch.step(v.tensor_tensor(
                    chosen4[:, bass.ds(b * TILES, TILES), :, :],
                    idxf[:, :, 0:TOPK].unsqueeze(3).to_broadcast([P, TILES, TOPK, NE]),
                    iota[:, 0:NE].unsqueeze(1).unsqueeze(1).to_broadcast([P, TILES, TOPK, NE]), ALU.is_equal))
                v.tensor_reduce(member[:, bass.ds(b * TILES, TILES), :],
                                chosen4[:, bass.ds(b * TILES, TILES), :, :].rearrange("p j k e -> p j e k"), AX_X, ALU.max)
                v.tensor_tensor(lgs[:, :, :], lg[:, :, 0:NE], top8[:, :, 0:1].to_broadcast([P, TILES, NE]),
                                ALU.subtract)
                v.tensor_tensor(idxf[:, :, 0:TOPK], top8[:, :, 0:TOPK], top8[:, :, 0:1].to_broadcast([P, TILES, TOPK]),
                                ALU.subtract).then_inc(s["logits"], 1)
                if has(2):
                    ln_stats(v, s, b + 2)
                need(v, s["ex"], b + 1)
                ch.step(v.tensor_reduce(den[:, :], ex[:, :, 0:NE], AX_X, ALU.add))
                ch.step(v.reciprocal(rden[:, :], den[:, :]))
                ch.step(v.tensor_scalar(rden[:, :], rden[:, :], 0.5, None, ALU.mult))
                v.tensor_tensor(wk[:, bass.ds(b * TILES, TILES), :], exk[:, :, :],
                                rden[:, :].unsqueeze(2).to_broadcast([P, TILES, TOPK]), ALU.mult)
                ch.step(v.tensor_scalar(den[:, :], ex[:, :, NE], 2.0, 2.0, ALU.mult, ALU.add))
                ch.step(v.reciprocal(rden[:, :], den[:, :]))
                ch.step(v.tensor_copy(wsh[:, bass.ds(b * TILES, TILES)], rden[:, :]))
                ch.end()

            for b in range(2):
                ln_stats(v, s, b)
            ln_normal(v, s, 0)
            with v.Fori(0, B - 2) as b:
                step(b, lambda i: True)
            for b in range(B - 2, B):
                step(b, lambda i, b=b: b + i < B)
            v.tensor_copy(den[:, :], rden[:, :]).then_inc(s["member"], 1)

        def slots_vector(v, s):
            c = Chain(v, s["ichain"], 21, need)
            c.start(0)
            need(v, s["count"], 1)
            c.step(v.tensor_copy(tot[:, 0].rearrange("p t e -> p (t e)"), bank[7][:, :]))
            src, n = 0, 1
            while n < B * TILES:
                v.tensor_copy(tot[:, 1 - src, 0:n, :], tot[:, src, 0:n, :])
                c.step(v.tensor_tensor(tot[:, 1 - src, n:, :], tot[:, src, n:, :], tot[:, src, 0:B * TILES - n, :], ALU.add))
                src, n = 1 - src, 2 * n
            flat = tot[:, 1 - src].rearrange("p t e -> p (t e)")
            c.step(v.tensor_tensor(flat, tot[:, src].rearrange("p t e -> p (t e)"), bank[7][:, :], ALU.subtract))
            c.step(v.tensor_tensor(pos.rearrange("p t e -> p (t e)"), flat, bank[6][:, :], ALU.add))
            c.step(v.tensor_scalar(ntile_i[:, :], tot[:, src, B * TILES - 1, :], 1.0 / P,
                                   (P - 1.0) / P - 0.5 + 0.5 / P, ALU.mult, ALU.add))
            c.step(v.tensor_copy(ntile[:, 0, :], ntile_i[:, :]))
            e_src, n = 0, 1
            while n < NE:
                v.tensor_copy(ntile[:, 1 - e_src, 0:n], ntile[:, e_src, 0:n])
                c.step(v.tensor_tensor(ntile[:, 1 - e_src, n:], ntile[:, e_src, n:], ntile[:, e_src, 0:NE - n], ALU.add))
                e_src, n = 1 - e_src, 2 * n
            ends = ntile[:, e_src, :]
            starts = ntile[:, 1 - e_src, :]
            c.step(v.tensor_copy(starts, ntile_i[:, :]))
            c.step(v.tensor_tensor(starts, ends, starts, ALU.subtract))
            c.step(v.tensor_scalar(starts, starts, float(P), None, ALU.mult))
            c.step(v.tensor_tensor(pos[:, :, :], pos[:, :, :], starts.unsqueeze(1).to_broadcast([P, B * TILES, NE]), ALU.add))
            picked = big[:, 0:B * TILES * TOPK * NE].rearrange("p (t k e) -> p t k e", k=TOPK, e=NE)
            c.step(v.tensor_tensor(picked, chosen4[:, :, :, :], pos[:, :, :].unsqueeze(2).to_broadcast([P, B * TILES, TOPK, NE]),
                                   ALU.mult))
            slotf = tot[:, 0].rearrange("p t e -> p (t e)")[:, 0:B * TILES * TOPK]
            c.step(v.tensor_reduce(slotf, big[:, 0:B * TILES * TOPK * NE].rearrange("p (a e) -> p a e", e=NE), AX_X, ALU.add))
            c.step(v.tensor_copy(slot[:, :], slotf))
            c.end()
            return ends

        def tiles_vector(v, s, ends):
            c = Chain(v, s["tchain"], 3, need)
            c.start(0)
            table = big_t[0:1, :].rearrange("p (i e) -> p i e", e=NE)
            wide = [1, SLOT_TILES, NE]
            c.step(v.tensor_tensor(table, iota[0:1, :].unsqueeze(2).to_broadcast(wide), ends[0:1].unsqueeze(1).to_broadcast(wide),
                                   ALU.is_ge))
            tef = tilef[0:1, :]
            c.step(v.tensor_reduce(tef, table, AX_X, ALU.add))
            c.step(v.tensor_scalar(tile_e[0:1, :], tef, float(NE - 1), None, ALU.min))
            c.end()
            v.tensor_copy(den[:, :], rden[:, :]).then_inc(s["ready"], 1)

        AHEAD = 2
        HALF = B // 2

        def each_of_half(eng, half, first, step):
            first(half * HALF)
            with eng.Fori(0, HALF - 1) as i:
                step(i + half * HALF, i, True)
            step(half * HALF + HALF - 1, HALF - 1, False)

        def shared_tensor(t, s, half):
            def turn(b):
                need(t, s["u_xn"], (b + 1) * TILES)
                need(t, s["u_xnT"], b * KT)
                for k in range(KT):
                    for j in range(TILES):
                        m = t.transpose(bank[k][:, j * P:(j + 1) * P], xn[:, j, k * P:(k + 1) * P], ident[:, :])
                m.then_inc(s["u_xt"], 1)

            def step(b, i, ahead):
                need(t, s["u_xnT"], (b + 1) * KT)
                for c, rows in enumerate(CHUNKS):
                    need(t, s["u_hid"], b * NC + c + 1)
                    for side in range(2):
                        first = NE * 2 * I + side * SI + c * P
                        for k in range(KT):
                            m = t.matmul(bank[2 + 2 * side + c % 2][0:rows, :], w13[:, k, first:first + rows], xnT[:, k, :],
                                         start=(k == 0), stop=(k == KT - 1))
                    m.then_inc(s["u_up"], 1)
                if ahead:
                    turn(b + 1)
                need(t, s["u_hid"], (b + 1) * NC + AHEAD)
                for j in range(TILES):
                    need(t, s["u_acc"], b * TILES + j + 1)
                    for c, rows in enumerate(CHUNKS):
                        m = t.matmul(bank[6 + j % 2][:, 0:E], shid[0:rows, c, j * P:(j + 1) * P], ws2[0:rows, c, :],
                                     start=(c == 0), stop=(c == NC - 1))
                    m.then_inc(s["u_down"], 1)

            each_of_half(t, half, turn, step)

        def shared_scalar(a, s, half):
            def copy(b):
                need(a, s["u_xt"], b + 1)
                need(a, s["u_up"], b * NC)
                for k in range(KT):
                    a.activation(xnT[:, k, :], bank[k][:, :], ACT.Copy).then_inc(s["u_xnT"], 1)

            def step(b, i, ahead):
                for c, rows in enumerate(CHUNKS):
                    need(a, s["u_up"], b * NC + c + 1)
                    need(a, s["u_hid"], b * NC + c + 1)
                    a.activation(ssg[0:rows, c % 2, :], bank[2 + c % 2][0:rows, :], ACT.Silu).then_inc(s["u_act"], 1)
                if ahead:
                    copy(b + 1)

            each_of_half(a, half, copy, step)

        def shared_vector(v, s, half, first, start, between):
            def normal(b):
                need(v, s["u_xt"], b)
                for j in range(TILES):
                    t = b * TILES + j
                    v.tensor_scalar(xn[:, j, :], X[:, t, :], mv[:, t, 0:1], rstd[:, bass.ds(t, 1)],
                                    ALU.subtract, ALU.mult).then_inc(s["u_xn"], 1)

            def step(b, i, ahead):
                start(i)
                need(v, s["u_down"], b * TILES)
                for c, rows in enumerate(CHUNKS):
                    need(v, s["u_act"], b * NC + c + 1)
                    v.tensor_tensor(shid[0:rows, c, :], ssg[0:rows, c % 2, :], bank[4 + c % 2][0:rows, :],
                                    ALU.mult).then_inc(s["u_hid"], 1)
                    if c == 1 and ahead:
                        normal(b + 1)
                    between(i, c, ahead)
                for j in range(TILES):
                    t = b * TILES + j
                    need(v, s["u_down"], t + 1)
                    v.scalar_tensor_tensor(out=X[:, t, :], in0=bank[6 + j % 2][:, 0:E], scalar=wsh[:, bass.ds(t, 1)],
                                           in1=X[:, t, :], op0=ALU.mult, op1=ALU.add).then_inc(s["u_acc"], 1)
                    if j % 2:
                        between(i, NC + j // 2, ahead)

            def begin(b):
                normal(b)
                first()

            each_of_half(v, half, begin, step)

        def scatter_vector(v, s, b, h):
            need(v, s["sfree"], b + 1)
            v.tensor_copy(slots16[:, h, :], slot[:, bass.ds(b * TILES * TOPK, TILES * TOPK)])
            for j in range(TILES):
                t = b * TILES + j
                ins = v.tensor_scalar(xsc[:, h, j, :], X[:, t, :], mv[:, t, 0:1], rstd[:, bass.ds(t, 1)], ALU.subtract, ALU.mult)
            ins.then_inc(s["sxn"], 1)

        def scatter_gpsimd(g, s, dma, b, h):
            need(g, s["sxn"], b + 1)
            g.sem_inc(s_stood, 1)
            for j in range(TILES):
                for k in range(TOPK):
                    c = j * TOPK + k
                    g.indirect_dma_start(XS[:, :], bass.IndirectOffsetOnAxis(slots16[:, h, c:c + 1], 0),
                                         xsc[:, h, j, :], None).then_inc(dma["scat"], 16)
            g.wait_ge(dma["scat"], (b + 1) * TILES * TOPK * 16)
            g.sem_inc(s["sfree"], 1)

        def gather_gpsimd(g, s, dma, tile, q):
            need(g, s["comb"], tile + 1)
            g.sem_inc(s_stood, 1)
            for k in range(TOPK):
                c = (q % (2 * TILES)) * TOPK + k
                idx = slots16.rearrange("p a c -> p (a c)")[:, c:c + 1]
                g.indirect_dma_start(got[:, q % 2, k, :], None, YS[:, :], bass.IndirectOffsetOnAxis(idx, 0)).then_inc(dma[f"gat{q % 2}"], 16)

        def combine_vector(v, s, dma, ch, i, q):
            tile = i * 2 * TILES + q
            need(v, s["u_acc"], (i + HALF) * TILES + max(q - NC + 1, 0) * 2 + AHEAD)
            v.wait_ge(dma[f"gat{q % 2}"], (i * TILES + q // 2 + 1) * TOPK * 16)
            for k in range(TOPK):
                ins = v.scalar_tensor_tensor(out=X[:, tile, :], in0=got[:, q % 2, k, :], scalar=wk[:, tile, k:k + 1],
                                             in1=X[:, tile, :], op0=ALU.mult, op1=ALU.add)
                if k < TOPK - 1:
                    ch.step(ins)
            ins.then_inc(s["comb"], 1)
            need(v, s["comb"], tile + 1 + AHEAD)

        UNROLL = 8
        RING = 4

        def routed(eng, step):
            for r in range(UNROLL):
                step(0, r, lambda lag, r=r: 0 <= r - lag)
            with eng.Fori(1, SLOT_TILES // UNROLL - 1) as n:
                for r in range(UNROLL):
                    step(n, r, lambda lag: True)
            for r in range(UNROLL + 2):
                n = SLOT_TILES // UNROLL - 1
                step(n, r, lambda lag, r=r: r - lag < UNROLL)

        def expert_of(t, i):
            return t.value_load(tile_e[0:1, bass.ds(i, 1)], min_val=0, max_val=NE - 1)

        def routed_tensor(t, s):
            def turn(n, r):
                i = n * UNROLL + r
                need(t, s[f"ld{r % RING}"], 16 * (n * (UNROLL // RING) + r // RING + 1))
                need(t, s["r_xT"], i + 1)
                for k in range(KT):
                    m = t.transpose(bank[r % 2][:, k * P:(k + 1) * P], xs[:, r % RING, k * P:(k + 1) * P], ident[:, :])
                m.then_inc(s["r_tx"], 1)

            expert = {}

            def step(n, r, has):
                i = n * UNROLL + r
                if r == 0:
                    for l in (-2, -1, 0):
                        if has(-l):
                            expert[l] = expert_of(t, i + l)
                if has(-1):
                    turn(n, r + 1)
                if has(0):
                    need(t, s["r_xT"], i + 1 + AHEAD)
                    need(t, s["r_hid"], i + 1)
                    for k in range(KT):
                        m = t.matmul(bank[2 + r % 2][:, 0:2 * I], xT[:, r % 2, k * P:(k + 1) * P],
                                     w13[:, k, bass.ds(expert[r] * (2 * I), 2 * I)], start=(k == 0), stop=(k == KT - 1))
                    m.then_inc(s["r_up"], 1)
                    if r + 1 < UNROLL:
                        expert[r + 1] = expert_of(t, i + 1)
                if has(1):
                    h = (r - 1) % 2
                    need(t, s["r_hid"], i + AHEAD)
                    need(t, s["r_hT"], i)
                    for c in range(2):
                        m = t.transpose(bank[4 + h][0:HK, c * P:(c + 1) * P], hid[:, h, c * HK:(c + 1) * HK], ident[:, :])
                    m.then_inc(s["r_tr"], 1)
                if has(2):
                    h = r % 2
                    need(t, s["r_hT"], i - 1 + AHEAD)
                    need(t, s["r_ys"], i - 1)
                    for c in range(2):
                        m = t.matmul(bank[6 + h][:, 0:E], hT[:, h, c * P:(c + 1) * P],
                                     w2[0:HK, c, bass.ds(expert[r - 2] * E, E)], start=(c == 0), stop=(c == 1))
                    m.then_inc(s["r_down"], 1)

            need(t, s["u_acc"], HALF * TILES + AHEAD)
            turn(0, 0)
            routed(t, step)

        def routed_scalar(a, s):
            def copy_x(n, r):
                i = n * UNROLL + r
                need(a, s["r_tx"], i + 1 + RING)
                need(a, s["r_up"], i + 1)
                a.activation(xT[:, r % 2, :], bank[r % 2][:, 0:2 * P], ACT.Copy).then_inc(s["r_xT"], 1)

            def step(n, r, has):
                i = n * UNROLL + r
                if has(-1):
                    copy_x(n, r + 1)
                if has(0):
                    need(a, s["r_up"], i + 1 + AHEAD)
                    need(a, s["r_hid"], i + 1)
                    a.activation(sg[:, r % 2, :], bank[2 + r % 2][:, 0:I], ACT.Silu).then_inc(s["r_act"], 1)
                if has(1):
                    h = (r - 1) % 2
                    need(a, s["r_tr"], i + AHEAD)
                    need(a, s["r_down"], i)
                    a.activation(hT[:, h, :], bank[4 + h][0:HK, 0:2 * P], ACT.Copy).then_inc(s["r_hT"], 1)

            copy_x(0, 0)
            routed(a, step)

        def routed_vector(v, s):
            def step(n, r, has):
                i = n * UNROLL + r
                if has(0):
                    need(v, s["r_act"], i + 1)
                    need(v, s["r_tr"], i + 1)
                    v.tensor_tensor(hid[:, r % 2, :], sg[:, r % 2, :], bank[2 + r % 2][:, I:2 * I], ALU.mult).then_inc(s["r_hid"], 1)
                if has(2):
                    need(v, s["r_down"], i - 1 + AHEAD)
                    need(v, s[f"st{(r - 2) % RING}"], 16 * (n * (UNROLL // RING) + (r - 2) // RING))
                    v.tensor_copy(ys[:, (r - 2) % RING, :], bank[6 + r % 2][:, 0:E]).then_inc(s["r_ys"], 1)

            routed(v, step)

        def routed_sync(sp, s, dma):
            def load(n, r):
                i = n * UNROLL + r
                need(sp, s["r_tx"], i + 1)
                sp.dma_start(xs[:, r % RING, :], XS[bass.ds(i * P, P), :]).then_inc(s[f"ld{r % RING}"], 16)

            def step(n, r, has):
                i = n * UNROLL + r
                if has(-3):
                    load(n, r + 3)
                if has(2):
                    need(sp, s["r_ys"], i - 1 + AHEAD)
                    sp.dma_start(YS[bass.ds((i - 2) * P, P), :], ys[:, (r - 2) % RING, :]).then_inc(s[f"st{(r - 2) % RING}"], 16)

            need(sp, s["u_acc"], HALF * TILES + AHEAD)
            sp.wait_ge(dma["scat"], 16 * B * TILES * TOPK)
            load(0, 0)
            load(0, 1)
            load(0, 2)
            routed(sp, step)

        def moe_tensor(t, s, loaded):
            router_tensor(t, s)
            t.wait_ge(s_w["ffn"], loaded)
            shared_tensor(t, s, 0)
            need(t, s["ready"], 1)
            routed_tensor(t, s)
            need(t, s["r_ys"], SLOT_TILES + AHEAD)
            shared_tensor(t, s, 1)

        def moe_scalar(a, s):
            router_scalar(a, s)
            shared_scalar(a, s, 0)
            routed_scalar(a, s)
            shared_scalar(a, s, 1)

        def moe_vector(v, s, dma):
            for n in ("u_hid", "u_acc", "r_hid", "r_ys", "r_tr", "r_down", "r_hT", "r_xT", "r_up",
                      "comb", "sfree"):
                v.sem_inc(s[n], AHEAD)
            v.sem_inc(s["r_tx"], RING)
            router_vector(v, s)
            ends = []

            def meanwhile(i, q, ahead):
                if q == 3:
                    scatter_vector(v, s, 2 * i + 1, 1)
                if q == 5 and not ahead:
                    tiles_vector(v, s, ends[0])

            shared_vector(v, s, 0, lambda: ends.append(slots_vector(v, s)), lambda i: scatter_vector(v, s, 2 * i, 0), meanwhile)
            routed_vector(v, s)
            ch = Chain(v, s["cchain"], 2 * TILES * (TOPK - 1), need)

            def slots_of(i, h):
                v.tensor_copy(slots16[:, h, :], slot[:, bass.ds((2 * i + h) * TILES * TOPK, TILES * TOPK)]).then_inc(s["gidx"], 1)

            def start(i):
                ch.start(i)
                slots_of(i, 1)

            def between(i, q, ahead):
                combine_vector(v, s, dma, ch, i, q)
                if q == TILES and ahead:
                    slots_of(i + 1, 0)

            for r in range(RING):
                need(v, s[f"st{r}"], 16 * SLOT_TILES // RING)
            shared_vector(v, s, 1, lambda: slots_of(0, 0), start, between)

        def moe_gpsimd(g, s, dma):
            router_gpsimd(g, s)
            g.wait_ge(s_w["slots"], 16)
            with g.Fori(0, HALF) as i:
                for h in range(2):
                    scatter_gpsimd(g, s, dma, 2 * i + h, h)
            for r in range(RING):
                need(g, s[f"st{r}"], 16 * SLOT_TILES // RING)
            with g.Fori(0, HALF) as i:
                for q in range(2 * TILES):
                    if q % TILES == 0:
                        need(g, s["gidx"], 2 * i + q // TILES + 1)
                    gather_gpsimd(g, s, dma, i * 2 * TILES + q, q)

        used[0] = 0
        SL = 4
        SH4 = H // SL
        NST = SH4 * TILES
        VW = 32
        OFF = [0, 512, 896, 1152]
        QT, KTt = ([w[:, i, 0:H * T // 2].bitcast(BF16).rearrange("p (h t) -> p h t", t=T) for w in (w2, w13)] for i in range(2))
        VV = [w13[:, i, H * T // 2:H * T // 2 + TILES * H * VW].rearrange("p (n h d) -> p n h d", h=H, d=VW) for i in range(2)]
        on = ws2[:, 0:TILES, :]
        oT = part([P, KT, T])
        stk = part([P, 2 * H, STACK], BF16)
        qk = part([P, 2 * H, D])
        rc = part([P, 2 * H, D])
        rs = part([P, 2 * H, D])
        nmx = part([P, TILES, SH4])
        nmx_rest = part([P, TILES, SH4])
        m3 = part([P, TILES, 3, SH4], BF16)
        m3T = part([3 * SH4, T], BF16)
        PT = part([P, SH4, 1280])
        OT = part([P, T])
        ors = part([P, TILES, SH4])

        def psT(i):
            return bank[i][:, :].bitcast(BF16)

        MAX_STEPS = [(0, [0, 1, 2, 3]), (1, [0, 1]), (1, [2, 3])] + [(n, [h]) for n in (2, 3) for h in range(SH4)]
        NMAX = len(MAX_STEPS)
        MAX_AT = {0: (0, 1), 1: (2,), 2: (3, 4), 3: (5,), 4: (6, 7), 5: (8,), 6: (9,), 7: (10,)}
        MAX_AT_LAST = {7: (0, 1), 8: (2, 3), 9: (4, 5), 10: (6, 7), 11: (8, 9), 12: (10,)}

        def each_slot_batch(eng, batch):
            batch(0, 0, lambda i: i >= 0)
            with eng.Fori(0, 2) as i:
                batch(2 * i + 1, 1, lambda i: True)
                batch(2 * i + 2, 0, lambda i: True)
            for b in range(5, B):
                batch(b, b % 2, lambda i, b=b: b + i < B)

        def attn_tensor(t):
            s = at

            def normal(b):
                need(t, s["xn"], (b + 1) * TILES)
                need(t, s["qkT"], b * 16)
                need(t, s["vb"], b * TILES)
                for k in range(KT):
                    for j in range(TILES):
                        m = t.transpose(bank[k][:, j * P:(j + 1) * P], xn[:, j, k * P:(k + 1) * P], ident[:, :])
                m.then_inc(s["xt"], 1)

            def project_qk(b, n):
                if n == 0:
                    need(t, s["xnT"], (b + 1) * KT)
                else:
                    need(t, s["qkT"], b * 16 + 4 * n - 1)
                for k in range(KT):
                    m = t.matmul(bank[0][:, :], xnT[:, k, n * P:(n + 1) * P], wqkv[:, k, 0:2 * E],
                                 start=(k == 0), stop=(k == KT - 1))
                m.then_inc(s["qk"], 1)

            def stacks(b, n, g):
                if g < 2:
                    need(t, s["split"], b * TILES + n + 1)
                    if g == 1:
                        need(t, s["vb"], b * TILES + n)
                else:
                    need(t, s["qkT"], b * 16 + 4 * n + g - 1)
                for h in range(8):
                    m = t.transpose(psT(g % 2)[0:STACK, h * P:(h + 1) * P], stk[:, g * 8 + h, :], identb[:, :])
                m.then_inc(s["tr"], 1)

            def project_v(b, n):
                need(t, s["qkT"], b * 16 + 4 * n + 4)
                for k in range(KT):
                    m = t.matmul(bank[1][:, 0:E], xnT[:, k, n * P:(n + 1) * P], wqkv[:, k, 2 * E:3 * E],
                                 start=(k == 0), stop=(k == KT - 1))
                m.then_inc(s["v"], 1)

            def score(b, g, buf, r):
                n, hs = MAX_STEPS[r]
                w = (n + 1) * P
                c = b * SL + g
                if r == 1:
                    need(t, s["m3s"], c)
                else:
                    need(t, s["mx"], c * NMAX + max(r - 1, 0))
                for c, h in enumerate(hs):
                    h += g * SH4
                    o = c * w
                    t.matmul(bank[2 + r % 2][:, o:o + w], QT[buf][0:STACK, h, n * P:(n + 1) * P], KTt[buf][0:STACK, h, 0:w],
                             start=(c == 0), stop=False, skip_group_check=True)
                    m = t.matmul(bank[2 + r % 2][:, o + n * P:o + w], identb[:, :], mask_qk[:, :],
                                 start=False, stop=True, skip_group_check=True)
                m.then_inc(s["s"], 1)

            def turn_maxima(b, g):
                stand(t, s["m3"], b * SL + g + 1)
                for n in range(TILES):
                    m = t.transpose(psT(3)[0:3 * SH4, n * P:(n + 1) * P], m3[:, n, :, :].rearrange("p c h -> p (c h)"), identb[:, :])
                m.then_inc(s["m3T"], 1)

            def score_t(b, g, buf, i):
                h, n = g * SH4 + i // TILES, i % TILES
                w = T - n * P
                need(t, s["pexp"], (b * SL + g) * NST + i - 1)
                t.matmul(bank[4 + i % 2][:, 0:w], KTt[buf][0:ROWS, h, n * P:(n + 1) * P], QT[buf][0:ROWS, h, n * P:T],
                         start=True, stop=False, skip_group_check=True)
                m = t.matmul(bank[4 + i % 2][:, 0:P], identb[:, :], mask_kq[:, :],
                             start=False, stop=True, skip_group_check=True)
                m.then_inc(s["st"], 1)

            def values(c, g, buf, p, k):
                need(t, s["pexp"], c * NST + p * NST // 2 + TILES + k + 1)
                if k == 0 and p == 0:
                    need(t, s["ot"], c)
                for h in (2 * p, 2 * p + 1):
                    m = t.matmul(bank[6][VW * h:VW * (h + 1), k * P:T], VV[buf][:, k, g * SH4 + h, :],
                                 PT[:, h, OFF[k]:OFF[k] + T - k * P], start=(k == 0), stop=(k == TILES - 1),
                                 skip_group_check=True)
                if k == TILES - 1:
                    m.then_inc(s["pv"], 1)

            def turn_back(c, b):
                need(t, s["ot"], c + 1)
                need(t, s["norm"], c)
                if b is not None:
                    need(t, s["x"], b * 2 + 2)
                for n in range(TILES):
                    m = t.transpose(bank[7][:, n * P:(n + 1) * P], OT[:, n * P:(n + 1) * P], ident[:, :])
                m.then_inc(s["bt"], 1)

            def turn_out(b, c):
                need(t, s["norm"], (b + 1) * SL)
                need(t, s["oT"], b * KT + c)
                for n in range(TILES):
                    m = t.transpose(bank[7][:, n * P:(n + 1) * P], on[:, n, c * P:(c + 1) * P], ident[:, :])
                m.then_inc(s["onT"], 1)

            def project_out(b, w):
                need(t, s["oT"], (b + 1) * KT)
                need(t, s["x"], b * 2 + w)
                for o in range(2):
                    for c in range(KT):
                        cols = oT[:, c, :].rearrange("p (h t o) -> p h o t", h=2, o=2)[:, w, o, :]
                        m = t.matmul(bank[7][:, o * E:(o + 1) * E], cols, wo[:, c, :], start=(c == 0), stop=(c == KT - 1),
                                     skip_group_check=True)
                m.then_inc(s["wo"], 1)

            def batch(b, buf, has):
                for g in range(SL):
                    c = b * SL + g
                    nb, ng, nbuf = (b, g + 1, buf) if g < 3 else (b + 1, 0, 1 - buf)
                    prev = g > 0 or has(-1)
                    need(t, s["maxrow"], (c + 1) * 48)
                    for i in range(NST):
                        score_t(b, g, buf, i)
                        if g < 3 or has(1):
                            for r in (MAX_AT if g < 3 else MAX_AT_LAST).get(i, ()):
                                if r == 0 and g == 3:
                                    need(t, s["qkT"], (b + 2) * 16)
                                score(nb, ng, nbuf, r)
                            if i == (9 if g < 3 else 14):
                                turn_maxima(nb, ng)
                        if 2 <= i < 6 and has(1):
                            stacks(b + 1, g, i - 2)
                        if i == 4 and prev:
                            turn_back(c - 1, b - 1 if g == 1 and has(-1) else None)
                        if i == 8 and g < 3 and has(1):
                            project_qk(b + 1, g + 1)
                        if i == (9 if g < 3 else 7) and has(1):
                            project_v(b + 1, g)
                        if i == 8 and g == 3 and has(2):
                            normal(b + 2)
                        if i == 13 and g == 3 and has(2):
                            project_qk(b + 2, 0)
                        if 9 <= i < 13:
                            values(c, g, buf, 0, i - 9)
                        if i == 15:
                            for k in range(TILES):
                                values(c, g, buf, 1, k)
                        if g == 0 and has(-1):
                            if i in (9, 11):
                                turn_out(b - 1, (i - 9) // 2)
                            if i in (13, 15):
                                project_out(b - 1, (i - 13) // 2)

            t.wait_ge(s_init, INIT + 1)
            normal(0)
            for n in range(TILES):
                project_qk(0, n)
                for g in range(4):
                    stacks(0, n, g)
                project_v(0, n)
            normal(1)
            project_qk(1, 0)
            for r in range(NMAX):
                score(0, 0, 0, r)
            turn_maxima(0, 0)
            each_slot_batch(t, batch)
            c = B * SL
            turn_back(c - 1, None)
            for k in range(KT):
                turn_out(B - 1, k)
            for w in range(2):
                project_out(B - 1, w)

        def attn_scalar(a):
            s = at

            def normal(b):
                need(a, s["xt"], b + 1)
                need(a, s["v"], b * TILES)
                for k in range(KT):
                    dst = xnT[:, k, :].rearrange("p (h t o) -> p h o t", h=2, o=2)
                    src = bank[k][:, :].rearrange("p (h o t) -> p h o t", h=2, o=2)
                    for hf in range(2):
                        ins = a.activation(dst[:, hf], src[:, hf], ACT.Copy)
                    ins.then_inc(s["xnT"], 1)

            def stacks(b, n, g, buf):
                need(a, s["tr"], b * 16 + 4 * n + g + 1)
                dst = QT[buf] if g < 2 else KTt[buf]
                a.activation(dst[0:STACK, (g % 2) * 8:(g % 2) * 8 + 8, n * P:(n + 1) * P],
                             psT(g % 2)[0:STACK, :].rearrange("p (h t) -> p h t", h=8), ACT.Copy).then_inc(s["qkT"], 1)

            def maxima(c):
                need(a, s["m3T"], c + 1)
                need(a, s["maxrow"], c * 48)
                a.activation(m3T[:, :], psT(3)[0:3 * SH4, 0:T], ACT.Copy).then_inc(s["m3s"], 1)

            def outputs(c):
                need(a, s["pv"], 2 * c + 2)
                need(a, s["bt"], c)
                a.activation(OT[:, :], bank[6][:, :], ACT.Copy).then_inc(s["ot"], 1)

            def turned(b, c):
                need(a, s["onT"], b * KT + c + 1)
                need(a, s["wo"], b * 2)
                a.activation(oT[:, c, :], bank[7][:, :], ACT.Copy).then_inc(s["oT"], 1)

            def batch(b, buf, has):
                for g in range(SL):
                    c = b * SL + g
                    for i in range(NST):
                        need(a, s["st"], c * NST + i + 1)
                        if i % (NST // 2) == 0:
                            need(a, s["pv"], 2 * (c - 1) + i // (NST // 2) + 1)
                        n = i % TILES
                        w = T - n * P
                        a.activation(PT[:, i // TILES, OFF[n]:OFF[n] + w], bank[4 + i % 2][:, 0:w], ACT.Exp,
                                     scale=float(D) ** -0.5).then_inc(s["pexp"], 1)
                        if i == 1 and (g > 0 or has(-1)):
                            outputs(c - 1)
                        if 3 <= i < 7 and has(1):
                            stacks(b + 1, g, i - 3, 1 - buf)
                        if g == 0 and has(-1) and i in (10, 12):
                            turned(b - 1, (i - 10) // 2)
                        if i == 9 and g == 3 and has(2):
                            normal(b + 2)
                        if i == (10 if g < 3 else 15) and (g < 3 or has(1)):
                            maxima(c + 1)

            normal(0)
            for n in range(TILES):
                for g in range(4):
                    stacks(0, n, g, 0)
            normal(1)
            maxima(0)
            each_slot_batch(a, batch)
            outputs(B * SL - 1)
            for k in range(KT):
                turned(B - 1, k)

        def attn_vector(v):
            s = at
            for i in range(2):
                v.memset(VV[i][:, :, :, D:VW], 1.0)
                v.memset(KTt[i][96:96 + 3, :, :], 1.0)
            v.memset(ors[:, :, :], 1.0).then_inc(s_init, 1)
            v.wait_ge(s_init, INIT + 1)

            def project_qk(b, n):
                i = b * TILES + n
                need(v, s["qk"], i + 1)
                need(v, s["rot_c"], i)
                v.tensor_tensor(qk[:, :, :].rearrange("p h d -> p (h d)"), bank[0][:, :], bqkv[:, 0:2 * E],
                                ALU.add).then_inc(s["qkb"], 1)

            def chained(ins, n):
                ins.then_inc(s["tile"], 1)
                need(v, s["tile"], n)

            def split(b, n):
                i = b * TILES + n
                need(v, s["qkb"], i + 1)
                pairs = qk[:, :, :].rearrange("p h (i o) -> p h i o", o=2)
                turned = rs[:, :, :].rearrange("p h (i o) -> p h i o", o=2)
                sine = rope_a[:, n, 1, :].rearrange("p (i o) -> p i o", o=2)
                for o in range(2):
                    ins = v.tensor_tensor(turned[:, :, :, o], pairs[:, :, :, 1 - o],
                                          sine[:, :, o].unsqueeze(1).to_broadcast([P, 2 * H, D // 2]), ALU.mult)
                chained(ins, i * 5 + 1)
                need(v, s["rot_c"], i + 1)
                chained(v.tensor_tensor(rc[:, :, :], rc[:, :, :], rs[:, :, :], ALU.add), i * 5 + 2)
                need(v, s["tr"], i * 4)
                q, k = slice(0, H), slice(H, 2 * H)

                def blocks(side, first, count, step=1):
                    return stk[:, side, :].rearrange("p h (c d) -> p h c d", d=D)[:, :, first:first + (count - 1) * step + 1:step, :]

                def wide(src, side, count):
                    return src[:, side, :].unsqueeze(2).to_broadcast([P, H, count, D])

                v.tensor_copy(blocks(q, 0, 3), wide(rc, q, 3))
                chained(v.tensor_copy(blocks(k, 2, 3), wide(rc, k, 3)), i * 5 + 3)
                v.tensor_tensor(rs[:, q, :], rc[:, q, :], stk[:, q, 0:D], ALU.subtract)
                chained(v.tensor_tensor(rs[:, k, :], rc[:, k, :], stk[:, k, 2 * D:3 * D], ALU.subtract), i * 5 + 4)
                v.tensor_copy(blocks(q, 4, 2), wide(rs, q, 2))
                chained(v.tensor_copy(blocks(k, 1, 2, 4), wide(rs, k, 2)), i * 5 + 5)
                v.tensor_tensor(stk[:, q, 3 * D:4 * D], rs[:, q, :], stk[:, q, 4 * D:5 * D], ALU.subtract)
                v.tensor_tensor(stk[:, k, 0:D], rs[:, k, :], stk[:, k, D:2 * D], ALU.subtract).then_inc(s["split"], 1)

            def project_v(b, n, buf):
                need(v, s["v"], b * TILES + n + 1)
                v.tensor_tensor(VV[buf][:, n, :, 0:D], bank[1][:, 0:E].rearrange("p (h d) -> p h d", d=D),
                                bqkv[:, 2 * E:3 * E].rearrange("p (h d) -> p h d", d=D), ALU.add).then_inc(s["vb"], 1)

            def maximum(c, r):
                n, hs = MAX_STEPS[r]
                w = (n + 1) * P
                need(v, s["s"], c * NMAX + r + 1)
                v.tensor_reduce(nmx[:, n, hs[0]:hs[0] + len(hs)],
                                bank[2 + r % 2][:, 0:len(hs) * w].rearrange("p (h k) -> p h k", k=w),
                                AX_X, ALU.max, negate=True).then_inc(s["mx"], 1)

            def split_maxima(c):
                need(v, s["mx"], (c + 1) * NMAX)
                need(v, s["m3T"], c)
                v.tensor_copy(m3[:, :, 0, :], nmx[:, :, :]).then_inc(s["rest"], 1)
                need(v, s["rest"], 3 * c + 1)
                v.tensor_tensor(nmx_rest[:, :, :], nmx[:, :, :], m3[:, :, 0, :], ALU.subtract).then_inc(s["rest"], 1)
                need(v, s["rest"], 3 * c + 2)
                v.tensor_copy(m3[:, :, 1, :], nmx_rest[:, :, :]).then_inc(s["rest"], 1)
                need(v, s["rest"], 3 * c + 3)
                v.tensor_tensor(m3[:, :, 2, :], nmx_rest[:, :, :], m3[:, :, 1, :], ALU.subtract).then_inc(s["m3"], 1)

            def norm(c, b, g):
                need(v, s["bt"], c + 1)
                if g == 0:
                    need(v, s["onT"], b * KT)
                ps = bank[7][:, :].rearrange("p (n h d) -> p n h d", h=SH4, d=VW)
                v.reciprocal(ors[:, :, :], ps[:, :, :, D]).then_inc(s["recip"], 1)
                need(v, s["recip"], c + 1)
                v.tensor_tensor(on[:, :, g * SH4 * D:(g + 1) * SH4 * D].rearrange("p n (h d) -> p n h d", d=D), ps[:, :, :, 0:D],
                                ors[:, :, :].unsqueeze(3).to_broadcast([P, TILES, SH4, D]), ALU.mult).then_inc(s["norm"], 1)

            def add(b, w):
                need(v, s["wo"], b * 2 + w + 1)
                need(v, s["xbo"], b + 1)
                x = X[:, bass.ds(b * TILES + 2 * w, 2), :]
                v.tensor_tensor(x, x, bank[7][:, :].rearrange("p (o e) -> p o e", e=E), ALU.add).then_inc(s["x"], 1)

            def batch(b, buf, has):
                for g in range(SL):
                    c = b * SL + g
                    prev = g > 0 or has(-1)
                    if g == 3:
                        if has(2):
                            ln_stats(v, s, b + 2)
                        norm(c - 1, b, g - 1)
                        if has(2):
                            ln_normal(v, s, b + 2)
                    if g < 3 or has(1):
                        for r in range(NMAX):
                            maximum(c + 1, r)
                            if r == 1 and g == 3:
                                project_v(b + 1, g, 1 - buf)
                        split_maxima(c + 1)
                    if g < 3 and prev:
                        norm(c - 1, b - (g == 0), (g - 1) % SL)
                    if has(1 if g < 3 else 2):
                        project_qk(b + (1 if g < 3 else 2), (g + 1) % TILES)
                    if g < 3 and has(1):
                        project_v(b + 1, g, 1 - buf)
                    if has(1 if g < 3 else 2):
                        split(b + (1 if g < 3 else 2), (g + 1) % TILES)
                    if g == 0 and has(-1):
                        add(b - 1, 0)
                        add(b - 1, 1)

            ln_vector(v, s, 0)
            for n in range(TILES):
                project_qk(0, n)
                split(0, n)
                project_v(0, n, 0)
            ln_vector(v, s, 1)
            project_qk(1, 0)
            split(1, 0)
            for r in range(NMAX):
                maximum(0, r)
            split_maxima(0)
            each_slot_batch(v, batch)
            norm(B * SL - 1, B - 1, SL - 1)
            for w in range(2):
                add(B - 1, w)

        def attn_gpsimd(g):
            s = at
            with each_batch(g) as b:
                ln_gpsimd(g, s, b)
                need(g, s["xn"], (b + 1) * TILES)
                x = X[:, bass.ds(b * TILES, TILES), :]
                g.tensor_tensor(x, x, bo[:, :].unsqueeze(1).to_broadcast([P, TILES, E]), ALU.add).then_inc(s["xbo"], 1)
                for n in range(TILES):
                    i = b * TILES + n
                    need(g, s["qkb"], i + 1)
                    need(g, s["split"], i)
                    g.tensor_tensor(rc[:, :, :], qk[:, :, :],
                                    rope_a[:, n, 0, :].unsqueeze(1).to_broadcast([P, 2 * H, D]), ALU.mult).then_inc(s["rot_c"], 1)

        def attn_sync(sp):
            s = at
            with sp.Fori(0, B // 2) as i:
                for buf in range(2):
                    for g in range(SL):
                        need(sp, s["m3s"], (2 * i + buf) * SL + g + 1)
                        for c in range(3):
                            sp.dma_start(QT[buf][STACK + c:STACK + c + 1, g * SH4:(g + 1) * SH4, :],
                                         m3T[c * SH4:(c + 1) * SH4, :]).then_inc(s["maxrow"], 16)

        used[0] = 0
        HT = TILES // 2
        llg = part([P, HT, LE])
        ltop = part([P, HT, 8])
        lidx = part([P, HT, 8], U32)
        lidxf = part([P, HT, 8])
        ldiff = part([P, HT, 1])
        lex = part([P, HT, 1])
        lgw = part([P, HT, LK])
        loh = part([P, HT, LK, LE])
        lgm = part([P, HT, LE])
        gxa = part([P, TILES, LR])
        gT = part([LR, 2, HT * P])

        def each_batch_lagging(eng, first, step):
            first()
            step(0, lambda i: i >= 0)
            with eng.Fori(1, B - 1) as b:
                step(b, lambda i: True)
            step(B - 1, lambda i: i <= 0)

        def lora_tensor(t, s):
            def project(b, j):
                if j == 0:
                    need(t, s["xnT"], (b + 1) * KT)
                need(t, s["read"], b * TILES + j + 1)
                for k in range(KT):
                    m = t.matmul(bank[2 + j][:, 0:LCOLS], xnT[:, k, j * P:(j + 1) * P], wl[:, k, :],
                                 start=(k == 0), stop=(k == KT - 1))
                m.then_inc(s["up"], 1)

            def turn(b, h):
                need(t, s["gated"], 2 * b + h + 1)
                need(t, s["gT"], 2 * b + h)
                for j in range(HT):
                    m = t.transpose(bank[6][:, j * P:(j + 1) * P], gxa[:, h * HT + j, :], ident[:, :])
                m.then_inc(s["tr"], 1)

            def lora(b, h):
                need(t, s["gT"], 2 * b + h + 1)
                for j in range(HT):
                    m = t.matmul(bank[2 + h * HT + j][:, 0:E], gT[:, h, j * P:(j + 1) * P], wlb[:, :], start=False, stop=True,
                                 skip_group_check=True)
                    m.then_inc(s["lora"], 1)

            def step(b, has):
                project(b, 0)
                project(b, 1)
                if has(-1):
                    turn(b - 1, 1)
                if has(1):
                    ln_tensor(t, s, b + 1)
                if has(-1):
                    lora(b - 1, 1)
                project(b, 2)
                turn(b, 0)
                project(b, 3)
                lora(b, 0)

            each_batch_lagging(t, lambda: ln_tensor(t, s, 0), step)
            turn(B - 1, 1)
            lora(B - 1, 1)

        def lora_scalar(a, s):
            def normal(b):
                need(a, s["xt"], b + 1)
                need(a, s["up"], b * TILES)
                for k in range(KT):
                    a.activation(xnT[:, k, :], bank[k][:, :], ACT.Copy).then_inc(s["xnT"], 1)

            def gates(b, h):
                need(a, s["lg"], 2 * b + h + 1)
                a.activation(lex[:, :, :], ldiff[:, :, :], ACT.Exp).then_inc(s["ex"], 1)

            def turned(b, h):
                need(a, s["tr"], 2 * b + h + 1)
                need(a, s["lora"], (b - 1) * TILES + (h + 1) * HT)
                a.activation(gT[:, h, :], bank[6][:, 0:HT * P], ACT.Copy).then_inc(s["gT"], 1)

            def step(b, has):
                if has(-1):
                    turned(b - 1, 1)
                gates(b, 0)
                turned(b, 0)
                if has(1):
                    normal(b + 1)
                gates(b, 1)

            each_batch_lagging(a, lambda: normal(0), step)
            turned(B - 1, 1)

        def lora_gpsimd(g, s):
            with each_batch(g) as b:
                ln_gpsimd(g, s, b)
                need(g, s["xn"], (b + 1) * TILES)
                x = X[:, bass.ds(b * TILES, TILES), :]
                g.tensor_tensor(x, x, blh[:, :].unsqueeze(1).to_broadcast([P, TILES, E]), ALU.add).then_inc(s["biased"], 1)

        def lora_vector(v, s):
            v.sem_inc(s["read"], TILES)
            ch = Chain(v, s["chain"], 10, need)

            def gates(b, h):
                u = 2 * b + h
                ch.start(u)
                need(v, s["up"], b * TILES + (h + 1) * HT)
                for j in range(HT):
                    ins = v.tensor_tensor(llg[:, j, :], bank[2 + h * HT + j][:, E + LR:LCOLS], bgate[:, :], ALU.add)
                ch.step(ins, stand)
                for j in range(HT):
                    ins = v.max(ltop[:, j, :], llg[:, j, :])
                ch.step(ins)
                v.tensor_tensor(ldiff[:, :, :], ltop[:, :, 1:2], ltop[:, :, 0:1], ALU.subtract).then_inc(s["lg"], 1)
                for j in range(HT):
                    ins = v.max_index(lidx[:, j, :], ltop[:, j, :], llg[:, j, :])
                ch.step(ins)
                ch.step(v.tensor_copy(lidxf[:, :, :], lidx[:, :, :]))
                ch.step(v.tensor_tensor(
                    loh[:, :, :, :], lidxf[:, :, 0:LK].unsqueeze(3).to_broadcast([P, HT, LK, LE]),
                    iota[:, 0:LE].unsqueeze(1).unsqueeze(1).to_broadcast([P, HT, LK, LE]), ALU.is_equal))
                need(v, s["ex"], u + 1)
                ch.step(v.tensor_scalar(ldiff[:, :, :], lex[:, :, :], 1.0, None, ALU.add))
                ch.step(v.reciprocal(lgw[:, :, 0:1], ldiff[:, :, :]))
                ch.step(v.tensor_tensor(lgw[:, :, 1:2], lex[:, :, :], lgw[:, :, 0:1], ALU.mult))
                ch.step(v.tensor_tensor(loh[:, :, :, :], loh[:, :, :, :],
                                        lgw[:, :, :].unsqueeze(3).to_broadcast([P, HT, LK, LE]), ALU.mult))
                ch.step(v.tensor_reduce(lgm[:, :, :], loh[:, :, :, :].rearrange("p j k e -> p j e k"), AX_X, ALU.add))
                ch.end()
                for j in range(HT):
                    ins = v.tensor_tensor(gxa[:, h * HT + j, :].rearrange("p (e r) -> p e r", r=R),
                                          bank[2 + h * HT + j][:, E:E + LR].rearrange("p (e r) -> p e r", r=R),
                                          lgm[:, j, :].unsqueeze(2).to_broadcast([P, LE, R]), ALU.mult)
                ins.then_inc(s["gated"], 1)

            def add(b, h):
                need(v, s["biased"], b + 1)
                for j in range(h * HT, h * HT + HT):
                    t = b * TILES + j
                    need(v, s["lora"], t + 1)
                    v.scalar_tensor_tensor(out=X[:, t, :], in0=bank[2 + j][:, 0:E], scalar=0.5, in1=X[:, t, :],
                                           op0=ALU.mult, op1=ALU.add).then_inc(s["read"], 1)

            def step(b, has):
                if has(1):
                    ln_normal(v, s, b + 1)
                gates(b, 0)
                if has(-1):
                    add(b - 1, 1)
                if has(2):
                    ln_stats(v, s, b + 2)
                add(b, 0)
                gates(b, 1)

            for b in range(2):
                ln_stats(v, s, b)
            ln_normal(v, s, 0)
            step(0, lambda i: i >= 0)
            with v.Fori(1, B - 2) as b:
                step(b, lambda i: True)
            for b in range(B - 2, B):
                step(b, lambda i, b=b: b + i < B)
            add(B - 1, 1)

        used[0] = 0
        mr = part([P, TILES, RD])
        ms = part([P, TILES, RD])
        pre = part([P, TILES, E])
        hh = part([P, TILES, E])
        sq = part([P, TILES, E])
        mu = part([P, TILES * G])
        var = part([P, TILES * G])
        sd = part([P, TILES * G])
        rs8 = part([P, TILES * G])

        def mix_tensor(t):
            s = mi

            def project(b):
                ln_tensor(t, s, b)
                need(t, s["xnT"], (b + 1) * KT)
                need(t, s["pre"], b)
                for j in range(TILES):
                    for k in range(KT):
                        m = t.matmul(bank[2 + j][:, 0:E], xnT[:, k, j * P:(j + 1) * P], wmix[:, k, :],
                                     start=(k == 0), stop=(k == KT - 1))
                m.then_inc(s["prev"], 1)

            def step(b, ahead):
                if ahead:
                    project(b + 1)
                need(t, s["gn"], b + 1)
                need(t, s["x"], b)
                for c in range(KT):
                    for j in range(TILES):
                        m = t.transpose(bank[6 + c][:, j * P:(j + 1) * P], hh[:, j, c * P:(c + 1) * P], ident[:, :])
                m.then_inc(s["tr"], 1)

            each_batch_ahead(t, lambda: project(0), step)

        def mix_scalar(a):
            s = mi

            def step(b, ahead):
                need(a, s["pre"], b + 1)
                need(a, s["tr"], b)
                a.activation(hh[:, :, :], pre[:, :, :], ACT.Tanh).then_inc(s["th"], 1)
                if ahead:
                    ln_scalar(a, s, b + 1)
                need(a, s["ve"], b + 1)
                a.activation(sd[:, :], var[:, :], ACT.Sqrt).then_inc(s["sd"], 1)

            each_batch_ahead(a, lambda: ln_scalar(a, s, 0), step)

        def mix_gpsimd(g):
            s = mi

            def normal(b):
                ln_gpsimd(g, s, b)
                need(g, s["xn"], (b + 1) * TILES)
                x = X[:, bass.ds(b * TILES, TILES), :].rearrange("p (c h) e -> p c (h e)", c=KT)
                g.tensor_tensor(x, x, gnb[:, :].unsqueeze(2).to_broadcast([P, KT, 2 * E]), ALU.add).then_inc(s["biased"], 1)

            def step(b, ahead):
                if ahead:
                    normal(b + 1)
                need(g, s["rs8"], b + 1)
                groups = hh[:, :, :].rearrange("p j (g c) -> p (j g) c", c=GC)
                g.tensor_tensor(groups, groups, rs8[:, :].unsqueeze(2).to_broadcast([P, TILES * G, GC]),
                                ALU.mult).then_inc(s["gn"], 1)

            each_batch_ahead(g, lambda: normal(0), step)

        def mix_vector(v):
            s = mi
            ch = Chain(v, s["chain"], 11, need)

            def add(b):
                need(v, s["tr"], b + 1)
                need(v, s["biased"], b + 1)
                for c in range(KT):
                    for hf in range(2):
                        x = X[:, b * TILES + 2 * c + hf, :]
                        src = bank[6 + c][:, hf * E:(hf + 1) * E].rearrange("p (o t) -> p t o", o=2)
                        ins = v.scalar_tensor_tensor(out=x.rearrange("p (t o) -> p t o", o=2), in0=src, scalar=gnw[:, c:c + 1],
                                                     in1=x.rearrange("p (t o) -> p t o", o=2), op0=ALU.mult, op1=ALU.add)
                ins.then_inc(s["x"], 1)

            def step(b, has):
                ch.start(b)
                if has(1):
                    ln_stats(v, s, b + 1)
                need(v, s["prev"], b + 1)
                for j in range(TILES):
                    ps = bank[2 + j][:, 0:RD]
                    v.tensor_tensor(mr[:, j, :], ps, rope_m[:, j, 0, :], ALU.mult)
                    for o in range(2):
                        ins = v.tensor_tensor(ms[:, j, :].rearrange("p (i o) -> p i o", o=2)[:, :, o],
                                              ps.rearrange("p (i o) -> p i o", o=2)[:, :, 1 - o],
                                              rope_m[:, j, 1, :].rearrange("p (i o) -> p i o", o=2)[:, :, o], ALU.mult)
                ch.step(ins)
                ins = v.tensor_tensor(mr[:, :, :], mr[:, :, :], ms[:, :, :], ALU.add)
                for j in range(TILES):
                    v.scalar_tensor_tensor(out=pre[:, j, RD:E], in0=bank[2 + j][:, RD:E], scalar=0.0,
                                           in1=bmix[:, RD:E], op0=ALU.max, op1=ALU.add)
                ch.step(ins)
                v.scalar_tensor_tensor(out=pre[:, :, 0:RD], in0=mr[:, :, :], scalar=0.0,
                                       in1=bmix[:, 0:RD].unsqueeze(1).to_broadcast([P, TILES, RD]),
                                       op0=ALU.max, op1=ALU.add).then_inc(s["pre"], 1)
                if has(-1):
                    add(b - 1)
                if has(1):
                    ln_normal(v, s, b + 1)
                need(v, s["th"], b + 1)
                groups = hh[:, :, :].rearrange("p j (g c) -> p (j g) c", c=GC)
                squares = sq[:, :, :].rearrange("p j (g c) -> p (j g) c", c=GC)
                wide = [P, TILES * G, GC]
                ch.step(v.tensor_reduce(mu[:, :], groups, AX_X, ALU.add))
                ch.step(v.tensor_scalar(mu[:, :], mu[:, :], 1.0 / GC, None, ALU.mult))
                ch.step(v.tensor_tensor(groups, groups, mu[:, :].unsqueeze(2).to_broadcast(wide), ALU.subtract))
                ch.step(v.tensor_tensor(squares, groups, groups, ALU.mult))
                ch.step(v.tensor_reduce(var[:, :], squares, AX_X, ALU.add))
                v.tensor_scalar(var[:, :], var[:, :], 1.0 / GC, EPS, ALU.mult, ALU.add).then_inc(s["ve"], 1)
                need(v, s["sd"], b + 1)
                ch.step(v.reciprocal(mu[:, :], sd[:, :]))
                ch.step(v.tensor_tensor(sq[:, 0, 0:TILES * G], mu[:, :], mu[:, :], ALU.mult))
                ch.step(v.tensor_tensor(sq[:, 0, 0:TILES * G], sq[:, 0, 0:TILES * G], var[:, :], ALU.mult))
                ch.step(v.tensor_scalar(sq[:, 0, 0:TILES * G], sq[:, 0, 0:TILES * G], -0.5, 1.5, ALU.mult, ALU.add))
                need(v, s["gn"], b)
                v.tensor_tensor(rs8[:, :], mu[:, :], sq[:, 0, 0:TILES * G], ALU.mult).then_inc(s["rs8"], 1)
                ch.end()

            each_batch_lagging(v, lambda: ln_vector(v, s, 0), step)
            add(B - 1)

        INIT = 1
        mask_f = (hh[:, 0, 0:P], hh[:, 1, 0:P])
        BIASES = ((bqkv[:, :], "bqkv"), (bo[:, :], "bo"), (bl[:, :], "bl"), (bgate[:, :], "bgate"), (bmix[:, :], "bmix"))
        WEIGHTS = ((wqkv, "wqkv"), (wo, "wo"), (wl, "wl"), (wmix, "wmix"))
        CONSTS = 16 * 5
        LATE = 16 * (2 + len(BIASES) + len(WEIGHTS) + 3)

        def load_shared_down(sp):
            full = SI // P * P
            sp.dma_start(ws2[:, 0:full // P, :], d["ws2"][0:full, :].rearrange("(c p) n -> p c n", p=P)).then_inc(s_w["ffn"], 16)
            sp.dma_start(ws2[0:SI - full, NC - 1, :], d["ws2"][full:SI, :]).then_inc(s_w["ffn"], 16)

        def restart(sp, s):
            for c in s.values():
                sp.sem_clear(c)
                sp.sem_inc(c, 1)
            sp.sem_inc(s_again, 1)

        @block.sync
        def _(sp):
            x = d["L0_attn_x"].rearrange("b (h p o) e -> b p h (o e)", h=2, o=2)
            for b in range(B):
                sp.dma_start(X[:, bass.ds(b * TILES, TILES), :].rearrange("p (h o) e -> p h (o e)", o=2), x[b]).then_inc(s_w["x"], 16)
            for c in counted:
                sp.sem_inc(c, 1)
            sp.sem_inc(s_go, 1)
            sp.wait_ge(s_zero, 1)
            sp.dma_start(XS.rearrange("(i p) e -> p i e", p=P), zeros[:, :].unsqueeze(1).to_broadcast([P, SLOT_TILES, E]))\
              .then_inc(s_w["slots"], 16)
            sp.dma_start(w13[:, :, :], d["w13"].rearrange("(k p) n -> p k n", p=P)).then_inc(s_w["ffn"], 16)
            sp.dma_start(w2[0:HK, :, :], d["w2"].rearrange("(k p) n -> p k n", p=HK)).then_inc(s_w["ffn"], 16)
            load_shared_down(sp)
            routed_sync(sp, mo, dmas[0])
            sp.wait_ge(done["f0"], 1)
            restart(sp, mo)
            attn_sync(sp)
            sp.wait_ge(done["at"], 1)
            sp.dma_start(w13[:, :, :], d["w13"].rearrange("(k p) n -> p k n", p=P)).then_inc(s_w["ffn"], 16)
            sp.dma_start(w2[0:HK, :, :], d["w2"].rearrange("(k p) n -> p k n", p=HK)).then_inc(s_w["ffn"], 16)
            load_shared_down(sp)
            routed_sync(sp, mo, dmas[1])
            sp.wait_ge(done["l0"], 1)
            restart(sp, lo)
            sp.wait_ge(done["l1"], 1)
            o = out.rearrange("b (h p o) e -> b p h (o e)", h=2, o=2)
            for b in range(B):
                sp.dma_start(o[b], X[:, bass.ds(b * TILES, TILES), :].rearrange("p (h o) e -> p h (o e)", o=2)).then_inc(s_out, 16)
            sp.wait_ge(s_out, 16 * B)

        @block.gpsimd
        def _(g):
            g.memset(zeros[:, :], 0.0).then_inc(s_zero, 1)
            g.memset(epsc[:, :], EPS).then_inc(s_pool, 1)
            g.memset(mhalf[:, :], -0.5).then_inc(s_pool, 1)
            for dst, name in ((ident, "ident"), (mask_f[0], "mask_qk"), (mask_f[1], "mask_kq")):
                g.dma_start(dst, d[name]).then_inc(s_w["const"], 16)
            g.dma_start(iota[:, :], d["iota"].rearrange("(a n) -> a n", a=1).to_broadcast([P, SLOT_TILES])).then_inc(s_w["const"], 16)
            g.dma_start(gates_w[:, :, :], d["gates_w"].rearrange("(k p) n -> p k n", p=P)).then_inc(s_w["const"], 16)
            g.dma_start(rope_a[:, :, :, :], d["rope_a"].rearrange("p (n s c) -> p n s c", n=TILES, s=2)).then_inc(s_w["late"], 16)
            g.dma_start(rope_m[:, :, :, :], d["rope_m"].rearrange("p (n s c) -> p n s c", n=TILES, s=2)).then_inc(s_w["late"], 16)
            for dst, name in BIASES:
                n = d[name].shape[0]
                g.dma_start(dst, d[name].rearrange("(a n) -> a n", a=1).to_broadcast([P, n])).then_inc(s_w["late"], 16)
            for dst, name in WEIGHTS:
                g.dma_start(dst[:, :, :], d[name].rearrange("(k p) n -> p k n", p=P)).then_inc(s_w["late"], 16)
            g.dma_start(wlb[:, :], d["wlb"]).then_inc(s_w["late"], 16)
            for dst, name in ((gnw, "gnw"), (gnb, "gnb")):
                g.dma_start(dst[:, :], d[name]).then_inc(s_w["late"], 16)
            g.wait_ge(s_pool, 2)
            g.wait_ge(s_go, 1)
            moe_gpsimd(g, mo, dmas[0])
            g.wait_ge(done["f0"], 1)
            g.wait_ge(s_w["late"], LATE)
            attn_gpsimd(g)
            g.wait_ge(done["at"], 1)
            g.wait_ge(s_again, 1)
            g.sem_inc(s_stood, 1)
            moe_gpsimd(g, mo, dmas[1])
            g.wait_ge(done["f1"], 1)
            lora_gpsimd(g, lo)
            g.wait_ge(done["l0"], 1)
            mix_gpsimd(g)
            g.wait_ge(done["mx"], 1)
            g.wait_ge(s_again, 2)
            g.sem_inc(s_stood, 1)
            lora_gpsimd(g, lo)

        @block.scalar
        def _(a):
            a.wait_ge(s_go, 1)
            moe_scalar(a, mo)
            a.wait_ge(done["f0"], 1)
            attn_scalar(a)
            a.wait_ge(done["at"], 1)
            a.wait_ge(s_again, 1)
            a.sem_inc(s_stood, 1)
            moe_scalar(a, mo)
            a.wait_ge(done["f1"], 1)
            lora_scalar(a, lo)
            a.wait_ge(done["l0"], 1)
            mix_scalar(a)
            a.wait_ge(done["mx"], 1)
            a.wait_ge(s_again, 2)
            a.sem_inc(s_stood, 1)
            lora_scalar(a, lo)

        @block.tensor
        def _(t):
            t.wait_ge(s_w["const"], CONSTS)
            t.wait_ge(s_init, INIT)
            t.wait_ge(s_go, 1)
            moe_tensor(t, mo, 64)
            t.wait_ge(done["f0"], 1)
            t.wait_ge(s_w["late"], LATE)
            attn_tensor(t)
            t.wait_ge(done["at"], 1)
            t.wait_ge(s_again, 1)
            t.sem_inc(s_stood, 1)
            moe_tensor(t, mo, 128)
            t.wait_ge(done["f1"], 1)
            lora_tensor(t, lo)
            t.wait_ge(done["l0"], 1)
            mix_tensor(t)
            t.wait_ge(done["mx"], 1)
            t.wait_ge(s_again, 2)
            t.sem_inc(s_stood, 1)
            lora_tensor(t, lo)

        @block.vector
        def _(v):
            v.wait_ge(s_w["const"], CONSTS)
            v.wait_ge(s_go, 1)
            v.tensor_copy(identb[:, :], ident[:, :])
            v.tensor_copy(mask_qk[:, :], mask_f[0])
            v.memset(ones[:, :], 1.0)
            v.tensor_scalar(tri[:, :], mask_f[0], 0.0, None, ALU.is_lt)
            v.tensor_copy(mask_kq[:, :], mask_f[1]).then_inc(s_init, 1)
            v.wait_ge(s_init, INIT)
            v.wait_ge(s_w["x"], 16 * B)

            def close(ph, sem_x, n):
                need(v, sem_x, n)
                v.tensor_copy(stats[:, 0, 0:1], mv[:, 0, 0:1]).then_inc(done[ph], 1)
                v.wait_ge(done[ph], 1)

            for ph in ("f0", "at", "f1", "l0", "mx", "l1"):
                if ph in ("f1", "l1"):
                    v.wait_ge(s_again, 1 if ph == "f1" else 2)
                    v.sem_inc(s_stood, 1)
                if ph in ("f0", "f1"):
                    moe_vector(v, mo, dmas[0 if ph == "f0" else 1])
                    need(v, mo["comb"], B * TILES + AHEAD)
                    close(ph, mo["u_acc"], B * TILES + AHEAD)
                elif ph == "at":
                    v.wait_ge(s_w["late"], LATE)
                    v.tensor_scalar(blh[:, :], bl[:, :], 0.5, None, ALU.mult)
                    attn_vector(v)
                    close(ph, at["x"], B * 2)
                elif ph == "mx":
                    mix_vector(v)
                    close(ph, mi["x"], B)
                else:
                    lora_vector(v, lo)
                    close(ph, lo["read"], (B + 1) * TILES)


def tables():
    c = {}
    c["ident"] = np.eye(P, dtype=np.float32)
    q, k = np.arange(P)[:, None], np.arange(P)[None, :]
    c["mask_qk"] = np.where(k > q, np.float32(NEG), np.float32(0))
    c["mask_kq"] = np.ascontiguousarray(c["mask_qk"].T)
    c["iota"] = np.arange(SLOT_TILES, dtype=np.float32)

    def rope(pos, dim):
        inv = (np.float32(1) / np.power(np.float32(10000.0), np.arange(0, dim, 2, dtype=np.float32) / np.float32(dim))).astype(np.float32)
        ang = pos.astype(np.float32)[..., None] * inv
        cos = np.repeat(np.cos(ang), 2, -1)
        sin = np.stack([-np.sin(ang), np.sin(ang)], -1).reshape(cos.shape)
        return np.stack([cos, sin], -2).astype(np.float32)

    p, n = np.arange(P)[:, None], np.arange(TILES)[None, :]
    c["rope_a"] = rope(n * P + p, D).reshape(P, -1)
    c["rope_m"] = rope((n // 2) * 256 + 2 * p + n % 2, RD).reshape(P, -1)
    return c


def kernel(**inputs):
    import numpy as _np
    import concourse.bacc as _bacc
    from concourse import mybir as _mybir
    from concourse.bass_utils import run_bass_kernel_spmd as _run

    a = {n: _np.asarray(v) for n, v in inputs.items()}
    host = {
        "L0_attn_x": a["L0_attn_x"],
        "gates_w": _np.concatenate([a["L0_ffn_gate_w"], a["L0_ffn_sgate_w"]], 0).T,
        "w13": _np.concatenate([a["L0_ffn_w13"].reshape(NE * 2 * I, E), a["L0_ffn_shared_gate_up_w"]], 0).T,
        "w2": a["L0_ffn_w2"].transpose(2, 0, 1).reshape(I, NE * E),
        "ws2": a["L0_ffn_shared_down_w"].T,
        "wqkv": _np.concatenate([a["L0_attn_Wq"], a["L0_attn_Wk"], a["L0_attn_Wv"]], 0).T,
        "wo": a["L0_attn_Wo"].T,
        "wl": _np.concatenate([a["L1_ffn_W"], a["L1_ffn_lora_A"].reshape(LR, E), a["L1_ffn_gate_w"]], 0).T,
        "wlb": a["L1_ffn_lora_B"].transpose(0, 2, 1).reshape(LR, E),
        "wmix": a["L1_attn_W_Q"],
        "bqkv": _np.concatenate([a["L0_attn_bq"], a["L0_attn_bk"], a["L0_attn_bv"]]),
        "bo": a["L0_attn_bo"], "bl": a["L1_ffn_b"], "bgate": a["L1_ffn_gate_b"], "bmix": a["L1_attn_hh_b"],
        "gnw": a["L1_attn_gn_weight"].reshape(KT, P).T, "gnb": a["L1_attn_gn_bias"].reshape(KT, P).T,
    }
    host.update(tables())
    nc = _bacc.Bacc("TRN2", target_bir_lowering=False, num_devices=1)
    arrays, d = {}, {}
    for name, v in host.items():
        arrays[f"in_{name}"] = _np.ascontiguousarray(v)
        d[name] = nc.dram_tensor(f"in_{name}", v.shape, _mybir.dt.from_np(v.dtype), kind="ExternalInput").ap()
    out = nc.dram_tensor("out_x", (B, T, E), F32, kind="ExternalOutput").ap()
    XS, YS = (nc.dram_tensor(n, (SLOT_TILES * P, E), F32, kind="Internal").ap() for n in ("slots_in", "slots_out"))
    build(nc, d, XS, YS, out)
    r = _run(nc, [arrays], core_ids=[0])
    return r.results[0]["out_x"]
```
